# Optimizing a Trainium2 kernel written in Bass

```python
import numpy as np
import jax
import jax.numpy as jnp

def _softmax(x, axis=-1):
    return jax.nn.softmax(x, axis=axis)

def _gelu(x):
    return jax.nn.gelu(x, approximate=True)

def _silu(x):
    return jax.nn.silu(x)

def _sigmoid(x):
    return jax.nn.sigmoid(x)

def _layernorm(x, axis=-1, eps=1e-05):
    m = jnp.mean(x, axis=axis, keepdims=True)
    v = jnp.var(x, axis=axis, keepdims=True)
    return (x - m) / jnp.sqrt(v + eps)

def _scatter_add(tgt, idx, src, axis=0):
    return tgt.at[idx].add(src)

def _segment_sum(src, seg, n):
    return jax.ops.segment_sum(src, seg, n)
kernel_name = 'mk_flamingo_gated_d1_seqx_r4_bd5774'

def setup_inputs(seed: int=0):
    np.random.seed(seed)
    _w = jnp.asarray

    def _rec_inputs():
        import jax
        import jax.numpy as jnp
        _rk = jax.random.key(seed)
        x = 0.0003765 + 1 * jax.random.normal(jax.random.fold_in(_rk, 1), (32, 112, 256), jnp.float32)
        _lenS = 112 - jax.random.randint(jax.random.fold_in(_rk, 7), (32,), 0, max(1, 112 // 4) + 1, jnp.int32)
        _lenS2 = 375 - jax.random.randint(jax.random.fold_in(_rk, 8), (32,), 0, max(1, 375 // 4) + 1, jnp.int32)
        _ctx_1024P = jax.random.normal(jax.random.fold_in(_rk, 11), (32, 16, 256), jnp.float32)
        _ctx_1024c = jax.random.dirichlet(jax.random.fold_in(_rk, 511), 0.3 * jnp.ones((16,), jnp.float32), (32, 375))
        _ctx_1024t = jnp.einsum('bsk,bkd->bsd', _ctx_1024c, _ctx_1024P)
        _ctx_1024t = _ctx_1024t * jax.lax.rsqrt(jnp.mean(jnp.square(_ctx_1024t)) + 1e-12) * 0.953939
        ctx_1024 = -0.000292821 + 1.00034 * (_ctx_1024t + 0.3 * jax.random.normal(jax.random.fold_in(_rk, 611), (32, 375, 256), jnp.float32))
        _validS = jnp.arange(112)[None, :] < _lenS[:, None]
        _validS2 = jnp.arange(375)[None, :] < _lenS2[:, None]
        _causal = jnp.tril(jnp.ones((112, 112), dtype=bool))
        mask_1x1xSxS2_fk1 = jnp.where(jnp.broadcast_to(_validS2[0:1, None, None, :], (1, 1, 112, 375)), 1.0, 0.0).astype(jnp.float32)
        _g = jax.random.normal(jax.random.fold_in(_rk, 9001), (2, 1), jnp.float32)
        _g = jnp.sign(_g) * jnp.maximum(jnp.abs(_g), 1.0) + (_g == 0) * 1.0
        g_xattn = _g[0]
        g_ffn = _g[1]
        return (x, ctx_1024, mask_1x1xSxS2_fk1, g_xattn, g_ffn)
    x, ctx_1024, mask_1x1xSxS2_fk1, g_xattn, g_ffn = _rec_inputs()

    def _L0_xattn_setup():
        import jax, jax.numpy as jnp
        import numpy as np
        B, S, E, H = (2, 512, 256, 16)
        D = E // H

        def _split_heads(x):
            b, s, _ = x.shape
            return x.reshape(b, s, H, D).transpose(0, 2, 1, 3)
        key = jax.random.key(seed)
        ks = jax.random.split(key, 12)
        scale = 1.0 / np.sqrt(E)
        inp = {'v': jax.random.normal(ks[0], (B, S, E), jnp.float32), 'k': jax.random.normal(ks[1], (B, S, E), jnp.float32), 'q': jax.random.normal(ks[2], (B, S, E), jnp.float32), 'mask': jnp.triu(jnp.ones((S, S), jnp.float32), k=1)[None, None, :, :], 'wq': jax.random.normal(ks[3], (E, E), jnp.float32) * scale, 'bq': jnp.zeros((E,), jnp.float32), 'wk': jax.random.normal(ks[4], (E, E), jnp.float32) * scale, 'bk': jnp.zeros((E,), jnp.float32), 'wv': jax.random.normal(ks[5], (E, E), jnp.float32) * scale, 'bv': jnp.zeros((E,), jnp.float32), 'wo': jax.random.normal(ks[6], (E, E), jnp.float32) * scale, 'bo': jnp.zeros((E,), jnp.float32)}
        return inp
    _L0_xattn_all = _L0_xattn_setup()
    _L0_xattn_in = {k: v for k, v in _L0_xattn_all.items() if k in ('wq', 'bq', 'wk', 'bk', 'wv', 'bv', 'wo', 'bo')}
    del _L0_xattn_all

    def _L0_ffn_setup():
        import jax, jax.numpy as jnp
        import numpy as np
        B, T, DIM = (2, 512, 256)
        H, DH, E, K = (16, 64, 8, 2)
        key = jax.random.key(seed)
        ks = jax.random.split(key, 7)
        s = 0.02
        return {'x': jax.random.normal(ks[0], (B, T, DIM), jnp.float32), 'Wq': jax.random.normal(ks[1], (H, DH, DIM), jnp.float32) * s, 'Wk': jax.random.normal(ks[2], (H, DH, DIM), jnp.float32) * s, 'Wv': jax.random.normal(ks[3], (E, DH, DIM), jnp.float32) * s, 'Ws': jax.random.normal(ks[4], (H, E, DIM), jnp.float32) * s, 'Wd': jax.random.normal(ks[5], (H, E, DIM), jnp.float32) * s, 'Wo': jax.random.normal(ks[6], (E, DIM, DH), jnp.float32) * s}
    _L0_ffn_all = _L0_ffn_setup()
    _L0_ffn_in = {k: v for k, v in _L0_ffn_all.items() if k in ('Wq', 'Wk', 'Wv', 'Ws', 'Wd', 'Wo')}
    del _L0_ffn_all
    return {'x': x, 'ctx_1024': ctx_1024, 'mask_1x1xSxS2_fk1': mask_1x1xSxS2_fk1, 'g_xattn': g_xattn, 'g_ffn': g_ffn, 'L0_xattn_wq': _L0_xattn_in['wq'], 'L0_xattn_bq': _L0_xattn_in['bq'], 'L0_xattn_wk': _L0_xattn_in['wk'], 'L0_xattn_bk': _L0_xattn_in['bk'], 'L0_xattn_wv': _L0_xattn_in['wv'], 'L0_xattn_bv': _L0_xattn_in['bv'], 'L0_xattn_wo': _L0_xattn_in['wo'], 'L0_xattn_bo': _L0_xattn_in['bo'], 'L0_ffn_Wq': _L0_ffn_in['Wq'], 'L0_ffn_Wk': _L0_ffn_in['Wk'], 'L0_ffn_Wv': _L0_ffn_in['Wv'], 'L0_ffn_Ws': _L0_ffn_in['Ws'], 'L0_ffn_Wd': _L0_ffn_in['Wd'], 'L0_ffn_Wo': _L0_ffn_in['Wo']}

def reference(x, ctx_1024, mask_1x1xSxS2_fk1, g_xattn, g_ffn, L0_xattn_wq, L0_xattn_bq, L0_xattn_wk, L0_xattn_bk, L0_xattn_wv, L0_xattn_bv, L0_xattn_wo, L0_xattn_bo, L0_ffn_Wq, L0_ffn_Wk, L0_ffn_Wv, L0_ffn_Ws, L0_ffn_Wd, L0_ffn_Wo):
    import jax
    import jax.numpy as jnp

    def _L0_xattn_ref(v, k, q, mask, wq, bq, wk, bk, wv, bv, wo, bo):
        import jax, jax.numpy as jnp
        import numpy as np
        B, S, E, H = (2, 512, 256, 16)
        D = E // H

        def _split_heads(x):
            b, s, _ = x.shape
            return x.reshape(b, s, H, D).transpose(0, 2, 1, 3)
        qh = _split_heads(q @ wq + bq)
        kh = _split_heads(k @ wk + bk)
        vh = _split_heads(v @ wv + bv)
        logits = jnp.einsum('bhqd,bhkd->bhqk', qh, kh) / jnp.sqrt(jnp.float32(D))
        logits = logits + mask * -1000000000.0
        attn = jax.nn.softmax(logits, axis=-1)
        out = jnp.einsum('bhqk,bhkd->bhqd', attn, vh)
        out = out.transpose(0, 2, 1, 3).reshape(q.shape[0], -1, E)
        return out @ wo + bo

    def _L0_ffn_ref(x, Wq, Wk, Wv, Ws, Wd, Wo):
        import jax, jax.numpy as jnp
        import numpy as np
        B, T, DIM = (2, 512, 256)
        H, DH, E, K = (16, 64, 8, 2)
        scale = DH ** (-0.5)
        q = jnp.einsum('btc,hdc->bhtd', x, Wq)
        k = jnp.einsum('btc,hdc->bhtd', x, Wk)
        gate_v = jnp.einsum('btc,hec->bthe', x, Ws)
        w, sel = jax.lax.top_k(gate_v, K)
        wsig = jax.nn.sigmoid(w)
        oh = jax.nn.one_hot(sel, E, dtype=x.dtype)
        mix_v = jnp.einsum('bthk,bthke->bthe', wsig, oh)
        proj_v = jnp.einsum('btc,edc->bted', x, Wv)
        v = jnp.einsum('bthe,bted->bhtd', mix_v, proj_v)
        scores = jnp.einsum('bhid,bhjd->bhij', q * scale, k)
        probs = jax.nn.softmax(scores, axis=-1)
        attn = jnp.einsum('bhij,bhjd->bihd', probs, v)
        gate_o = jnp.einsum('btc,hec->bthe', x, Wd)
        _, sel_o = jax.lax.top_k(gate_o, K)
        mask_o = jax.nn.one_hot(sel_o, E, dtype=x.dtype).sum(axis=3)
        res = jnp.einsum('bthe,bthd,efd->bthf', mask_o, attn, Wo)
        return res.sum(axis=2)
    x = x + jnp.tanh(g_xattn[0]) * _L0_xattn_ref(ctx_1024, ctx_1024, _layernorm(x, axis=-1), mask_1x1xSxS2_fk1, L0_xattn_wq, L0_xattn_bq, L0_xattn_wk, L0_xattn_bk, L0_xattn_wv, L0_xattn_bv, L0_xattn_wo, L0_xattn_bo)
    x = x + jnp.tanh(g_ffn[0]) * _L0_ffn_ref(_layernorm(x, axis=-1), L0_ffn_Wq, L0_ffn_Wk, L0_ffn_Wv, L0_ffn_Ws, L0_ffn_Wd, L0_ffn_Wo)
    return x

_drawn_inputs = setup_inputs


def setup_inputs(seed=0):
    import zlib

    import numpy as np

    out = dict(_drawn_inputs(seed))
    spreads = {'L0_xattn_bq': (0.0, 0.354),
     'L0_xattn_bk': (0.0, 0.8),
     'L0_xattn_bv': (0.0, 0.1),
     'L0_xattn_bo': (0.0, 0.1)}
    factors = {'L0_ffn_Wq': 8.0, 'L0_ffn_Wk': 8.0}
    for name, (base, spread) in spreads.items():
        noise = np.random.default_rng([zlib.crc32(name.encode()), seed]).standard_normal(out[name].shape)
        drawn = base * np.exp(spread * noise) if base else spread * noise
        out[name] = jnp.asarray(drawn.astype(out[name].dtype))
    for name, factor in factors.items():
        out[name] = (out[name] * factor).astype(out[name].dtype)
    return out
```

```python
from contextlib import ExitStack

import concourse.bass as bass
from concourse import mybir

F32 = mybir.dt.float32
ALU = mybir.AluOpType
ACT = mybir.ActivationFunctionType
AXX = mybir.AxisListType.X

P = 128
PSUM_BANK = 512
LN_EPS = 1e-5
MASK_SCALE = -1e9
LEAST = -3.0e38


def wait_all(eng, met, *waits):
    waits = [(sem, n if isinstance(n, int) else eng.to_reg(n)) for sem, n in waits]
    eng.wait_ge(met, 1)
    for sem, n in waits:
        eng.wait_ge(sem, n)


def flat(ap):
    return ap.rearrange("a s e -> (a s) e")


class Shapes:

    def __init__(self, x, ctx, wq2, wv2):
        self.B, self.S, self.E = x.shape
        self.S2 = ctx.shape[1]
        self.H, self.D = 16, self.E // 16
        self.KC, self.KP = 3, self.S2 // 3
        self.G = 4
        self.H2, self.D2, _ = wq2.shape
        self.X = wv2.shape[0]
        self.EC = self.E // P
        self.HT = P // self.D
        self.M2 = self.H2 * self.D2 // P
        assert self.KC * self.KP == self.S2 and self.KP <= P and self.B % 4 == 0


def prepare(nc, z, d, c):
    B, S, E, EC, HT = z.B, z.S, z.E, z.EC, z.HT
    GB = 4
    NG = B // GB
    with ExitStack() as ctx:
        sb = lambda name, shape: ctx.enter_context(nc.sbuf_tensor(name, shape, F32))
        ps = lambda name, shape: ctx.enter_context(nc.psum_tensor(name, shape, F32))
        sem = lambda name: ctx.enter_context(nc.semaphore(name))
        wq_in, wk_in = sb("wq_in", [P, z.M2, E]), sb("wk_in", [P, z.M2, E])
        wv_in = sb("wv_in", [P, z.X * z.D2 // P, E])
        wg_in = sb("wg_in", [P, 2, E])
        wo_in = sb("wo_in", [P, EC, z.X, z.D2])
        bq = sb("bq", [P, EC])
        bo = sb("bo", [S, E])
        gates_in = sb("gates_in", [S, 2])
        stats, moments = sb("stats", [S, GB, 6]), sb("moments", [S, 2, GB, 2])
        minus_half = sb("minus_half", [S, GB])
        var_eps, rstd = sb("var_eps", [S, GB]), sb("rstd", [S, 2, GB])
        xn, xnT = sb("xn", [S, 2, GB, E]), sb("xnT", [P, 2, EC, GB * S])
        psum_t = [ps(f"p_t{i}", [P, PSUM_BANK]) for i in range(2)]
        psum_x = [ps(f"p_x{i}", [P, EC, S]) for i in range(2)]
        psum_q = [ps(f"p_q{i}", [P, PSUM_BANK]) for i in range(2)]
        x_loaded = [sem(f"x_loaded{i}") for i in range(2)]
        small_loaded, weights_loaded = sem("small_loaded"), sem("weights_loaded")
        cross_loaded = sem("cross_loaded")
        zeroed, consts_ready = sem("zeroed"), sem("consts_ready")
        stats_done, moments_done = sem("stats_done"), sem("moments_done")
        eps_added, rstd_done = sem("eps_added"), sem("rstd_done")
        xn_done, xbias_done = sem("xn_done"), sem("xbias_done")
        xt_ready, xt_copied = sem("xt_ready"), sem("xt_copied")
        q_ready, q_copied = sem("q_ready"), sem("q_copied")
        wt_ready, wt_copied = sem("wt_ready"), sem("wt_copied")
        tanh_done, bias_done = sem("tanh_done"), sem("bias_done")
        block = ctx.enter_context(nc.Block())

        turns = []
        for src, dst, tiles in ((wq_in, c.wq2T, z.M2), (wk_in, c.wk2T, z.M2), (wv_in, c.wv2T, z.X * z.D2 // P)):
            for e in range(EC):
                for m in range(0, tiles, 4):
                    turns.append(([src[:, m + k, e * P:(e + 1) * P] for k in range(4)],
                                  dst[:, e, m * P:(m + 4) * P]))
        turns.append(([wg_in[:, k, e * P:(e + 1) * P] for e in range(EC) for k in range(2)],
                      c.wgT[:, :, :].rearrange("p e n -> p (e n)")))
        for m in range(0, z.X // 2, 2):
            turns.append(([wo_in[:, f, 2 * (m + k):2 * (m + k) + 2, :].rearrange("p e d -> p (e d)")
                           for k in range(2) for f in range(EC)],
                          c.wo2T[:, m:m + 2, :].rearrange("p e f -> p (e f)")))

        @block.sync
        def _(sp):
            with nc.allow_non_contiguous_dma(reason="biases, one column each"):
                sp.dma_start(bq[:, :], d.bq.rearrange("(t p) -> p t", p=P)).then_inc(small_loaded, 16)
                sp.dma_start(c.bk[:, :], d.bk.rearrange("(t p) -> p t", p=P)).then_inc(small_loaded, 16)
            row = lambda v: v.rearrange("(a n) -> a n", a=1)
            sp.dma_start(bo[:, :], row(d.bo).to_broadcast([S, E])).then_inc(small_loaded, 16)
            sp.dma_start(c.bv[:, :], row(d.bv).to_broadcast([z.KP, E])).then_inc(small_loaded, 16)
            sp.dma_start(gates_in[:, 0:1], row(d.g_xattn).to_broadcast([S, 1])).then_inc(small_loaded, 16)
            sp.dma_start(gates_in[:, 1:2], row(d.g_ffn).to_broadcast([S, 1])).then_inc(small_loaded, 16)
            sp.dma_start(c.maskb[:, :], d.mask.rearrange("a b s k -> (a b s) k")).then_inc(small_loaded, 16)
            sp.dma_start(c.wq[:, :, :], d.wq.rearrange("(e p) n -> p e n", p=P)).then_inc(small_loaded, 16)
            xs = d.x.rearrange("b s e -> s b e")

            def load_x(i, p):
                g = 2 * i + p
                sp.dma_start(c.X[:, bass.ds(GB * g, GB), :], xs[:, bass.ds(GB * g, GB), :]).then_inc(x_loaded[p], 16)

            load_x(0, 0)
            load_x(0, 1)
            with sp.Fori(1, NG // 2) as i:
                for p in range(2):
                    sp.wait_ge(x_loaded[p], 16 * i)
                    load_x(i, p)

        @block.scalar
        def _(act):
            for dst, src in ((c.wk, d.wk), (c.wv, d.wv), (c.wo, d.wo)):
                act.dma_start(dst[:, :, :], src.rearrange("(e p) n -> p e n", p=P)).then_inc(cross_loaded, 16)
            act.dma_start(wq_in[:, :, :], d.wq2.rearrange("h d c -> (h d) c").rearrange("(m p) c -> p m c", p=P)).then_inc(weights_loaded, 16)
            act.dma_start(wk_in[:, :, :], d.wk2.rearrange("h d c -> (h d) c").rearrange("(m p) c -> p m c", p=P)).then_inc(weights_loaded, 16)
            act.dma_start(wv_in[:, :, :], d.wv2.rearrange("h d c -> (h d) c").rearrange("(m p) c -> p m c", p=P)).then_inc(weights_loaded, 16)
            act.dma_start(wg_in[:, 0, :], d.ws.rearrange("h e c -> (h e) c")).then_inc(weights_loaded, 16)
            act.dma_start(wg_in[:, 1, :], d.wd.rearrange("h e c -> (h e) c")).then_inc(weights_loaded, 16)
            for f in range(EC):
                act.dma_start(wo_in[:, f, :, :], d.wo2[:, f * P:(f + 1) * P, :].rearrange("e f d -> f e d")).then_inc(weights_loaded, 16)
            act.wait_ge(small_loaded, 16 * 8)
            act.activation(c.tanh_g[:, :], gates_in[:, :], ACT.Tanh).then_inc(tanh_done, 1)
            act.wait_ge(bias_done, 1)
            with act.Fori(0, NG // 2) as i:
                for p in range(2):
                    g = 2 * i + p
                    for j in range(GB):
                        act.wait_ge(xt_ready, GB * g + j + 1)
                        act.activation(xnT[:, p, :, j * S:(j + 1) * S], psum_x[j % 2][:, :, :], ACT.Copy).then_inc(xt_copied, 1)
                    for t in range(EC):
                        act.wait_ge(q_ready, EC * g + t + 1)
                        act.activation(c.QT[:, t, bass.ds(GB * S * g, GB * S)], psum_q[t][:, 0:GB * S], ACT.Identity,
                                       bias=bq[:, t:t + 1], scale=float(z.D) ** -0.5).then_inc(q_copied, 1)
            for n, (_, dst) in enumerate(turns):
                act.wait_ge(wt_ready, n + 1)
                act.activation(dst, psum_t[n % 2][:, :], ACT.Copy).then_inc(wt_copied, 1)
            act.wait_ge(cross_loaded, 16 * 3)

        @block.gpsimd
        def _(pool):
            pool.memset(c.ident[:, :], 0.0).then_inc(zeroed, 1)
            pool.memset(c.headmask[:, :], 1.0).then_inc(zeroed, 1)
            pool.memset(c.tok16[:, :], 1.0).then_inc(zeroed, 1)
            pool.memset(c.tok8[:, :, :], 1.0).then_inc(zeroed, 1)
            pool.memset(minus_half[:, :], -0.5).then_inc(zeroed, 1)
            pool.wait_ge(zeroed, 5)
            steps = 0

            def keep(t, compare, fill, base, pattern, mult):
                nonlocal steps
                nc.gpsimd.affine_select(out=t, in_=t, compare_op=compare, fill=fill, base=base,
                                        pattern=pattern, channel_multiplier=mult).then_inc(consts_ready, 1)
                steps += 1
                pool.wait_ge(consts_ready, steps)

            keep(c.ident[:, :], ALU.not_equal, 1.0, 0, [[-1, P]], 1)
            for t, base, pattern, width in (
                (c.headmask[:, :], 0, [[-z.D, HT]], z.D),
                (c.tok16[:, :], 0, [[-z.X, 16]], z.X),
                (c.tok8[:, :, :], 0, [[8 * z.H2, 2], [-z.H2, 16]], z.H2),
            ):
                keep(t, ALU.is_ge, 0.0, base, pattern, 1)
                keep(t, ALU.is_ge, 0.0, width - 1 - base, [[-a, n] for a, n in pattern], -1)
            with pool.Fori(0, NG // 2) as i:
                for p in range(2):
                    g = 2 * i + p
                    wait_all(pool, zeroed, (moments_done, GB * g + GB))
                    pool.tensor_scalar(var_eps[:, :], moments[:, p, :, 1], LN_EPS, None, ALU.add).then_inc(eps_added, 1)
                    pool.wait_ge(eps_added, g + 1)
                    pool.tensor_tensor(rstd[:, p, :], var_eps[:, :], minus_half[:, :], ALU.pow).then_inc(rstd_done, 1)
                    pool.wait_ge(bias_done, 2)
                    pool.wait_ge(xn_done, GB * g + GB)
                    for j in range(GB):
                        xb = c.X[:, bass.ds(GB * g + j, 1), :].rearrange("s a e -> s (a e)")
                        pool.tensor_tensor(xb, xb, bo[:, :], ALU.add).then_inc(xbias_done, 1)

        @block.vector
        def _(dve):
            dve.wait_ge(small_loaded, 16 * 8)
            dve.tensor_scalar(bq[:, :], bq[:, :], float(z.D) ** -0.5, None, ALU.mult).then_inc(bias_done, 1)
            dve.wait_ge(tanh_done, 1)
            dve.tensor_scalar(bo[:, :], bo[:, :], c.tanh_g[:, 0:1], None, ALU.mult).then_inc(bias_done, 1)
            dve.tensor_scalar(c.maskb[:, :], c.maskb[:, :], MASK_SCALE, None, ALU.mult).then_inc(bias_done, 1)

            def group(i, p, first):
                g = 2 * i + p
                entry = lambda j: c.X[:, bass.ds(GB * g + j, 1), :].rearrange("s a e -> s (a e)")
                dve.wait_ge(x_loaded[p], 16 * i + 16)
                for j in range(GB):
                    dve.bn_stats(stats[:, j, :], entry(j)).then_inc(stats_done, 1)
                for j in range(GB):
                    wait_all(dve, small_loaded, (stats_done, GB * g + j + 1))
                    dve.bn_aggr(moments[:, p, j, :], stats[:, j, :]).then_inc(moments_done, 1)
                dve.wait_ge(rstd_done, g + 1)
                if not first:
                    dve.wait_ge(xt_ready, GB * g - GB)
                for j in range(GB):
                    dve.tensor_scalar(xn[:, p, j, :], entry(j), moments[:, p, j, 0:1], rstd[:, p, j:j + 1],
                                      ALU.subtract, ALU.mult).then_inc(xn_done, 1)

            group(0, 0, True)
            group(0, 1, True)
            with dve.Fori(1, NG // 2) as i:
                group(i, 0, False)
                group(i, 1, False)

        @block.tensor
        def _(pe):
            pe.wait_ge(consts_ready, 7)
            pe.wait_ge(small_loaded, 16 * 8)

            def group(i, p, first):
                g = 2 * i + p
                for j in range(GB):
                    pe.wait_ge(xn_done, GB * g + j + 1)
                    if not (first and j < 2):
                        pe.wait_ge(xt_copied, GB * g + j - 1)
                    for e in range(EC):
                        last = nc.tensor.transpose(psum_x[j % 2][:, e, :], xn[:, p, j, e * P:(e + 1) * P], c.ident[0:S, 0:S])
                    last.then_inc(xt_ready, 1)
                pe.wait_ge(xt_copied, GB * g + GB)
                for t in range(EC):
                    if not first:
                        pe.wait_ge(q_copied, EC * g - EC + t + 1)
                    for e in range(EC):
                        last = nc.tensor.matmul(psum_q[t][:, 0:GB * S], c.wq[:, e, t * P:(t + 1) * P], xnT[:, p, e, :],
                                                start=(e == 0), stop=(e == EC - 1))
                    last.then_inc(q_ready, 1)

            group(0, 0, True)
            group(0, 1, False)
            with pe.Fori(1, NG // 2) as i:
                group(i, 0, False)
                group(i, 1, False)
            pe.wait_ge(weights_loaded, 16 * 7)
            for n, (srcs, _) in enumerate(turns):
                if n >= 2:
                    pe.wait_ge(wt_copied, n - 1)
                for k, src in enumerate(srcs):
                    last = nc.tensor.transpose(psum_t[n % 2][:, k * P:(k + 1) * P], src, c.ident[:, :])
                last.then_inc(wt_ready, 1)


def cross(nc, z, d, c):
    B, S, E, EC, HT, H, G, KC, KP, S2, D = z.B, z.S, z.E, z.EC, z.HT, z.H, z.G, z.KC, z.KP, z.S2, z.D
    NG = H // G
    VW = 32
    with ExitStack() as ctx:
        sb = lambda name, shape: ctx.enter_context(nc.sbuf_tensor(name, shape, F32))
        ps = lambda name, shape: ctx.enter_context(nc.psum_tensor(name, shape, F32))
        sem = lambda name: ctx.enter_context(nc.semaphore(name))
        ctx_in = sb("ctx_in", [KP, 2, KC, E])
        ctxT = sb("ctxT", [P, EC, S2])
        KT = sb("KT", [P, 2, EC, S2])
        V = sb("V", [KP, 2, KC, H, VW])
        Qz = sb("Qz", [P, 2, EC, HT, S])
        raw = sb("raw", [S, 2, G, S2])
        neg_max = sb("neg_max", [S, 2, G])
        shifted = sb("shifted", [S, 2, G, S2])
        probsT = sb("probsT", [KP, 2, KC, G * S])
        headsT = sb("headsT", [P, NG * S])
        recip = sb("recip", [S, H])
        heads = sb("heads", [S, H, D])
        outT = sb("outT", [P, EC, S])
        bank_s = [ps(f"bank_s{i}", [P, PSUM_BANK]) for i in range(2)]
        bank_t = ps("bank_t", [P, KC, PSUM_BANK])
        bank_o = ps("bank_o", [P, PSUM_BANK])
        bank_ab = ps("bank_ab", [P, 2, PSUM_BANK])
        ctx_loaded = [sem(f"ctx_loaded{i}") for i in range(2)]
        v_cleared, v_set = sem("v_cleared"), sem("v_set")
        ctxT_ready, ctxT_copied = sem("ctxT_ready"), sem("ctxT_copied")
        k_ready, k_copied = sem("k_ready"), sem("k_copied")
        va_ready, vb_ready, v_copied = sem("va_ready"), sem("vb_ready"), sem("v_copied")
        qz_ready = sem("qz_ready")
        scores_ready, scores_read, shift_done = sem("scores_ready"), sem("scores_read"), sem("shift_done")
        turned, exp_done, pv_done = sem("turned"), sem("exp_done"), sem("pv_done")
        headsT_copied, heads_ready, recip_done, heads_done = sem("headsT_copied"), sem("heads_ready"), sem("recip_done"), sem("heads_done")
        outT_ready, outT_copied, y_ready, x_done = sem("outT_ready"), sem("outT_copied"), sem("y_ready"), sem("x_done")
        block = ctx.enter_context(nc.Block())

        def batches(eng, body):
            body(0, 0, True, False)
            body(1, 1, False, False)
            with eng.Fori(1, B // 2 - 1) as i:
                body(2 * i, 0, False, False)
                body(2 * i + 1, 1, False, False)
            body(B - 2, 0, False, False)
            body(B - 1, 1, False, True)

        @block.sync
        def _(sp):
            def load(b, p):
                sp.dma_start(ctx_in[:, p, :, :], flat(d.ctx[bass.ds(b, 1)]).rearrange("(k p) e -> p k e", p=KP)).then_inc(ctx_loaded[p], 16)

            load(0, 0)
            load(1, 1)
            with sp.Fori(1, B // 2) as i:
                for p in range(2):
                    sp.wait_ge(ctxT_ready, 2 * i + p - 1)
                    load(2 * i + p, p)

        @block.tensor
        def _(pe):
            def transposes(b, i, p, first):
                pe.wait_ge(ctx_loaded[p], 16 * i + 16)
                if not first:
                    pe.wait_ge(v_copied, 2 * b)
                for e in range(EC):
                    for k in range(KC):
                        last = nc.tensor.transpose(bank_ab[:, e, k * KP:(k + 1) * KP],
                                                   ctx_in[:, p, k, e * P:(e + 1) * P], c.ident[0:KP, 0:KP])
                last.then_inc(ctxT_ready, 1)

            def keys(b):
                pe.wait_ge(ctxT_copied, b + 1)
                for t in range(EC):
                    for e in range(EC):
                        last = nc.tensor.matmul(bank_ab[:, t, 0:S2], c.wk[:, e, t * P:(t + 1) * P], ctxT[:, e, :],
                                                start=(e == 0), stop=(e == EC - 1))
                    last.then_inc(k_ready, 1)

            def values(k):
                for e in range(EC):
                    last = nc.tensor.matmul(bank_ab[0:KP, k // 2, (k % 2) * E:(k % 2 + 1) * E], ctxT[:, e, k * KP:(k + 1) * KP],
                                            c.wv[:, e, :], start=(e == 0), stop=(e == EC - 1))
                return last

            def scores(b, p, g, first):
                if g == 0:
                    pe.wait_ge(qz_ready, NG * b + NG)
                    pe.wait_ge(k_copied, EC * b + EC)
                for j in range(G):
                    h = G * g + j
                    if not (first and h < 2):
                        pe.wait_ge(scores_read, H * b + h - 1)
                    nc.tensor.matmul(bank_s[h % 2][0:S, 0:S2], Qz[:, p, h // HT, h % HT, :], KT[:, p, h // HT, :],
                                     start=True, stop=True).then_inc(scores_ready, 1)

            def turn(b, g, first):
                pe.wait_ge(shift_done, H * b + G * g + G)
                if not (first and g == 0):
                    pe.wait_ge(exp_done, NG * b + g)
                for k in range(KC):
                    for j in range(G):
                        last = nc.tensor.transpose(bank_t[0:KP, k, j * S:(j + 1) * S],
                                                   shifted[:, g % 2, j, k * KP:(k + 1) * KP], c.ident[0:S, 0:S])
                last.then_inc(turned, 1)

            def weigh(b, p, g, first):
                pe.wait_ge(exp_done, NG * b + g + 1)
                if g == 0:
                    pe.wait_ge(v_copied, 2 * b + 2)
                    if first:
                        pe.wait_ge(v_set, 1)
                    else:
                        pe.wait_ge(headsT_copied, b)
                for j in range(G):
                    for k in range(KC):
                        last = nc.tensor.matmul(bank_o[j * VW:(j + 1) * VW, g * S:(g + 1) * S], V[:, p, k, G * g + j, :],
                                                probsT[:, g % 2, k, j * S:(j + 1) * S], start=(k == 0), stop=(k == KC - 1))
                last.then_inc(pv_done, 1)

            def heads_back(b):
                pe.wait_ge(headsT_copied, b + 1)
                for g in range(NG):
                    last = nc.tensor.transpose(bank_ab[0:S, 0, g * P:(g + 1) * P], headsT[:, g * S:(g + 1) * S], c.ident[:, :])
                last.then_inc(heads_ready, 1)

            def heads_turn(b):
                pe.wait_ge(heads_done, b + 1)
                flat_heads = heads[:, :, :].rearrange("s h d -> s (h d)")
                for e in range(EC):
                    last = nc.tensor.transpose(bank_ab[:, 1, e * S:(e + 1) * S], flat_heads[:, e * P:(e + 1) * P], c.ident[0:S, 0:S])
                last.then_inc(outT_ready, 1)

            def project(b):
                pe.wait_ge(outT_copied, b + 1)
                for e in range(EC):
                    last = nc.tensor.matmul(bank_ab[0:S, 1, 0:E], outT[:, e, :], c.wo[:, e, :], start=(e == 0), stop=(e == EC - 1))
                last.then_inc(y_ready, 1)

            def body(b, p, first, last, i):
                scores(b, p, 0, first)
                if not first:
                    turn(b - 1, NG - 1, False)
                if not last:
                    transposes(b + 1, i + p, 1 - p, False)
                if not first:
                    weigh(b - 1, 1 - p, NG - 1, False)
                scores(b, p, 1, False)
                if not last:
                    keys(b + 1)
                turn(b, 0, first)
                if not first:
                    if not last:
                        pe.wait_ge(k_copied, EC * b + EC + 1)
                    heads_back(b - 1)
                weigh(b, p, 0, first)
                scores(b, p, 2, False)
                turn(b, 1, False)
                if not last:
                    pe.wait_ge(k_copied, EC * b + 2 * EC)
                if not first:
                    heads_turn(b - 1)
                if not last:
                    values(0)
                    values(1).then_inc(va_ready, 1)
                weigh(b, p, 1, False)
                if not first:
                    project(b - 1)
                scores(b, p, 3, False)
                turn(b, 2, False)
                if not last:
                    if not first:
                        pe.wait_ge(x_done, b)
                    values(2).then_inc(vb_ready, 1)
                weigh(b, p, 2, False)

            transposes(0, 0, 0, True)
            keys(0)
            pe.wait_ge(k_copied, EC)
            values(0)
            values(1).then_inc(va_ready, 1)
            values(2).then_inc(vb_ready, 1)
            body(0, 0, True, False, 0)
            body(1, 1, False, False, 0)
            with pe.Fori(1, B // 2 - 1) as i:
                body(2 * i, 0, False, False, i)
                body(2 * i + 1, 1, False, False, i)
            body(B - 2, 0, False, False, B // 2 - 1)
            body(B - 1, 1, False, True, B // 2 - 1)
            turn(B - 1, NG - 1, False)
            weigh(B - 1, 1, NG - 1, False)
            heads_back(B - 1)
            heads_turn(B - 1)
            project(B - 1)

        @block.scalar
        def _(act):
            def ctx_copy(b, first):
                act.wait_ge(ctxT_ready, b + 1)
                if not first:
                    act.wait_ge(vb_ready, b)
                act.activation(ctxT[:, :, :], bank_ab[:, :, 0:S2], ACT.Copy).then_inc(ctxT_copied, 1)

            def key_copy(b, p, first):
                for t in range(EC):
                    act.wait_ge(k_ready, EC * b + t + 1)
                    if t == 0 and not first:
                        act.wait_ge(scores_ready, H * (b - 1))
                    act.activation(KT[:, p, t, :], bank_ab[:, t, 0:S2], ACT.Identity, bias=c.bk[:, t:t + 1]).then_inc(k_copied, 1)

            def exps(b, g, first):
                act.wait_ge(turned, NG * b + g + 1)
                if not (first and g < 2):
                    act.wait_ge(pv_done, NG * b + g - 1)
                act.activation(probsT[:, g % 2, :, :], bank_t[0:KP, :, 0:G * S], ACT.Exp).then_inc(exp_done, 1)

            def heads_copy(b, first):
                act.wait_ge(pv_done, NG * b + NG)
                if not first:
                    act.wait_ge(heads_ready, b)
                act.activation(headsT[:, :], bank_o[:, 0:NG * S], ACT.Copy).then_inc(headsT_copied, 1)

            def out_copy(b, first):
                act.wait_ge(outT_ready, b + 1)
                if not first:
                    act.wait_ge(y_ready, b)
                act.activation(outT[:, :, :].rearrange("p e s -> p (e s)"), bank_ab[:, 1, 0:EC * S], ACT.Copy).then_inc(outT_copied, 1)

            def body(b, p, first, last):
                second = isinstance(b, int) and b == 1
                if not first:
                    exps(b - 1, NG - 1, False)
                if not last:
                    ctx_copy(b + 1, False)
                if not first:
                    heads_copy(b - 1, second)
                if not last:
                    key_copy(b + 1, 1 - p, first)
                exps(b, 0, first)
                exps(b, 1, first)
                if not first:
                    out_copy(b - 1, second)
                exps(b, 2, False)

            ctx_copy(0, True)
            key_copy(0, 0, True)
            batches(act, body)
            exps(B - 1, NG - 1, False)
            heads_copy(B - 1, False)
            out_copy(B - 1, False)

        @block.vector
        def _(dve):
            dve.memset(V[:, :, :, :, :], 0.0).then_inc(v_cleared, 1)
            dve.wait_ge(v_cleared, 1)
            for p in range(2):
                for k in range(KC):
                    last_set = dve.memset(V[:, p, k, :, D:D + 1], 1.0)
            last_set.then_inc(v_set, 1)

            def value_copy(b, p, half):
                dve.wait_ge(va_ready if half == 0 else vb_ready, b + 1)
                for k in ((0, 1) if half == 0 else (2,)):
                    last = dve.tensor_tensor(V[:, p, k, :, 0:D],
                                             bank_ab[0:KP, k // 2, (k % 2) * E:(k % 2 + 1) * E].rearrange("p (h d) -> p h d", d=D),
                                             c.bv[:, :].rearrange("p (h d) -> p h d", d=D), ALU.add)
                last.then_inc(v_copied, 1)

            def score_max(b, g, first):
                for j in range(G):
                    h = G * g + j
                    free = [] if first and h < 2 * G else [(shift_done, H * b + h - 2 * G + 1)]
                    wait_all(dve, v_set, (scores_ready, H * b + h + 1), *free)
                    dve.tensor_tensor_reduce(raw[:, g % 2, j, :], bank_s[h % 2][0:S, 0:S2], c.maskb[:, :], -1.0, -LEAST,
                                             ALU.add, ALU.min, neg_max[:, g % 2, j:j + 1]).then_inc(scores_read, 1)

            def normalise(b, first):
                sums = bank_ab[0:S, 0, :].rearrange("s (h w) -> s h w", w=VW)
                dve.wait_ge(heads_ready, b + 1)
                if not first:
                    dve.wait_ge(heads_done, b)
                dve.reciprocal(recip[:, :].unsqueeze(2), sums[:, :, D:D + 1]).then_inc(recip_done, 1)
                dve.wait_ge(recip_done, b + 1)
                if not first:
                    dve.wait_ge(outT_ready, b)
                dve.tensor_tensor(heads[:, :, :], sums[:, :, 0:D], recip[:, :].unsqueeze(2).to_broadcast([S, H, D]), ALU.mult).then_inc(heads_done, 1)

            def residual(b):
                dve.wait_ge(y_ready, b + 1)
                xb = c.X[:, bass.ds(b, 1), :].rearrange("s a e -> s (a e)")
                dve.scalar_tensor_tensor(xb, bank_ab[0:S, 1, 0:E], c.tanh_g[:, 0:1], xb, ALU.mult, ALU.add).then_inc(x_done, 1)

            def body(b, p, first, last):
                second = isinstance(b, int) and b == 1
                score_max(b, 0, first)
                score_max(b, 1, first)
                if not first:
                    normalise(b - 1, second)
                score_max(b, 2, False)
                if not last:
                    value_copy(b + 1, 1 - p, 0)
                if not first:
                    residual(b - 1)
                score_max(b, 3, False)
                if not last:
                    value_copy(b + 1, 1 - p, 1)

            dve.wait_ge(v_set, 1)
            value_copy(0, 0, 0)
            value_copy(0, 0, 1)
            batches(dve, body)
            normalise(B - 1, False)
            residual(B - 1)

        @block.gpsimd
        def _(pool):
            def spread(b, p, n, first):
                t, h0 = G * n // HT, G * n % HT
                if n == 0 and not first:
                    pool.wait_ge(scores_ready, H * (b - 1))
                q = c.QT[:, t, bass.ds(S * b, S)]
                pool.tensor_tensor(Qz[:, p, t, h0:h0 + G, :], q.unsqueeze(1).to_broadcast([P, G, S]),
                                   c.headmask[:, h0:h0 + G].unsqueeze(2).to_broadcast([P, G, S]), ALU.mult).then_inc(qz_ready, 1)

            def body(b, p, first, last):
                for g in range(NG):
                    for j in range(G):
                        h = G * g + j
                        free = [] if j or (first and g < 2) else [(turned, NG * b + g - 1)]
                        wait_all(pool, v_set, (scores_read, H * b + h + 1), *free)
                        pool.tensor_scalar(shifted[:, g % 2, j, :], raw[:, g % 2, j, :], -1.0, neg_max[:, g % 2, j:j + 1],
                                           ALU.mult, ALU.add).then_inc(shift_done, 1)
                    if not last:
                        spread(b + 1, 1 - p, g, first)

            for n in range(NG):
                spread(0, 0, n, True)
            batches(pool, body)


def switch(nc, z, d, c):
    B, S, E, EC, G, H, D, X, M2 = z.B, z.S, z.E, z.EC, z.G, z.H2, z.D2, z.X, z.M2
    NG = H // G
    T16, T8 = S // 16, S // 8
    W = D + 1
    TOP_STEPS, TOP_BEST = 13, 7
    with ExitStack() as ctx:
        sb = lambda name, shape: ctx.enter_context(nc.sbuf_tensor(name, shape, F32))
        ps = lambda name, shape: ctx.enter_context(nc.psum_tensor(name, shape, F32))
        sem = lambda name: ctx.enter_context(nc.semaphore(name))
        dram = lambda name, shape: nc.dram_tensor(name, shape, F32).ap()
        proj_dram = dram("proj_dram", (B, S, X * D))
        mix_dram = dram("mix_dram", (B, S, X * H))
        pick_dram = dram("pick_dram", (B, S, H * X))

        minus_half = sb("minus_half2", [S, 1])
        rank_w = sb("rank_w", [S, X])
        stats, moments = sb("stats2", [S, 6]), sb("moments2", [S, 2])
        var_eps, rstd = sb("var_eps2", [S, 1]), sb("rstd2", [S, 1])
        xn = sb("xn2", [S, E])
        xnT = sb("xnT2", [P, 2, EC, S])
        gates = sb("gates", [S, 2 * H, X])
        proj = sb("proj", [S, X * D])
        best = sb("best", [S, 2, 2 * H])
        tie = sb("tie", [S, 2 * H, X])
        first_tie = sb("first_tie", [S, 2 * H])
        one_hot = sb("one_hot", [S, 2, 2 * H, X])
        rest = sb("rest", [S, 2 * H, X])
        sig = sb("sig", [S, 2, H])
        mix_part = sb("mix_part", [S, 2, H, X])
        mix, pick = sb("mix", [S, X, H]), sb("pick", [S, H, X])
        proj_te = sb("proj_te", [P, 2, T16, 2, D])
        mix_te = sb("mix_te", [P, 2, T16, H])
        pick_th = sb("pick_th", [P, 2, T8, X])
        mix_bd = sb("mix_bd", [P, T16, 16, H])
        pick_bd = sb("pick_bd", [P, T8, 16, X])
        qT = sb("qT", [P, M2, S])
        kz = sb("kz", [P, M2, 2, S])
        vT = sb("vT", [P, H // 2, S])
        v = sb("v", [S, H, W])
        neg_max = sb("max2", [S, 2, G])
        shifted = sb("shifted2", [S, 2, G, S])
        probsT = sb("probsT2", [S, 2, G * S])
        attT = sb("attT", [W, S, H])
        recip = sb("recip2", [P, T8])
        att = sb("att", [P, T8, 2, D])
        uT = sb("uT", [P, X // 2, S])
        bank_ab = ps("bank2_ab", [P, 2, PSUM_BANK])
        bank_s = [ps(f"bank2_s{i}", [P, PSUM_BANK]) for i in range(2)]
        bank_t, bank_o = ps("bank2_t", [P, PSUM_BANK]), ps("bank2_o", [P, PSUM_BANK])
        bank_gh = ps("bank2_gh", [P, 2, PSUM_BANK])

        consts_done = sem("consts_done")
        stats_done, moments_done, eps_added, rstd_done, xn_done = (sem(n) for n in ("stats2_done", "moments2_done", "eps2_added", "rstd2_done", "xn2_done"))
        xt_ready, xt_copied = sem("xt2_ready"), sem("xt2_copied")
        gates_ready, gates_copied = sem("gates_ready"), sem("gates_copied")
        proj_ready, proj_copied = sem("proj_ready"), sem("proj_copied")
        mix_part_done = sem("mix_part_done")
        top_step, negexp_done, mix_done, pick_done = sem("top_step"), sem("negexp_done"), sem("mix_done"), sem("pick_done")
        proj_stored, mix_stored, pick_stored = ([sem(f"{n}{p}") for p in range(2)] for n in ("proj_stored", "mix_stored", "pick_stored"))
        te_loaded = [sem(f"te_loaded{p}") for p in range(2)]
        mix_bd_done, pick_bd_done = sem("mix_bd_done"), sem("pick_bd_done")
        q_ready, q_copied, kk_ready, kk_copied = sem("q2_ready"), sem("q2_copied"), sem("k2_ready"), sem("k2_copied")
        vt_ready, vt_copied, v_ready, v_copied = sem("vt_ready"), sem("vt_copied"), sem("v2_ready"), sem("v2_copied")
        scores_ready, max_done, shift_done = sem("scores2_ready"), sem("max2_done"), sem("shift2_done")
        turned, exp_done, pv_done, attT_copied = sem("turned2"), sem("exp2_done"), sem("pv2_done"), sem("attT_copied")
        att_ready, recip_done, att_done = sem("att_ready"), sem("recip2_done"), sem("att_done")
        u_ready, u_copied, y_ready, out_done = sem("u_ready"), sem("u_copied"), sem("y2_ready"), sem("out_done")
        stored = [sem(f"out_stored{p}") for p in range(2)]
        block = ctx.enter_context(nc.Block())

        def pipeline(eng, pre, main):
            pre(0, 0, 0, True)
            pre(1, 1, 0, False)
            main(0, 0, 0, True)
            pre(2, 0, 1, False)
            main(1, 1, 0, False)
            pre(3, 1, 1, False)
            with eng.Fori(1, B // 2 - 1) as i:
                for p in range(2):
                    main(2 * i + p, p, i, False)
                    pre(2 * i + p + 2, p, i + 1, False)
            for p in range(2):
                main(B - 2 + p, p, B // 2 - 1, False)

        @block.sync
        def _(sp):
            def pre(b, p, i, first):
                sp.wait_ge(proj_copied, b + 1)
                sp.dma_start(flat(proj_dram[bass.ds(b, 1)]), proj[:, :]).then_inc(proj_stored[p], 16)
                sp.wait_ge(mix_done, b + 1)
                sp.dma_start(flat(mix_dram[bass.ds(b, 1)]), mix[:, :, :].rearrange("s e h -> s (e h)")).then_inc(mix_stored[p], 16)
                sp.wait_ge(pick_done, b + 1)
                sp.dma_start(flat(pick_dram[bass.ds(b, 1)]), pick[:, :, :].rearrange("s h e -> s (h e)")).then_inc(pick_stored[p], 16)
                rows = lambda t, w: t[bass.ds(b, 1)].rearrange("a s n -> (a s n)").rearrange("(g p w) -> p g w", p=P, w=w)
                free = [] if isinstance(b, int) and b < 2 else [
                    (vt_ready, 4 * (b - 1)), (mix_bd_done, T16 * (b - 1)), (pick_bd_done, T8 * (b - 1))]
                wait_all(sp, consts_done, (proj_stored[p], 16 * i + 16), *free)
                for a in range(2):
                    sp.dma_start(proj_te[:, p, :, a, :], rows(proj_dram, D)).then_inc(te_loaded[p], 16)
                sp.wait_ge(mix_stored[p], 16 * i + 16)
                sp.dma_start(mix_te[:, p, :, :], rows(mix_dram, H)).then_inc(te_loaded[p], 16)
                sp.wait_ge(pick_stored[p], 16 * i + 16)
                sp.dma_start(pick_th[:, p, :, :], rows(pick_dram, X)).then_inc(te_loaded[p], 16)

            def main(b, p, i, first):
                sp.wait_ge(out_done, b + 1)
                sp.dma_start(flat(d.out[bass.ds(b, 1)]), c.X[:, bass.ds(b, 1), :].rearrange("s a e -> s (a e)")).then_inc(stored[p], 16)

            pipeline(sp, pre, main)
            for p in range(2):
                sp.wait_ge(stored[p], 16 * (B // 2))

        @block.tensor
        def _(pe):
            def pre(b, p, i, first):
                pe.wait_ge(xn_done, b + 1)
                if not first:
                    pe.wait_ge(gates_copied, b)
                    pe.wait_ge(proj_copied, b)
                if not (isinstance(b, int) and b < 2):
                    pe.wait_ge(out_done, b - 1)
                for e in range(EC):
                    last = nc.tensor.transpose(bank_ab[:, 0, e * S:(e + 1) * S], xn[:, e * P:(e + 1) * P], c.ident[0:S, 0:S])
                last.then_inc(xt_ready, 1)
                pe.wait_ge(xt_copied, b + 1)
                for e in range(EC):
                    last = nc.tensor.matmul(bank_ab[0:S, 0, 0:2 * H * X], xnT[:, p, e, :], c.wgT[:, e, :], start=(e == 0), stop=(e == EC - 1))
                last.then_inc(gates_ready, 1)
                for e in range(EC):
                    last = nc.tensor.matmul(bank_ab[0:S, 1, 0:X * D], xnT[:, p, e, :], c.wv2T[:, e, :], start=(e == 0), stop=(e == EC - 1))
                last.then_inc(proj_ready, 1)

            def project(b, p, weights, half, ready):
                for m in range(M2 // 2):
                    for e in range(EC):
                        w = weights[:, e, (half * M2 // 2 + m) * P:(half * M2 // 2 + m + 1) * P]
                        last = nc.tensor.matmul(bank_ab[:, half, m * S:(m + 1) * S], w, xnT[:, p, e, :], start=(e == 0), stop=(e == EC - 1))
                last.then_inc(ready, 1)

            def scores(b, g, first):
                if g == 0:
                    pe.wait_ge(q_copied, 2 * b + 2)
                    pe.wait_ge(kk_copied, 4 * b + 4)
                if not (first and g < 2):
                    pe.wait_ge(shift_done, NG * b + g - 1)
                for m in (2 * g, 2 * g + 1):
                    last = nc.tensor.matmul(bank_s[g % 2][0:S, (m % 2) * 2 * S:(m % 2 + 1) * 2 * S], qT[:, m, :],
                                            kz[:, m, :, :].rearrange("p a s -> p (a s)"), start=True, stop=True)
                last.then_inc(scores_ready, 1)

            def turn(b, g, first):
                pe.wait_ge(shift_done, NG * b + g + 1)
                if not (first and g == 0):
                    pe.wait_ge(exp_done, NG * b + g)
                for j in range(G):
                    last = nc.tensor.transpose(bank_t[0:S, j * S:(j + 1) * S], shifted[:, g % 2, j, :], c.ident[0:S, 0:S])
                last.then_inc(turned, 1)

            def weigh(b, g, first):
                pe.wait_ge(exp_done, NG * b + g + 1)
                if not (first and g == 0):
                    pe.wait_ge(attT_copied, NG * b + g)
                for j in range(G):
                    last = nc.tensor.matmul(bank_o[0:W, j * S:(j + 1) * S], v[:, G * g + j, :], probsT[:, g % 2, j * S:(j + 1) * S],
                                            start=True, stop=True)
                last.then_inc(pv_done, 1)

            def mix_values(b, p, n):
                if n >= 2:
                    pe.wait_ge(vt_copied, 8 * b + 2 * (n - 2) + 2)
                for k in (2 * n, 2 * n + 1):
                    if k < T16:
                        pe.wait_ge(mix_bd_done, T16 * b + k + 1)
                        last = nc.tensor.matmul(bank_gh[:, n % 2, (k % 2) * 256:(k % 2 + 1) * 256],
                                                proj_te[:, p, k, :, :].rearrange("p a d -> p (a d)"),
                                                mix_bd[:, k, :, :].rearrange("p t h -> p (t h)"), start=True, stop=True)
                last.then_inc(vt_ready, 1)

            def main(b, p, i, first):
                pe.wait_ge(te_loaded[p], 64 * i + 64)
                if not first:
                    pe.wait_ge(out_done, b)
                pe.wait_ge(gates_copied, b + (1 if isinstance(b, int) and b == B - 1 else 2))
                pe.wait_ge(proj_copied, b + (1 if isinstance(b, int) and b == B - 1 else 2))
                for half in range(2):
                    project(b, p, c.wq2T, half, q_ready)
                if not first:
                    pe.wait_ge(u_copied, 4 * b)
                for n in range(4):
                    mix_values(b, p, n)
                for half in range(2):
                    pe.wait_ge(q_copied, 2 * b + half + 1)
                    project(b, p, c.wk2T, half, kk_ready)
                scores(b, 0, first)
                pe.wait_ge(vt_copied, 8 * b + 8)
                for n in range(2):
                    for m in range(H // 4):
                        last = nc.tensor.transpose(bank_gh[0:S, n, m * P:(m + 1) * P], vT[:, n * H // 4 + m, :], c.ident[:, :])
                    last.then_inc(v_ready, 1)
                scores(b, 1, first)
                turn(b, 0, first)
                pe.wait_ge(v_copied, 2 * b + 2)
                for g in range(NG):
                    if g + 2 < NG:
                        scores(b, g + 2, False)
                    if g + 1 < NG:
                        turn(b, g + 1, False)
                    weigh(b, g, first)
                pe.wait_ge(attT_copied, NG * b + NG)
                for n in range(T8):
                    last = nc.tensor.transpose(bank_gh[:, n // 7, (n % 7) * W:(n % 7 + 1) * W],
                                               attT[:, 8 * n:8 * n + 8, :].rearrange("d t h -> d (t h)"), c.ident[0:W, 0:W])
                    if n % 7 == 6:
                        last.then_inc(att_ready, 1)
                pe.wait_ge(att_done, 2 * b + 2)
                pe.wait_ge(pick_bd_done, T8 * b + T8)
                for k in range(T16):
                    for s in range(2):
                        n = 2 * k + s
                        last = nc.tensor.matmul(bank_gh[:, k // 4, (k % 4) * P:(k % 4 + 1) * P],
                                                att[:, n, :, :].rearrange("p a d -> p (a d)"),
                                                pick_bd[:, n, :, :].rearrange("p t e -> p (t e)"), start=(s == 0), stop=(s == 1))
                    if k in (3, T16 - 1):
                        last.then_inc(u_ready, 1)
                pe.wait_ge(u_copied, 4 * b + 4)
                for m in range(X // 2):
                    last = nc.tensor.matmul(bank_ab[0:S, 0, 0:E], uT[:, m, :], c.wo2T[:, m, :], start=(m == 0), stop=(m == X // 2 - 1))
                last.then_inc(y_ready, 1)

            pe.wait_ge(consts_done, 4)
            pipeline(pe, pre, main)

        @block.scalar
        def _(act):
            def pre(b, p, i, first):
                act.wait_ge(xt_ready, b + 1)
                if not (isinstance(b, int) and b < 2):
                    act.wait_ge(kk_ready, 2 * (b - 1))
                act.activation(xnT[:, p, :, :].rearrange("p e s -> p (e s)"), bank_ab[:, 0, 0:EC * S], ACT.Copy).then_inc(xt_copied, 1)
                act.wait_ge(gates_ready, b + 1)
                if not first:
                    act.wait_ge(top_step, TOP_STEPS * b)
                act.activation(gates[:, :, :].rearrange("s g e -> s (g e)"), bank_ab[0:S, 0, 0:2 * H * X], ACT.Copy).then_inc(gates_copied, 1)
                act.wait_ge(proj_ready, b + 1)
                if not first:
                    act.wait_ge(proj_stored[1 - p], 16 * (i + p))
                act.activation(proj[:, :], bank_ab[0:S, 1, 0:X * D], ACT.Copy).then_inc(proj_copied, 1)
                act.wait_ge(top_step, TOP_STEPS * b + TOP_BEST)
                act.activation(sig[:, :, :], best[:, :, 0:H], ACT.Exp, scale=-1.0).then_inc(negexp_done, 1)

            def main(b, p, i, first):
                for half in range(2):
                    act.wait_ge(q_ready, 2 * b + half + 1)
                    act.activation(qT[:, half * M2 // 2:(half + 1) * M2 // 2, :].rearrange("p m s -> p (m s)"),
                                   bank_ab[:, half, 0:M2 // 2 * S], ACT.Copy, scale=float(D) ** -0.5).then_inc(q_copied, 1)
                for n in range(4):
                    act.wait_ge(vt_ready, 4 * b + n + 1)
                    tokens = min(32, S - 32 * n)
                    for a in range(2):
                        src = bank_gh[64 * a:64 * a + 64, n % 2, 0:tokens * H].rearrange("p (t m a) -> p m t a", a=2, m=H // 2)[:, :, :, a]
                        act.activation(vT[64 * a:64 * a + 64, :, 32 * n:32 * n + tokens], src, ACT.Copy).then_inc(vt_copied, 1)
                for g in range(NG):
                    act.wait_ge(turned, NG * b + g + 1)
                    act.activation(probsT[:, g % 2, :], bank_t[0:S, 0:G * S], ACT.Exp).then_inc(exp_done, 1)
                    act.wait_ge(pv_done, NG * b + g + 1)
                    act.activation(attT[:, :, G * g:G * g + G], bank_o[0:W, 0:G * S].rearrange("w (j s) -> w s j", j=G), ACT.Copy).then_inc(attT_copied, 1)

            pipeline(act, pre, main)

        @block.vector
        def _(dve):
            gsz = [S, 2 * H, X]

            def pre(b, p, i, first):
                xb = c.X[:, bass.ds(b, 1), :].rearrange("s a e -> s (a e)")
                dve.bn_stats(stats[:, :], xb).then_inc(stats_done, 1)
                wait_all(dve, consts_done, (stats_done, b + 1))
                dve.bn_aggr(moments[:, :], stats[:, :]).then_inc(moments_done, 1)
                dve.wait_ge(rstd_done, b + 1)
                if not first:
                    dve.wait_ge(xt_ready, b)
                dve.tensor_scalar(xn[:, :], xb, moments[:, 0:1], rstd[:, 0:1], ALU.subtract, ALU.mult).then_inc(xn_done, 1)
                dve.wait_ge(gates_copied, b + 1)
                steps = 0

                def step(ins):
                    nonlocal steps
                    steps += 1
                    ins.then_inc(top_step, 1)
                    dve.wait_ge(top_step, TOP_STEPS * b + steps)

                if not first:
                    dve.wait_ge(negexp_done, b)
                src = gates
                for r in range(2):
                    step(dve.tensor_reduce(best[:, r, :], src[:, :, :], AXX, ALU.max))
                    step(dve.tensor_tensor(tie[:, :, :], src[:, :, :], best[:, r, :].unsqueeze(2).to_broadcast(gsz), ALU.is_ge))
                    step(dve.tensor_tensor(tie[:, :, :], tie[:, :, :], rank_w[:, :].unsqueeze(1).to_broadcast(gsz), ALU.mult))
                    step(dve.tensor_reduce(first_tie[:, :], tie[:, :, :], AXX, ALU.max))
                    step(dve.tensor_tensor(one_hot[:, r, :, :], tie[:, :, :], first_tie[:, :].unsqueeze(2).to_broadcast(gsz), ALU.is_ge))
                    if r == 0:
                        step(dve.scalar_tensor_tensor(rest[:, :, :], one_hot[:, 0, :, :], LEAST, gates[:, :, :], ALU.mult, ALU.add))
                    src = rest
                if not first:
                    dve.wait_ge(pick_stored[1 - p], 16 * (i + p))
                dve.tensor_tensor(pick[:, :, :], one_hot[:, 0, H:2 * H, :], one_hot[:, 1, H:2 * H, :], ALU.add).then_inc(pick_done, 1)
                dve.wait_ge(negexp_done, b + 1)
                step(dve.tensor_scalar(sig[:, :, :], sig[:, :, :], 1.0, None, ALU.add))
                step(dve.reciprocal(sig[:, :, :], sig[:, :, :]))
                for r in range(2):
                    last = dve.tensor_tensor(mix_part[:, r, :, :], one_hot[:, r, 0:H, :], sig[:, r, :].unsqueeze(2).to_broadcast([S, H, X]), ALU.mult)
                    last.then_inc(mix_part_done, 1)
                dve.wait_ge(mix_part_done, 2 * b + 2)
                if not first:
                    dve.wait_ge(mix_stored[1 - p], 16 * (i + p))
                dve.tensor_tensor(mix[:, :, :].rearrange("s e h -> s h e"), mix_part[:, 0, :, :], mix_part[:, 1, :, :], ALU.add).then_inc(mix_done, 1)

            def shift(b, g, first):
                dve.wait_ge(scores_ready, NG * b + g + 1)
                sc = bank_s[g % 2][0:S, 0:G * S].rearrange("s (j t) -> s j t", j=G)
                dve.tensor_reduce(neg_max[:, g % 2, :], sc, AXX, ALU.max).then_inc(max_done, 1)
                dve.wait_ge(max_done, NG * b + g + 1)
                if not (first and g < 2):
                    dve.wait_ge(turned, NG * b + g - 1)
                dve.tensor_tensor(shifted[:, g % 2, :, :], sc, neg_max[:, g % 2, :].unsqueeze(2).to_broadcast([S, G, S]), ALU.subtract).then_inc(shift_done, 1)

            def main(b, p, i, first):
                for half in range(2):
                    dve.wait_ge(kk_ready, 2 * b + half + 1)
                    for a in range(2):
                        dve.tensor_copy(kz[64 * a:64 * a + 64, half * M2 // 2:(half + 1) * M2 // 2, a, :],
                                        bank_ab[64 * a:64 * a + 64, half, 0:M2 // 2 * S].rearrange("p (m s) -> p m s", s=S)).then_inc(kk_copied, 1)
                shift(b, 0, first)
                for n in range(2):
                    dve.wait_ge(v_ready, 2 * b + n + 1)
                    if n == 0 and not first:
                        dve.wait_ge(pv_done, NG * b)
                    dve.tensor_copy(v[:, n * H // 2:(n + 1) * H // 2, 0:D], bank_gh[0:S, n, :].rearrange("s (h d) -> s h d", d=D)).then_inc(v_copied, 1)
                for g in range(1, NG):
                    shift(b, g, first)
                for n in range(2):
                    a = bank_gh[:, n, 0:7 * W].rearrange("p (t w) -> p t w", w=W)
                    dve.wait_ge(att_ready, 2 * b + n + 1)
                    dve.reciprocal(recip[:, 7 * n:7 * n + 7].unsqueeze(2), a[:, :, D:W]).then_inc(recip_done, 1)
                    dve.wait_ge(recip_done, 2 * b + n + 1)
                    dve.tensor_tensor(att[:, 7 * n:7 * n + 7, :, :], a[:, :, 0:D].unsqueeze(2).to_broadcast([P, 7, 2, D]),
                                      recip[:, 7 * n:7 * n + 7].unsqueeze(2).unsqueeze(3).to_broadcast([P, 7, 2, D]), ALU.mult).then_inc(att_done, 1)
                for n in range(2):
                    dve.wait_ge(u_ready, 2 * b + n + 1)
                    tokens = min(64, S - 64 * n)
                    for a in range(2):
                        src = bank_gh[64 * a:64 * a + 64, n, 0:tokens * X].rearrange("p (t m a) -> p m t a", a=2, m=X // 2)[:, :, :, a]
                        dve.tensor_copy(uT[64 * a:64 * a + 64, :, 64 * n:64 * n + tokens], src).then_inc(u_copied, 1)
                dve.wait_ge(y_ready, b + 1)
                xb = c.X[:, bass.ds(b, 1), :].rearrange("s a e -> s (a e)")
                dve.scalar_tensor_tensor(xb, bank_ab[0:S, 0, 0:E], c.tanh_g[:, 1:2], xb, ALU.mult, ALU.add).then_inc(out_done, 1)

            for t in (kz[:, :, :, :],):
                dve.memset(t, 0.0).then_inc(consts_done, 1)
            dve.memset(v[:, :, D:W], 1.0).then_inc(consts_done, 1)
            for e in range(X):
                last = dve.memset(rank_w[:, e:e + 1], float(X - e))
            last.then_inc(consts_done, 1)
            dve.wait_ge(consts_done, 4)
            pipeline(dve, pre, main)

        @block.gpsimd
        def _(pool):
            def pre(b, p, i, first):
                wait_all(pool, consts_done, (moments_done, b + 1))
                pool.tensor_scalar(var_eps[:, :], moments[:, 1:2], LN_EPS, None, ALU.add).then_inc(eps_added, 1)
                pool.wait_ge(eps_added, b + 1)
                pool.tensor_tensor(rstd[:, :], var_eps[:, :], minus_half[:, :], ALU.pow).then_inc(rstd_done, 1)

            def main(b, p, i, first):
                pool.wait_ge(te_loaded[p], 64 * i + 64)
                for k in range(T16):
                    if k == 0 and not first:
                        pool.wait_ge(vt_ready, 4 * b)
                    pool.tensor_tensor(mix_bd[:, k, :, :], mix_te[:, p, k, :].unsqueeze(1).to_broadcast([P, 16, H]),
                                       c.tok16[:, :].unsqueeze(2).to_broadcast([P, 16, H]), ALU.mult).then_inc(mix_bd_done, 1)
                for n in range(T8):
                    if n == 0 and not first:
                        pool.wait_ge(u_ready, 2 * b)
                    pool.tensor_tensor(pick_bd[:, n, :, :], pick_th[:, p, n, :].unsqueeze(1).to_broadcast([P, 16, X]),
                                       c.tok8[:, n % 2, :].unsqueeze(2).to_broadcast([P, 16, X]), ALU.mult).then_inc(pick_bd_done, 1)

            pool.memset(minus_half[:, :], -0.5).then_inc(consts_done, 1)
            pool.wait_ge(consts_done, 4)
            pipeline(pool, pre, main)


class Names:
    pass


def flamingo_kernel(nc, ins, out):
    d = Names()
    (d.x, d.ctx, d.mask, d.g_xattn, d.g_ffn, d.wq, d.bq, d.wk, d.bk, d.wv, d.bv, d.wo, d.bo,
     d.wq2, d.wk2, d.wv2, d.ws, d.wd, d.wo2) = ins
    d.out = out
    z = Shapes(d.x, d.ctx, d.wq2, d.wv2)
    with ExitStack() as ctx:
        sb = lambda name, shape: ctx.enter_context(nc.sbuf_tensor(name, shape, F32))
        c = Names()
        c.X = sb("X", [z.S, z.B, z.E])
        c.ident = sb("ident", [P, P])
        c.headmask = sb("headmask", [P, z.HT])
        c.tok16, c.tok8 = sb("tok16", [P, 16]), sb("tok8", [P, 2, 16])
        c.tanh_g = sb("tanh_g", [z.S, 2])
        c.wq2T, c.wk2T = sb("wq2T", [P, z.EC, z.M2 * P]), sb("wk2T", [P, z.EC, z.M2 * P])
        c.wv2T = sb("wv2T", [P, z.EC, z.X * z.D2])
        c.wgT = sb("wgT", [P, z.EC, 2 * z.H2 * z.X])
        c.wo2T = sb("wo2T", [P, z.X // 2, z.E])
        with ExitStack() as inner:
            sb1 = lambda name, shape: inner.enter_context(nc.sbuf_tensor(name, shape, F32))
            c.QT = sb1("QT", [P, z.EC, z.B * z.S])
            c.wq, c.wk, c.wv, c.wo = (sb1(n, [P, z.EC, z.E]) for n in ("wq_sb", "wk_sb", "wv_sb", "wo_sb"))
            c.bk, c.bv = sb1("bk_sb", [P, z.EC]), sb1("bv_sb", [z.KP, z.E])
            c.maskb = sb1("maskb", [z.S, z.S2])
            prepare(nc, z, d, c)
            cross(nc, z, d, c)
        switch(nc, z, d, c)


_INS = ['x', 'ctx_1024', 'mask_1x1xSxS2_fk1', 'g_xattn', 'g_ffn', 'L0_xattn_wq', 'L0_xattn_bq', 'L0_xattn_wk',
        'L0_xattn_bk', 'L0_xattn_wv', 'L0_xattn_bv', 'L0_xattn_wo', 'L0_xattn_bo', 'L0_ffn_Wq', 'L0_ffn_Wk',
        'L0_ffn_Wv', 'L0_ffn_Ws', 'L0_ffn_Wd', 'L0_ffn_Wo']


def kernel(**inputs):
    import numpy as _np
    import concourse.bacc as _bacc
    from concourse import mybir as _mybir
    from concourse.bass_utils import run_bass_kernel_spmd as _run

    nc = _bacc.Bacc("TRN2", target_bir_lowering=False, num_devices=1)
    arrays, args = {}, []
    for name in _INS:
        a = _np.ascontiguousarray(inputs[name])
        arrays[f"in_{name}_dram"] = a
        args.append(nc.dram_tensor(f"in_{name}_dram", a.shape, _mybir.dt.from_np(a.dtype), kind="ExternalInput").ap())
    out = nc.dram_tensor("out_0_dram", inputs["x"].shape, _mybir.dt.float32, kind="ExternalOutput").ap()
    flamingo_kernel(nc, args, out)
    r = _run(nc, [arrays], core_ids=[0])
    return r.results[0]["out_0_dram"]
```

```python
from contextlib import ExitStack

import concourse.bass as bass
from concourse import mybir

F32 = mybir.dt.float32
ALU = mybir.AluOpType
ACT = mybir.ActivationFunctionType
AXX = mybir.AxisListType.X

P = 128
PSUM_BANK = 512
LN_EPS = 1e-5
MASK_SCALE = -1e9
LEAST = -3.0e38


def wait_all(eng, met, *waits):
    waits = [(sem, n if isinstance(n, int) else eng.to_reg(n)) for sem, n in waits]
    eng.wait_ge(met, 1)
    for sem, n in waits:
        eng.wait_ge(sem, n)


def flat(ap):
    return ap.rearrange("a s e -> (a s) e")


class Shapes:

    def __init__(self, x, ctx, wq2, wv2):
        self.B, self.S, self.E = x.shape
        self.S2 = ctx.shape[1]
        self.H, self.D = 16, self.E // 16
        self.KC, self.KP = 3, self.S2 // 3
        self.G = 4
        self.H2, self.D2, _ = wq2.shape
        self.X = wv2.shape[0]
        self.EC = self.E // P
        self.HT = P // self.D
        self.M2 = self.H2 * self.D2 // P
        assert self.KC * self.KP == self.S2 and self.KP <= P and self.B % 4 == 0


def prepare(nc, z, d, c):
    B, S, E, EC, HT = z.B, z.S, z.E, z.EC, z.HT
    GB = 4
    NG = B // GB
    with ExitStack() as ctx:
        sb = lambda name, shape: ctx.enter_context(nc.sbuf_tensor(name, shape, F32))
        ps = lambda name, shape: ctx.enter_context(nc.psum_tensor(name, shape, F32))
        sem = lambda name: ctx.enter_context(nc.semaphore(name))
        wq_in, wk_in = sb("wq_in", [P, z.M2, E]), sb("wk_in", [P, z.M2, E])
        wv_in = sb("wv_in", [P, z.X * z.D2 // P, E])
        wg_in = sb("wg_in", [P, 2, E])
        wo_in = sb("wo_in", [P, EC, z.X, z.D2])
        bq = sb("bq", [P, EC])
        bo = sb("bo", [S, E])
        gates_in = sb("gates_in", [S, 2])
        stats, moments = sb("stats", [S, GB, 6]), sb("moments", [S, 2, GB, 2])
        minus_half = sb("minus_half", [S, GB])
        var_eps, rstd = sb("var_eps", [S, GB]), sb("rstd", [S, 2, GB])
        xn, xnT = sb("xn", [S, 2, GB, E]), sb("xnT", [P, 2, EC, GB * S])
        psum_t = [ps(f"p_t{i}", [P, PSUM_BANK]) for i in range(2)]
        psum_x = [ps(f"p_x{i}", [P, EC, S]) for i in range(2)]
        psum_q = [ps(f"p_q{i}", [P, PSUM_BANK]) for i in range(2)]
        x_loaded = [sem(f"x_loaded{i}") for i in range(2)]
        small_loaded, weights_loaded = sem("small_loaded"), sem("weights_loaded")
        cross_loaded = sem("cross_loaded")
        zeroed, consts_ready = sem("zeroed"), sem("consts_ready")
        stats_done, moments_done = sem("stats_done"), sem("moments_done")
        eps_added, rstd_done = sem("eps_added"), sem("rstd_done")
        xn_done, xbias_done = sem("xn_done"), sem("xbias_done")
        xt_ready, xt_copied = sem("xt_ready"), sem("xt_copied")
        q_ready, q_copied = sem("q_ready"), sem("q_copied")
        wt_ready, wt_copied = sem("wt_ready"), sem("wt_copied")
        tanh_done, bias_done = sem("tanh_done"), sem("bias_done")
        block = ctx.enter_context(nc.Block())

        turns = []
        for src, dst, tiles in ((wq_in, c.wq2T, z.M2), (wk_in, c.wk2T, z.M2), (wv_in, c.wv2T, z.X * z.D2 // P)):
            for e in range(EC):
                for m in range(0, tiles, 4):
                    turns.append(([src[:, m + k, e * P:(e + 1) * P] for k in range(4)],
                                  dst[:, e, m * P:(m + 4) * P]))
        turns.append(([wg_in[:, k, e * P:(e + 1) * P] for e in range(EC) for k in range(2)],
                      c.wgT[:, :, :].rearrange("p e n -> p (e n)")))
        for m in range(0, z.X // 2, 2):
            turns.append(([wo_in[:, f, 2 * (m + k):2 * (m + k) + 2, :].rearrange("p e d -> p (e d)")
                           for k in range(2) for f in range(EC)],
                          c.wo2T[:, m:m + 2, :].rearrange("p e f -> p (e f)")))

        @block.sync
        def _(sp):
            with nc.allow_non_contiguous_dma(reason="biases, one column each"):
                sp.dma_start(bq[:, :], d.bq.rearrange("(t p) -> p t", p=P)).then_inc(small_loaded, 16)
                sp.dma_start(c.bk[:, :], d.bk.rearrange("(t p) -> p t", p=P)).then_inc(small_loaded, 16)
            row = lambda v: v.rearrange("(a n) -> a n", a=1)
            sp.dma_start(bo[:, :], row(d.bo).to_broadcast([S, E])).then_inc(small_loaded, 16)
            sp.dma_start(c.bv[:, :], row(d.bv).to_broadcast([z.KP, E])).then_inc(small_loaded, 16)
            sp.dma_start(gates_in[:, 0:1], row(d.g_xattn).to_broadcast([S, 1])).then_inc(small_loaded, 16)
            sp.dma_start(gates_in[:, 1:2], row(d.g_ffn).to_broadcast([S, 1])).then_inc(small_loaded, 16)
            sp.dma_start(c.maskb[:, :], d.mask.rearrange("a b s k -> (a b s) k")).then_inc(small_loaded, 16)
            sp.dma_start(c.wq[:, :, :], d.wq.rearrange("(e p) n -> p e n", p=P)).then_inc(small_loaded, 16)
            xs = d.x.rearrange("b s e -> s b e")

            def load_x(i, p):
                g = 2 * i + p
                sp.dma_start(c.X[:, bass.ds(GB * g, GB), :], xs[:, bass.ds(GB * g, GB), :]).then_inc(x_loaded[p], 16)

            load_x(0, 0)
            load_x(0, 1)
            with sp.Fori(1, NG // 2) as i:
                for p in range(2):
                    sp.wait_ge(x_loaded[p], 16 * i)
                    load_x(i, p)

        @block.scalar
        def _(act):
            for dst, src in ((c.wk, d.wk), (c.wv, d.wv), (c.wo, d.wo)):
                act.dma_start(dst[:, :, :], src.rearrange("(e p) n -> p e n", p=P)).then_inc(cross_loaded, 16)
            act.dma_start(wq_in[:, :, :], d.wq2.rearrange("h d c -> (h d) c").rearrange("(m p) c -> p m c", p=P)).then_inc(weights_loaded, 16)
            act.dma_start(wk_in[:, :, :], d.wk2.rearrange("h d c -> (h d) c").rearrange("(m p) c -> p m c", p=P)).then_inc(weights_loaded, 16)
            act.dma_start(wv_in[:, :, :], d.wv2.rearrange("h d c -> (h d) c").rearrange("(m p) c -> p m c", p=P)).then_inc(weights_loaded, 16)
            act.dma_start(wg_in[:, 0, :], d.ws.rearrange("h e c -> (h e) c")).then_inc(weights_loaded, 16)
            act.dma_start(wg_in[:, 1, :], d.wd.rearrange("h e c -> (h e) c")).then_inc(weights_loaded, 16)
            for f in range(EC):
                act.dma_start(wo_in[:, f, :, :], d.wo2[:, f * P:(f + 1) * P, :].rearrange("e f d -> f e d")).then_inc(weights_loaded, 16)
            act.wait_ge(small_loaded, 16 * 8)
            act.activation(c.tanh_g[:, :], gates_in[:, :], ACT.Tanh).then_inc(tanh_done, 1)
            act.wait_ge(bias_done, 1)
            with act.Fori(0, NG // 2) as i:
                for p in range(2):
                    g = 2 * i + p
                    for j in range(GB):
                        act.wait_ge(xt_ready, GB * g + j + 1)
                        act.activation(xnT[:, p, :, j * S:(j + 1) * S], psum_x[j % 2][:, :, :], ACT.Copy).then_inc(xt_copied, 1)
                    for t in range(EC):
                        act.wait_ge(q_ready, EC * g + t + 1)
                        act.activation(c.QT[:, t, bass.ds(GB * S * g, GB * S)], psum_q[t][:, 0:GB * S], ACT.Identity,
                                       bias=bq[:, t:t + 1], scale=float(z.D) ** -0.5).then_inc(q_copied, 1)
            for n, (_, dst) in enumerate(turns):
                act.wait_ge(wt_ready, n + 1)
                act.activation(dst, psum_t[n % 2][:, :], ACT.Copy).then_inc(wt_copied, 1)
            act.wait_ge(cross_loaded, 16 * 3)

        @block.gpsimd
        def _(pool):
            pool.memset(c.ident[:, :], 0.0).then_inc(zeroed, 1)
            pool.memset(c.headmask[:, :], 1.0).then_inc(zeroed, 1)
            pool.memset(c.tok16[:, :], 1.0).then_inc(zeroed, 1)
            pool.memset(c.tok8[:, :, :], 1.0).then_inc(zeroed, 1)
            pool.memset(minus_half[:, :], -0.5).then_inc(zeroed, 1)
            pool.wait_ge(zeroed, 5)
            steps = 0

            def keep(t, compare, fill, base, pattern, mult):
                nonlocal steps
                nc.gpsimd.affine_select(out=t, in_=t, compare_op=compare, fill=fill, base=base,
                                        pattern=pattern, channel_multiplier=mult).then_inc(consts_ready, 1)
                steps += 1
                pool.wait_ge(consts_ready, steps)

            keep(c.ident[:, :], ALU.not_equal, 1.0, 0, [[-1, P]], 1)
            for t, base, pattern, width in (
                (c.headmask[:, :], 0, [[-z.D, HT]], z.D),
                (c.tok16[:, :], 0, [[-z.X, 16]], z.X),
                (c.tok8[:, :, :], 0, [[8 * z.H2, 2], [-z.H2, 16]], z.H2),
            ):
                keep(t, ALU.is_ge, 0.0, base, pattern, 1)
                keep(t, ALU.is_ge, 0.0, width - 1 - base, [[-a, n] for a, n in pattern], -1)
            with pool.Fori(0, NG // 2) as i:
                for p in range(2):
                    g = 2 * i + p
                    wait_all(pool, zeroed, (moments_done, GB * g + GB))
                    pool.tensor_scalar(var_eps[:, :], moments[:, p, :, 1], LN_EPS, None, ALU.add).then_inc(eps_added, 1)
                    pool.wait_ge(eps_added, g + 1)
                    pool.tensor_tensor(rstd[:, p, :], var_eps[:, :], minus_half[:, :], ALU.pow).then_inc(rstd_done, 1)
                    pool.wait_ge(bias_done, 2)
                    pool.wait_ge(xn_done, GB * g + GB)
                    for j in range(GB):
                        xb = c.X[:, bass.ds(GB * g + j, 1), :].rearrange("s a e -> s (a e)")
                        pool.tensor_tensor(xb, xb, bo[:, :], ALU.add).then_inc(xbias_done, 1)

        @block.vector
        def _(dve):
            dve.wait_ge(small_loaded, 16 * 8)
            dve.tensor_scalar(bq[:, :], bq[:, :], float(z.D) ** -0.5, None, ALU.mult).then_inc(bias_done, 1)
            dve.wait_ge(tanh_done, 1)
            dve.tensor_scalar(bo[:, :], bo[:, :], c.tanh_g[:, 0:1], None, ALU.mult).then_inc(bias_done, 1)
            dve.tensor_scalar(c.maskb[:, :], c.maskb[:, :], MASK_SCALE, None, ALU.mult).then_inc(bias_done, 1)

            def group(i, p, first):
                g = 2 * i + p
                entry = lambda j: c.X[:, bass.ds(GB * g + j, 1), :].rearrange("s a e -> s (a e)")
                dve.wait_ge(x_loaded[p], 16 * i + 16)
                for j in range(GB):
                    dve.bn_stats(stats[:, j, :], entry(j)).then_inc(stats_done, 1)
                for j in range(GB):
                    wait_all(dve, small_loaded, (stats_done, GB * g + j + 1))
                    dve.bn_aggr(moments[:, p, j, :], stats[:, j, :]).then_inc(moments_done, 1)
                dve.wait_ge(rstd_done, g + 1)
                if not first:
                    dve.wait_ge(xt_ready, GB * g - GB)
                for j in range(GB):
                    dve.tensor_scalar(xn[:, p, j, :], entry(j), moments[:, p, j, 0:1], rstd[:, p, j:j + 1],
                                      ALU.subtract, ALU.mult).then_inc(xn_done, 1)

            group(0, 0, True)
            group(0, 1, True)
            with dve.Fori(1, NG // 2) as i:
                group(i, 0, False)
                group(i, 1, False)

        @block.tensor
        def _(pe):
            pe.wait_ge(consts_ready, 7)
            pe.wait_ge(small_loaded, 16 * 8)

            def group(i, p, first):
                g = 2 * i + p
                for j in range(GB):
                    pe.wait_ge(xn_done, GB * g + j + 1)
                    if not (first and j < 2):
                        pe.wait_ge(xt_copied, GB * g + j - 1)
                    for e in range(EC):
                        last = nc.tensor.transpose(psum_x[j % 2][:, e, :], xn[:, p, j, e * P:(e + 1) * P], c.ident[0:S, 0:S])
                    last.then_inc(xt_ready, 1)
                pe.wait_ge(xt_copied, GB * g + GB)
                for t in range(EC):
                    if not first:
                        pe.wait_ge(q_copied, EC * g - EC + t + 1)
                    for e in range(EC):
                        last = nc.tensor.matmul(psum_q[t][:, 0:GB * S], c.wq[:, e, t * P:(t + 1) * P], xnT[:, p, e, :],
                                                start=(e == 0), stop=(e == EC - 1))
                    last.then_inc(q_ready, 1)

            group(0, 0, True)
            group(0, 1, False)
            with pe.Fori(1, NG // 2) as i:
                group(i, 0, False)
                group(i, 1, False)
            pe.wait_ge(weights_loaded, 16 * 7)
            for n, (srcs, _) in enumerate(turns):
                if n >= 2:
                    pe.wait_ge(wt_copied, n - 1)
                for k, src in enumerate(srcs):
                    last = nc.tensor.transpose(psum_t[n % 2][:, k * P:(k + 1) * P], src, c.ident[:, :])
                last.then_inc(wt_ready, 1)


def cross(nc, z, d, c):
    B, S, E, EC, HT, H, G, KC, KP, S2, D = z.B, z.S, z.E, z.EC, z.HT, z.H, z.G, z.KC, z.KP, z.S2, z.D
    NG = H // G
    VW = 32
    with ExitStack() as ctx:
        sb = lambda name, shape: ctx.enter_context(nc.sbuf_tensor(name, shape, F32))
        ps = lambda name, shape: ctx.enter_context(nc.psum_tensor(name, shape, F32))
        sem = lambda name: ctx.enter_context(nc.semaphore(name))
        ctx_in = sb("ctx_in", [KP, 2, KC, E])
        ctxT = sb("ctxT", [P, EC, S2])
        KT = sb("KT", [P, 2, EC, S2])
        V = sb("V", [KP, 2, KC, H, VW])
        Qz = sb("Qz", [P, 2, EC, HT, S])
        raw = sb("raw", [S, 2, G, S2])
        neg_max = sb("neg_max", [S, 2, G])
        shifted = sb("shifted", [S, 2, G, S2])
        probsT = sb("probsT", [KP, 2, KC, G * S])
        headsT = sb("headsT", [P, NG * S])
        recip = sb("recip", [S, H])
        heads = sb("heads", [S, H, D])
        outT = sb("outT", [P, EC, S])
        bank_s = [ps(f"bank_s{i}", [P, PSUM_BANK]) for i in range(2)]
        bank_t = ps("bank_t", [P, KC, PSUM_BANK])
        bank_o = ps("bank_o", [P, PSUM_BANK])
        bank_ab = ps("bank_ab", [P, 2, PSUM_BANK])
        ctx_loaded = [sem(f"ctx_loaded{i}") for i in range(2)]
        v_cleared, v_set = sem("v_cleared"), sem("v_set")
        ctxT_ready, ctxT_copied = sem("ctxT_ready"), sem("ctxT_copied")
        k_ready, k_copied = sem("k_ready"), sem("k_copied")
        va_ready, vb_ready, v_copied = sem("va_ready"), sem("vb_ready"), sem("v_copied")
        qz_ready = sem("qz_ready")
        scores_ready, scores_read, shift_done = sem("scores_ready"), sem("scores_read"), sem("shift_done")
        turned, exp_done, pv_done = sem("turned"), sem("exp_done"), sem("pv_done")
        headsT_copied, heads_ready, recip_done, heads_done = sem("headsT_copied"), sem("heads_ready"), sem("recip_done"), sem("heads_done")
        outT_ready, outT_copied, y_ready, x_done = sem("outT_ready"), sem("outT_copied"), sem("y_ready"), sem("x_done")
        block = ctx.enter_context(nc.Block())

        def batches(eng, body):
            body(0, 0, True, False)
            body(1, 1, False, False)
            with eng.Fori(1, B // 2 - 1) as i:
                body(2 * i, 0, False, False)
                body(2 * i + 1, 1, False, False)
            body(B - 2, 0, False, False)
            body(B - 1, 1, False, True)

        @block.sync
        def _(sp):
            def load(b, p):
                sp.dma_start(ctx_in[:, p, :, :], flat(d.ctx[bass.ds(b, 1)]).rearrange("(k p) e -> p k e", p=KP)).then_inc(ctx_loaded[p], 16)

            load(0, 0)
            load(1, 1)
            with sp.Fori(1, B // 2) as i:
                for p in range(2):
                    sp.wait_ge(ctxT_ready, 2 * i + p - 1)
                    load(2 * i + p, p)

        @block.tensor
        def _(pe):
            def transposes(b, i, p, first):
                pe.wait_ge(ctx_loaded[p], 16 * i + 16)
                if not first:
                    pe.wait_ge(v_copied, 2 * b)
                for e in range(EC):
                    for k in range(KC):
                        last = nc.tensor.transpose(bank_ab[:, e, k * KP:(k + 1) * KP],
                                                   ctx_in[:, p, k, e * P:(e + 1) * P], c.ident[0:KP, 0:KP])
                last.then_inc(ctxT_ready, 1)

            def keys(b):
                pe.wait_ge(ctxT_copied, b + 1)
                for t in range(EC):
                    for e in range(EC):
                        last = nc.tensor.matmul(bank_ab[:, t, 0:S2], c.wk[:, e, t * P:(t + 1) * P], ctxT[:, e, :],
                                                start=(e == 0), stop=(e == EC - 1))
                    last.then_inc(k_ready, 1)

            def values(k):
                for e in range(EC):
                    last = nc.tensor.matmul(bank_ab[0:KP, k // 2, (k % 2) * E:(k % 2 + 1) * E], ctxT[:, e, k * KP:(k + 1) * KP],
                                            c.wv[:, e, :], start=(e == 0), stop=(e == EC - 1))
                return last

            def scores(b, p, g, first):
                if g == 0:
                    pe.wait_ge(qz_ready, NG * b + NG)
                    pe.wait_ge(k_copied, EC * b + EC)
                for j in range(G):
                    h = G * g + j
                    if not (first and h < 2):
                        pe.wait_ge(scores_read, H * b + h - 1)
                    nc.tensor.matmul(bank_s[h % 2][0:S, 0:S2], Qz[:, p, h // HT, h % HT, :], KT[:, p, h // HT, :],
                                     start=True, stop=True).then_inc(scores_ready, 1)

            def turn(b, g, first):
                pe.wait_ge(shift_done, H * b + G * g + G)
                if not (first and g == 0):
                    pe.wait_ge(exp_done, NG * b + g)
                for k in range(KC):
                    for j in range(G):
                        last = nc.tensor.transpose(bank_t[0:KP, k, j * S:(j + 1) * S],
                                                   shifted[:, g % 2, j, k * KP:(k + 1) * KP], c.ident[0:S, 0:S])
                last.then_inc(turned, 1)

            def weigh(b, p, g, first):
                pe.wait_ge(exp_done, NG * b + g + 1)
                if g == 0:
                    pe.wait_ge(v_copied, 2 * b + 2)
                    if first:
                        pe.wait_ge(v_set, 1)
                    else:
                        pe.wait_ge(headsT_copied, b)
                for j in range(G):
                    for k in range(KC):
                        last = nc.tensor.matmul(bank_o[j * VW:(j + 1) * VW, g * S:(g + 1) * S], V[:, p, k, G * g + j, :],
                                                probsT[:, g % 2, k, j * S:(j + 1) * S], start=(k == 0), stop=(k == KC - 1))
                last.then_inc(pv_done, 1)

            def heads_back(b):
                pe.wait_ge(headsT_copied, b + 1)
                for g in range(NG):
                    last = nc.tensor.transpose(bank_ab[0:S, 0, g * P:(g + 1) * P], headsT[:, g * S:(g + 1) * S], c.ident[:, :])
                last.then_inc(heads_ready, 1)

            def heads_turn(b):
                pe.wait_ge(heads_done, b + 1)
                flat_heads = heads[:, :, :].rearrange("s h d -> s (h d)")
                for e in range(EC):
                    last = nc.tensor.transpose(bank_ab[:, 1, e * S:(e + 1) * S], flat_heads[:, e * P:(e + 1) * P], c.ident[0:S, 0:S])
                last.then_inc(outT_ready, 1)

            def project(b):
                pe.wait_ge(outT_copied, b + 1)
                for e in range(EC):
                    last = nc.tensor.matmul(bank_ab[0:S, 1, 0:E], outT[:, e, :], c.wo[:, e, :], start=(e == 0), stop=(e == EC - 1))
                last.then_inc(y_ready, 1)

            def body(b, p, first, last, i):
                scores(b, p, 0, first)
                if not first:
                    turn(b - 1, NG - 1, False)
                if not last:
                    transposes(b + 1, i + p, 1 - p, False)
                if not first:
                    weigh(b - 1, 1 - p, NG - 1, False)
                scores(b, p, 1, False)
                if not last:
                    keys(b + 1)
                turn(b, 0, first)
                if not first:
                    if not last:
                        pe.wait_ge(k_copied, EC * b + EC + 1)
                    heads_back(b - 1)
                weigh(b, p, 0, first)
                scores(b, p, 2, False)
                turn(b, 1, False)
                if not last:
                    pe.wait_ge(k_copied, EC * b + 2 * EC)
                if not first:
                    heads_turn(b - 1)
                if not last:
                    values(0)
                    values(1).then_inc(va_ready, 1)
                weigh(b, p, 1, False)
                if not first:
                    project(b - 1)
                scores(b, p, 3, False)
                turn(b, 2, False)
                if not last:
                    if not first:
                        pe.wait_ge(x_done, b)
                    values(2).then_inc(vb_ready, 1)
                weigh(b, p, 2, False)

            transposes(0, 0, 0, True)
            keys(0)
            pe.wait_ge(k_copied, EC)
            values(0)
            values(1).then_inc(va_ready, 1)
            values(2).then_inc(vb_ready, 1)
            body(0, 0, True, False, 0)
            body(1, 1, False, False, 0)
            with pe.Fori(1, B // 2 - 1) as i:
                body(2 * i, 0, False, False, i)
                body(2 * i + 1, 1, False, False, i)
            body(B - 2, 0, False, False, B // 2 - 1)
            body(B - 1, 1, False, True, B // 2 - 1)
            turn(B - 1, NG - 1, False)
            weigh(B - 1, 1, NG - 1, False)
            heads_back(B - 1)
            heads_turn(B - 1)
            project(B - 1)

        @block.scalar
        def _(act):
            def ctx_copy(b, first):
                act.wait_ge(ctxT_ready, b + 1)
                if not first:
                    act.wait_ge(vb_ready, b)
                act.activation(ctxT[:, :, :], bank_ab[:, :, 0:S2], ACT.Copy).then_inc(ctxT_copied, 1)

            def key_copy(b, p, first):
                for t in range(EC):
                    act.wait_ge(k_ready, EC * b + t + 1)
                    if t == 0 and not first:
                        act.wait_ge(scores_ready, H * (b - 1))
                    act.activation(KT[:, p, t, :], bank_ab[:, t, 0:S2], ACT.Identity, bias=c.bk[:, t:t + 1]).then_inc(k_copied, 1)

            def exps(b, g, first):
                act.wait_ge(turned, NG * b + g + 1)
                if not (first and g < 2):
                    act.wait_ge(pv_done, NG * b + g - 1)
                act.activation(probsT[:, g % 2, :, :], bank_t[0:KP, :, 0:G * S], ACT.Exp).then_inc(exp_done, 1)

            def heads_copy(b, first):
                act.wait_ge(pv_done, NG * b + NG)
                if not first:
                    act.wait_ge(heads_ready, b)
                act.activation(headsT[:, :], bank_o[:, 0:NG * S], ACT.Copy).then_inc(headsT_copied, 1)

            def out_copy(b, first):
                act.wait_ge(outT_ready, b + 1)
                if not first:
                    act.wait_ge(y_ready, b)
                act.activation(outT[:, :, :].rearrange("p e s -> p (e s)"), bank_ab[:, 1, 0:EC * S], ACT.Copy).then_inc(outT_copied, 1)

            def body(b, p, first, last):
                second = isinstance(b, int) and b == 1
                if not first:
                    exps(b - 1, NG - 1, False)
                if not last:
                    ctx_copy(b + 1, False)
                if not first:
                    heads_copy(b - 1, second)
                if not last:
                    key_copy(b + 1, 1 - p, first)
                exps(b, 0, first)
                exps(b, 1, first)
                if not first:
                    out_copy(b - 1, second)
                exps(b, 2, False)

            ctx_copy(0, True)
            key_copy(0, 0, True)
            batches(act, body)
            exps(B - 1, NG - 1, False)
            heads_copy(B - 1, False)
            out_copy(B - 1, False)

        @block.vector
        def _(dve):
            dve.memset(V[:, :, :, :, :], 0.0).then_inc(v_cleared, 1)
            dve.wait_ge(v_cleared, 1)
            for p in range(2):
                for k in range(KC):
                    last_set = dve.memset(V[:, p, k, :, D:D + 1], 1.0)
            last_set.then_inc(v_set, 1)

            def value_copy(b, p, half):
                dve.wait_ge(va_ready if half == 0 else vb_ready, b + 1)
                for k in ((0, 1) if half == 0 else (2,)):
                    last = dve.tensor_tensor(V[:, p, k, :, 0:D],
                                             bank_ab[0:KP, k // 2, (k % 2) * E:(k % 2 + 1) * E].rearrange("p (h d) -> p h d", d=D),
                                             c.bv[:, :].rearrange("p (h d) -> p h d", d=D), ALU.add)
                last.then_inc(v_copied, 1)

            def score_max(b, g, first):
                for j in range(G):
                    h = G * g + j
                    free = [] if first and h < 2 * G else [(shift_done, H * b + h - 2 * G + 1)]
                    wait_all(dve, v_set, (scores_ready, H * b + h + 1), *free)
                    dve.tensor_tensor_reduce(raw[:, g % 2, j, :], bank_s[h % 2][0:S, 0:S2], c.maskb[:, :], -1.0, -LEAST,
                                             ALU.add, ALU.min, neg_max[:, g % 2, j:j + 1]).then_inc(scores_read, 1)

            def normalise(b, first):
                sums = bank_ab[0:S, 0, :].rearrange("s (h w) -> s h w", w=VW)
                dve.wait_ge(heads_ready, b + 1)
                if not first:
                    dve.wait_ge(heads_done, b)
                dve.reciprocal(recip[:, :].unsqueeze(2), sums[:, :, D:D + 1]).then_inc(recip_done, 1)
                dve.wait_ge(recip_done, b + 1)
                if not first:
                    dve.wait_ge(outT_ready, b)
                dve.tensor_tensor(heads[:, :, :], sums[:, :, 0:D], recip[:, :].unsqueeze(2).to_broadcast([S, H, D]), ALU.mult).then_inc(heads_done, 1)

            def residual(b):
                dve.wait_ge(y_ready, b + 1)
                xb = c.X[:, bass.ds(b, 1), :].rearrange("s a e -> s (a e)")
                dve.scalar_tensor_tensor(xb, bank_ab[0:S, 1, 0:E], c.tanh_g[:, 0:1], xb, ALU.mult, ALU.add).then_inc(x_done, 1)

            def body(b, p, first, last):
                second = isinstance(b, int) and b == 1
                score_max(b, 0, first)
                score_max(b, 1, first)
                if not first:
                    normalise(b - 1, second)
                score_max(b, 2, False)
                if not last:
                    value_copy(b + 1, 1 - p, 0)
                if not first:
                    residual(b - 1)
                score_max(b, 3, False)
                if not last:
                    value_copy(b + 1, 1 - p, 1)

            dve.wait_ge(v_set, 1)
            value_copy(0, 0, 0)
            value_copy(0, 0, 1)
            batches(dve, body)
            normalise(B - 1, False)
            residual(B - 1)

        @block.gpsimd
        def _(pool):
            def spread(b, p, n, first):
                t, h0 = G * n // HT, G * n % HT
                if n == 0 and not first:
                    pool.wait_ge(scores_ready, H * (b - 1))
                q = c.QT[:, t, bass.ds(S * b, S)]
                pool.tensor_tensor(Qz[:, p, t, h0:h0 + G, :], q.unsqueeze(1).to_broadcast([P, G, S]),
                                   c.headmask[:, h0:h0 + G].unsqueeze(2).to_broadcast([P, G, S]), ALU.mult).then_inc(qz_ready, 1)

            def body(b, p, first, last):
                for g in range(NG):
                    for j in range(G):
                        h = G * g + j
                        free = [] if j or (first and g < 2) else [(turned, NG * b + g - 1)]
                        wait_all(pool, v_set, (scores_read, H * b + h + 1), *free)
                        pool.tensor_scalar(shifted[:, g % 2, j, :], raw[:, g % 2, j, :], -1.0, neg_max[:, g % 2, j:j + 1],
                                           ALU.mult, ALU.add).then_inc(shift_done, 1)
                    if not last:
                        spread(b + 1, 1 - p, g, first)

            for n in range(NG):
                spread(0, 0, n, True)
            batches(pool, body)


def switch(nc, z, d, c):
    B, S, E, EC, G, H, D, X, M2 = z.B, z.S, z.E, z.EC, z.G, z.H2, z.D2, z.X, z.M2
    NG = H // G
    T16, T8 = S // 16, S // 8
    W = D + 1
    TOP_STEPS, TOP_BEST = 13, 7
    with ExitStack() as ctx:
        sb = lambda name, shape: ctx.enter_context(nc.sbuf_tensor(name, shape, F32))
        ps = lambda name, shape: ctx.enter_context(nc.psum_tensor(name, shape, F32))
        sem = lambda name: ctx.enter_context(nc.semaphore(name))
        dram = lambda name, shape: nc.dram_tensor(name, shape, F32).ap()
        proj_dram = dram("proj_dram", (B, S, X * D))
        mix_dram = dram("mix_dram", (B, S, X * H))
        pick_dram = dram("pick_dram", (B, S, H * X))

        minus_half = sb("minus_half2", [S, 1])
        rank_w = sb("rank_w", [S, X])
        stats, moments = sb("stats2", [S, 6]), sb("moments2", [S, 2])
        var_eps, rstd = sb("var_eps2", [S, 1]), sb("rstd2", [S, 1])
        xn = sb("xn2", [S, E])
        xnT = sb("xnT2", [P, 2, EC, S])
        gates = sb("gates", [S, 2 * H, X])
        proj = sb("proj", [S, X * D])
        best = sb("best", [S, 2, 2 * H])
        tie = sb("tie", [S, 2 * H, X])
        first_tie = sb("first_tie", [S, 2 * H])
        one_hot = sb("one_hot", [S, 2, 2 * H, X])
        rest = sb("rest", [S, 2 * H, X])
        sig = sb("sig", [S, 2, H])
        mix_part = sb("mix_part", [S, 2, H, X])
        mix, pick = sb("mix", [S, X, H]), sb("pick", [S, H, X])
        proj_te = sb("proj_te", [P, 2, T16, 2, D])
        mix_te = sb("mix_te", [P, 2, T16, H])
        pick_th = sb("pick_th", [P, 2, T8, X])
        mix_bd = sb("mix_bd", [P, T16, 16, H])
        pick_bd = sb("pick_bd", [P, T8, 16, X])
        qT = sb("qT", [P, 2, M2, S])
        kz = sb("kz", [P, 2, M2, 2, S])
        vT = sb("vT", [P, H // 2, S])
        v = sb("v", [S, 2, H, W])
        neg_max = sb("max2", [S, 2, G])
        shifted = sb("shifted2", [S, 2, G, S])
        probsT = sb("probsT2", [S, 2, G * S])
        attT = sb("attT", [W, S, H])
        recip = sb("recip2", [P, T8])
        att = sb("att", [P, T8, 2, D])
        uT = sb("uT", [P, X // 2, S])
        bank_ab = ps("bank2_ab", [P, 2, PSUM_BANK])
        bank_s = [ps(f"bank2_s{i}", [P, PSUM_BANK]) for i in range(2)]
        bank_t, bank_o = ps("bank2_t", [P, PSUM_BANK]), ps("bank2_o", [P, PSUM_BANK])
        bank_gh = ps("bank2_gh", [P, 2, PSUM_BANK])

        consts_done = sem("consts_done")
        stats_done, moments_done, eps_added, rstd_done, xn_done = (sem(n) for n in ("stats2_done", "moments2_done", "eps2_added", "rstd2_done", "xn2_done"))
        xt_ready, xt_copied = sem("xt2_ready"), sem("xt2_copied")
        gates_ready, gates_copied = sem("gates_ready"), sem("gates_copied")
        proj_ready, proj_copied = sem("proj_ready"), sem("proj_copied")
        mix_part_done = sem("mix_part_done")
        top_step, negexp_done, mix_done, pick_done = sem("top_step"), sem("negexp_done"), sem("mix_done"), sem("pick_done")
        proj_stored, mix_stored, pick_stored = ([sem(f"{n}{p}") for p in range(2)] for n in ("proj_stored", "mix_stored", "pick_stored"))
        te_loaded = [sem(f"te_loaded{p}") for p in range(2)]
        mix_bd_done, pick_bd_done = sem("mix_bd_done"), sem("pick_bd_done")
        q_ready, q_copied, kk_ready, kk_copied = sem("q2_ready"), sem("q2_copied"), sem("k2_ready"), sem("k2_copied")
        vt_ready, vt_copied, v_ready, v_copied = sem("vt_ready"), sem("vt_copied"), sem("v2_ready"), sem("v2_copied")
        scores_ready, max_done, shift_done = sem("scores2_ready"), sem("max2_done"), sem("shift2_done")
        turned, exp_done, pv_done, attT_copied = sem("turned2"), sem("exp2_done"), sem("pv2_done"), sem("attT_copied")
        att_ready, recip_done, att_done = sem("att_ready"), sem("recip2_done"), sem("att_done")
        u_ready, u_copied, y_ready, out_done = sem("u_ready"), sem("u_copied"), sem("y2_ready"), sem("out_done")
        stored = [sem(f"out_stored{p}") for p in range(2)]
        block = ctx.enter_context(nc.Block())

        def pipeline(eng, start, body, end):
            start()
            body((0, 0, 0), False, True, True)
            body((1, 1, 0), True, True, True)
            with eng.Fori(1, B // 2 - 1) as i:
                for p in range(2):
                    body((2 * i + p, p, i), True, True, True)
            body((B - 2, 0, B // 2 - 1), True, True, False)
            body((B - 1, 1, B // 2 - 1), True, False, False)
            end((B - 1, 1, B // 2 - 1))

        def before(e):
            b, p, i = e
            return b - 1, 1 - p, i - 1 + p

        def after(e, n=1):
            b, p, i = e
            return (b + 1, 1 - p, i + p) if n == 1 else (b + 2, p, i + 1)

        def wait(eng, sem, n):
            if not isinstance(n, int) or n > 0:
                eng.wait_ge(sem, n)

        def capped(n, last):
            return min(n, last) if isinstance(n, int) else n

        @block.sync
        def _(sp):
            def exchange(e):
                b, p, i = e
                rows = lambda t, w: t[bass.ds(b, 1)].rearrange("a s n -> (a s n)").rearrange("(g p w) -> p g w", p=P, w=w)
                start = isinstance(b, int) and b < 2
                sp.wait_ge(pick_done, b + 1)
                sp.dma_start(flat(pick_dram[bass.ds(b, 1)]), pick[:, :, :].rearrange("s h e -> s (h e)")).then_inc(pick_stored[p], 16)
                sp.wait_ge(mix_done, b + 1)
                sp.dma_start(flat(mix_dram[bass.ds(b, 1)]), mix[:, :, :].rearrange("s e h -> s (e h)")).then_inc(mix_stored[p], 16)
                sp.wait_ge(proj_copied, b + 1)
                sp.dma_start(flat(proj_dram[bass.ds(b, 1)]), proj[:, :]).then_inc(proj_stored[p], 16)
                wait_all(sp, consts_done, (mix_stored[p], 16 * i + 16), *([] if start else [(mix_bd_done, T16 * (b - 1))]))
                sp.dma_start(mix_te[:, p, :, :], rows(mix_dram, H)).then_inc(te_loaded[p], 16)
                wait_all(sp, consts_done, (proj_stored[p], 16 * i + 16), *([] if start else [(vt_ready, 4 * (b - 1))]))
                for a in range(2):
                    sp.dma_start(proj_te[:, p, :, a, :], rows(proj_dram, D)).then_inc(te_loaded[p], 16)
                wait_all(sp, consts_done, (pick_stored[p], 16 * i + 16), *([] if start else [(pick_bd_done, T8 * (b - 1))]))
                sp.dma_start(pick_th[:, p, :, :], rows(pick_dram, X)).then_inc(te_loaded[p], 16)

            def store(e):
                b, p, i = e
                sp.wait_ge(out_done, b + 1)
                sp.dma_start(flat(d.out[bass.ds(b, 1)]), c.X[:, bass.ds(b, 1), :].rearrange("s a e -> s (a e)")).then_inc(stored[p], 16)

            def start():
                exchange((0, 0, 0))
                exchange((1, 1, 0))

            def body(cur, back, front, pre):
                if back:
                    store(before(cur))
                if pre:
                    exchange(after(cur, 2))

            pipeline(sp, start, body, store)
            for p in range(2):
                sp.wait_ge(stored[p], 16 * (B // 2))

        @block.tensor
        def _(pe):
            def turn_x(e):
                b, p, i = e
                pe.wait_ge(xn_done, b + 1)
                wait(pe, kk_copied, 4 * b)
                for e in range(EC):
                    last = nc.tensor.transpose(bank_ab[:, 0, e * S:(e + 1) * S], xn[:, e * P:(e + 1) * P], c.ident[0:S, 0:S])
                last.then_inc(xt_ready, 1)

            def make_gates(e):
                b, p, i = e
                pe.wait_ge(xt_copied, b + 1)
                for e in range(EC):
                    last = nc.tensor.matmul(bank_ab[0:S, 1, 0:2 * H * X], xnT[:, p, e, :], c.wgT[:, e, :], start=(e == 0), stop=(e == EC - 1))
                last.then_inc(gates_ready, 1)

            def make_proj(e):
                b, p, i = e
                pe.wait_ge(gates_copied, b + 1)
                for e in range(EC):
                    last = nc.tensor.matmul(bank_ab[0:S, 1, 0:X * D], xnT[:, p, e, :], c.wv2T[:, e, :], start=(e == 0), stop=(e == EC - 1))
                last.then_inc(proj_ready, 1)

            def project(p, weights, half, ready):
                for m in range(M2 // 2):
                    for e in range(EC):
                        w = weights[:, e, (half * M2 // 2 + m) * P:(half * M2 // 2 + m + 1) * P]
                        last = nc.tensor.matmul(bank_ab[:, half, m * S:(m + 1) * S], w, xnT[:, p, e, :], start=(e == 0), stop=(e == EC - 1))
                last.then_inc(ready, 1)

            def queries(e):
                b, p, i = e
                wait(pe, out_done, b - 2)
                project(p, c.wq2T, 0, q_ready)
                pe.wait_ge(proj_copied, b + 1)
                project(p, c.wq2T, 1, q_ready)

            def keys(e):
                b, p, i = e
                for half in range(2):
                    pe.wait_ge(q_copied, 2 * b + half + 1)
                    project(p, c.wk2T, half, kk_ready)

            def mix_values(e, n):
                b, p, i = e
                if n == 0:
                    pe.wait_ge(te_loaded[p], 64 * i + 64)
                if n < 2:
                    wait(pe, u_copied, 4 * (b - 1))
                else:
                    pe.wait_ge(vt_copied, 8 * b + 2 * (n - 2) + 2)
                for k in (2 * n, 2 * n + 1):
                    if k < T16:
                        pe.wait_ge(mix_bd_done, T16 * b + k + 1)
                        last = nc.tensor.matmul(bank_gh[:, n % 2, (k % 2) * 256:(k % 2 + 1) * 256],
                                                proj_te[:, p, k, :, :].rearrange("p a d -> p (a d)"),
                                                mix_bd[:, k, :, :].rearrange("p t h -> p (t h)"), start=True, stop=True)
                last.then_inc(vt_ready, 1)

            def turn_values(e):
                b, p, i = e
                pe.wait_ge(vt_copied, 8 * b + 8)
                for n in range(2):
                    for m in range(H // 4):
                        last = nc.tensor.transpose(bank_gh[0:S, n, m * P:(m + 1) * P], vT[:, n * H // 4 + m, :], c.ident[:, :])
                    last.then_inc(v_ready, 1)

            def scores(e, g):
                b, p, i = e
                if g == 0:
                    pe.wait_ge(q_copied, 2 * b + 2)
                    pe.wait_ge(kk_copied, 4 * b + 4)
                wait(pe, shift_done, NG * b + g - 1)
                for m in (2 * g, 2 * g + 1):
                    last = nc.tensor.matmul(bank_s[g % 2][0:S, (m % 2) * 2 * S:(m % 2 + 1) * 2 * S], qT[:, p, m, :],
                                            kz[:, p, m, :, :].rearrange("p a s -> p (a s)"), start=True, stop=True)
                last.then_inc(scores_ready, 1)

            def turn(e, g):
                b, p, i = e
                pe.wait_ge(shift_done, NG * b + g + 1)
                wait(pe, exp_done, NG * b + g)
                for j in range(G):
                    last = nc.tensor.transpose(bank_t[0:S, j * S:(j + 1) * S], shifted[:, g % 2, j, :], c.ident[0:S, 0:S])
                last.then_inc(turned, 1)

            def weigh(e, g):
                b, p, i = e
                if g == 0:
                    pe.wait_ge(v_copied, 2 * b + 2)
                pe.wait_ge(exp_done, NG * b + g + 1)
                wait(pe, attT_copied, NG * b + g)
                for j in range(G):
                    last = nc.tensor.matmul(bank_o[0:W, j * S:(j + 1) * S], v[:, p, G * g + j, :], probsT[:, g % 2, j * S:(j + 1) * S],
                                            start=True, stop=True)
                last.then_inc(pv_done, 1)

            def attention_rows(e):
                b, p, i = e
                pe.wait_ge(attT_copied, NG * b + NG)
                pe.wait_ge(v_copied, capped(2 * b + 4, 2 * B))
                for n in range(T8):
                    last = nc.tensor.transpose(bank_gh[:, n // 7, (n % 7) * W:(n % 7 + 1) * W],
                                               attT[:, 8 * n:8 * n + 8, :].rearrange("d t h -> d (t h)"), c.ident[0:W, 0:W])
                    if n % 7 == 6:
                        last.then_inc(att_ready, 1)

            def sum_heads(e):
                b, p, i = e
                pe.wait_ge(att_done, 2 * b + 2)
                pe.wait_ge(pick_bd_done, T8 * b + T8)
                for k in range(T16):
                    for s in range(2):
                        n = 2 * k + s
                        last = nc.tensor.matmul(bank_gh[:, k // 4, (k % 4) * P:(k % 4 + 1) * P],
                                                att[:, n, :, :].rearrange("p a d -> p (a d)"),
                                                pick_bd[:, n, :, :].rearrange("p t e -> p (t e)"), start=(s == 0), stop=(s == 1))
                    if k in (3, T16 - 1):
                        last.then_inc(u_ready, 1)

            def output(e):
                b, p, i = e
                pe.wait_ge(u_copied, 4 * b + 4)
                if isinstance(b, int) and b >= B - 3:
                    pe.wait_ge(kk_copied, 4 * B)
                    pe.wait_ge(out_done, b)
                else:
                    pe.wait_ge(xt_copied, b + 4)
                for m in range(X // 2):
                    last = nc.tensor.matmul(bank_ab[0:S, 0, 0:E], uT[:, m, :], c.wo2T[:, m, :], start=(m == 0), stop=(m == X // 2 - 1))
                last.then_inc(y_ready, 1)

            def start():
                for b in range(2):
                    e = (b, b, 0)
                    turn_x(e)
                    make_gates(e)
                    make_proj(e)
                    if b == 0:
                        queries(e)
                        keys(e)
                for n in range(4):
                    mix_values((0, 0, 0), n)
                turn_values((0, 0, 0))
                scores((0, 0, 0), 0)

            def body(cur, back, front, pre):
                scores(cur, 1)
                if front:
                    queries(after(cur))
                turn(cur, 0)
                if back:
                    attention_rows(before(cur))
                weigh(cur, 0)

                scores(cur, 2)
                if front:
                    keys(after(cur))
                turn(cur, 1)
                if back:
                    sum_heads(before(cur))
                weigh(cur, 1)

                scores(cur, 3)
                if pre:
                    turn_x(after(cur, 2))
                if front:
                    mix_values(after(cur), 0)
                    mix_values(after(cur), 1)
                if pre:
                    make_gates(after(cur, 2))
                turn(cur, 2)
                if back:
                    output(before(cur))
                weigh(cur, 2)

                if front:
                    scores(after(cur), 0)
                    mix_values(after(cur), 2)
                    mix_values(after(cur), 3)
                turn(cur, 3)
                if pre:
                    make_proj(after(cur, 2))
                if front:
                    turn_values(after(cur))
                weigh(cur, 3)

            def end(e):
                attention_rows(e)
                sum_heads(e)
                output(e)

            pe.wait_ge(consts_done, 4)
            pipeline(pe, start, body, end)

        @block.scalar
        def _(act):
            def copy_x(e):
                b, p, i = e
                act.wait_ge(xt_ready, b + 1)
                wait(act, kk_ready, 2 * (b - 1))
                act.activation(xnT[:, p, :, :].rearrange("p e s -> p (e s)"), bank_ab[:, 0, 0:EC * S], ACT.Copy).then_inc(xt_copied, 1)

            def copy_gates(e):
                b, p, i = e
                act.wait_ge(gates_ready, b + 1)
                wait(act, top_step, TOP_STEPS * b)
                act.activation(gates[:, :, :].rearrange("s g e -> s (g e)"), bank_ab[0:S, 1, 0:2 * H * X], ACT.Copy).then_inc(gates_copied, 1)

            def negated_exp(e):
                b, p, i = e
                act.wait_ge(top_step, TOP_STEPS * b + TOP_BEST)
                act.activation(sig[:, :, :], best[:, :, 0:H], ACT.Exp, scale=-1.0).then_inc(negexp_done, 1)

            def copy_proj(e):
                b, p, i = e
                act.wait_ge(proj_ready, b + 1)
                wait(act, proj_stored[1 - p], 16 * (i + p))
                act.activation(proj[:, :], bank_ab[0:S, 1, 0:X * D], ACT.Copy).then_inc(proj_copied, 1)

            def copy_queries(e):
                b, p, i = e
                wait(act, scores_ready, NG * (b - 1))
                for half in range(2):
                    act.wait_ge(q_ready, 2 * b + half + 1)
                    act.activation(qT[:, p, half * M2 // 2:(half + 1) * M2 // 2, :].rearrange("p m s -> p (m s)"),
                                   bank_ab[:, half, 0:M2 // 2 * S], ACT.Copy, scale=float(D) ** -0.5).then_inc(q_copied, 1)

            def copy_keys(e):
                b, p, i = e
                for half in range(2):
                    act.wait_ge(kk_ready, 2 * b + half + 1)
                    for a in range(2):
                        act.activation(kz[64 * a:64 * a + 64, p, half * M2 // 2:(half + 1) * M2 // 2, a, :],
                                       bank_ab[64 * a:64 * a + 64, half, 0:M2 // 2 * S].rearrange("p (m s) -> p m s", s=S), ACT.Copy).then_inc(kk_copied, 1)

            def copy_mixed(e, n):
                b, p, i = e
                act.wait_ge(vt_ready, 4 * b + n + 1)
                if n == 0:
                    wait(act, v_ready, 2 * b)
                tokens = min(32, S - 32 * n)
                for a in range(2):
                    src = bank_gh[64 * a:64 * a + 64, n % 2, 0:tokens * H].rearrange("p (t m a) -> p m t a", a=2, m=H // 2)[:, :, :, a]
                    act.activation(vT[64 * a:64 * a + 64, :, 32 * n:32 * n + tokens], src, ACT.Copy).then_inc(vt_copied, 1)

            def exps(e, g):
                b, p, i = e
                act.wait_ge(turned, NG * b + g + 1)
                wait(act, pv_done, NG * b + g - 1)
                act.activation(probsT[:, g % 2, :], bank_t[0:S, 0:G * S], ACT.Exp).then_inc(exp_done, 1)

            def copy_attention(e, g):
                b, p, i = e
                act.wait_ge(pv_done, NG * b + g + 1)
                if g == 0:
                    wait(act, att_ready, 2 * b)
                act.activation(attT[:, :, G * g:G * g + G], bank_o[0:W, 0:G * S].rearrange("w (j s) -> w s j", j=G), ACT.Copy).then_inc(attT_copied, 1)

            def start():
                for b in range(2):
                    e = (b, b, 0)
                    copy_x(e)
                    copy_gates(e)
                    negated_exp(e)
                    copy_proj(e)
                    if b == 0:
                        copy_queries(e)
                        copy_keys(e)
                for n in range(4):
                    copy_mixed((0, 0, 0), n)

            def body(cur, back, front, pre):
                if front:
                    copy_queries(after(cur))
                exps(cur, 0)
                copy_attention(cur, 0)
                if front:
                    copy_keys(after(cur))
                exps(cur, 1)
                copy_attention(cur, 1)
                if pre:
                    copy_x(after(cur, 2))
                if front:
                    copy_mixed(after(cur), 0)
                    copy_mixed(after(cur), 1)
                if pre:
                    copy_gates(after(cur, 2))
                exps(cur, 2)
                copy_attention(cur, 2)
                if front:
                    copy_mixed(after(cur), 2)
                    copy_mixed(after(cur), 3)
                exps(cur, 3)
                if pre:
                    negated_exp(after(cur, 2))
                    copy_proj(after(cur, 2))
                copy_attention(cur, 3)

            pipeline(act, start, body, lambda e: None)

        @block.vector
        def _(dve):
            gsz = [S, 2 * H, X]

            def moments_of(e):
                b, p, i = e
                xb = c.X[:, bass.ds(b, 1), :].rearrange("s a e -> s (a e)")
                dve.bn_stats(stats[:, :], xb).then_inc(stats_done, 1)
                wait_all(dve, consts_done, (stats_done, b + 1))
                dve.bn_aggr(moments[:, :], stats[:, :]).then_inc(moments_done, 1)

            def normalise_x(e):
                b, p, i = e
                xb = c.X[:, bass.ds(b, 1), :].rearrange("s a e -> s (a e)")
                dve.wait_ge(rstd_done, b + 1)
                wait(dve, xt_ready, b)
                dve.tensor_scalar(xn[:, :], xb, moments[:, 0:1], rstd[:, 0:1], ALU.subtract, ALU.mult).then_inc(xn_done, 1)

            def select(e):
                b, p, i = e
                dve.wait_ge(gates_copied, b + 1)
                steps = 0

                def step(ins):
                    nonlocal steps
                    steps += 1
                    ins.then_inc(top_step, 1)
                    dve.wait_ge(top_step, TOP_STEPS * b + steps)

                wait(dve, negexp_done, b)
                src = gates
                for r in range(2):
                    step(dve.tensor_reduce(best[:, r, :], src[:, :, :], AXX, ALU.max))
                    step(dve.tensor_tensor(tie[:, :, :], src[:, :, :], best[:, r, :].unsqueeze(2).to_broadcast(gsz), ALU.is_ge))
                    step(dve.tensor_tensor(tie[:, :, :], tie[:, :, :], rank_w[:, :].unsqueeze(1).to_broadcast(gsz), ALU.mult))
                    step(dve.tensor_reduce(first_tie[:, :], tie[:, :, :], AXX, ALU.max))
                    step(dve.tensor_tensor(one_hot[:, r, :, :], tie[:, :, :], first_tie[:, :].unsqueeze(2).to_broadcast(gsz), ALU.is_ge))
                    if r == 0:
                        step(dve.scalar_tensor_tensor(rest[:, :, :], one_hot[:, 0, :, :], LEAST, gates[:, :, :], ALU.mult, ALU.add))
                    src = rest
                wait(dve, pick_stored[1 - p], 16 * (i + p))
                dve.tensor_tensor(pick[:, :, :], one_hot[:, 0, H:2 * H, :], one_hot[:, 1, H:2 * H, :], ALU.add).then_inc(pick_done, 1)
                dve.wait_ge(negexp_done, b + 1)
                step(dve.tensor_scalar(sig[:, :, :], sig[:, :, :], 1.0, None, ALU.add))
                step(dve.reciprocal(sig[:, :, :], sig[:, :, :]))
                for r in range(2):
                    last = dve.tensor_tensor(mix_part[:, r, :, :], one_hot[:, r, 0:H, :], sig[:, r, :].unsqueeze(2).to_broadcast([S, H, X]), ALU.mult)
                    last.then_inc(mix_part_done, 1)
                dve.wait_ge(mix_part_done, 2 * b + 2)
                wait(dve, mix_stored[1 - p], 16 * (i + p))
                dve.tensor_tensor(mix[:, :, :].rearrange("s e h -> s h e"), mix_part[:, 0, :, :], mix_part[:, 1, :, :], ALU.add).then_inc(mix_done, 1)

            def shift(e, g):
                b, p, i = e
                dve.wait_ge(scores_ready, NG * b + g + 1)
                sc = bank_s[g % 2][0:S, 0:G * S].rearrange("s (j t) -> s j t", j=G)
                dve.tensor_reduce(neg_max[:, g % 2, :], sc, AXX, ALU.max).then_inc(max_done, 1)
                dve.wait_ge(max_done, NG * b + g + 1)
                wait(dve, turned, NG * b + g - 1)
                dve.tensor_tensor(shifted[:, g % 2, :, :], sc, neg_max[:, g % 2, :].unsqueeze(2).to_broadcast([S, G, S]), ALU.subtract).then_inc(shift_done, 1)

            def copy_values(e):
                b, p, i = e
                wait(dve, pv_done, NG * (b - 1))
                for n in range(2):
                    dve.wait_ge(v_ready, 2 * b + n + 1)
                    dve.tensor_copy(v[:, p, n * H // 2:(n + 1) * H // 2, 0:D], bank_gh[0:S, n, :].rearrange("s (h d) -> s h d", d=D)).then_inc(v_copied, 1)

            def normalise(e):
                b, p, i = e
                wait(dve, u_ready, 2 * b)
                for n in range(2):
                    a = bank_gh[:, n, 0:7 * W].rearrange("p (t w) -> p t w", w=W)
                    dve.wait_ge(att_ready, 2 * b + n + 1)
                    dve.reciprocal(recip[:, 7 * n:7 * n + 7].unsqueeze(2), a[:, :, D:W]).then_inc(recip_done, 1)
                    dve.wait_ge(recip_done, 2 * b + n + 1)
                    dve.tensor_tensor(att[:, 7 * n:7 * n + 7, :, :], a[:, :, 0:D].unsqueeze(2).to_broadcast([P, 7, 2, D]),
                                      recip[:, 7 * n:7 * n + 7].unsqueeze(2).unsqueeze(3).to_broadcast([P, 7, 2, D]), ALU.mult).then_inc(att_done, 1)

            def copy_sums(e):
                b, p, i = e
                wait(dve, y_ready, b)
                for n in range(2):
                    dve.wait_ge(u_ready, 2 * b + n + 1)
                    tokens = min(64, S - 64 * n)
                    for a in range(2):
                        src = bank_gh[64 * a:64 * a + 64, n, 0:tokens * X].rearrange("p (t m a) -> p m t a", a=2, m=X // 2)[:, :, :, a]
                        dve.tensor_copy(uT[64 * a:64 * a + 64, :, 64 * n:64 * n + tokens], src).then_inc(u_copied, 1)

            def residual(e):
                b, p, i = e
                dve.wait_ge(y_ready, b + 1)
                xb = c.X[:, bass.ds(b, 1), :].rearrange("s a e -> s (a e)")
                dve.scalar_tensor_tensor(xb, bank_ab[0:S, 0, 0:E], c.tanh_g[:, 1:2], xb, ALU.mult, ALU.add).then_inc(out_done, 1)

            def start():
                for b in range(2):
                    e = (b, b, 0)
                    moments_of(e)
                    normalise_x(e)
                    select(e)
                copy_values((0, 0, 0))
                shift((0, 0, 0), 0)

            def body(cur, back, front, pre):
                shift(cur, 1)
                if pre:
                    moments_of(after(cur, 2))
                if back:
                    normalise(before(cur))
                if pre:
                    normalise_x(after(cur, 2))
                shift(cur, 2)
                if back:
                    copy_sums(before(cur))
                shift(cur, 3)
                if back:
                    residual(before(cur))
                if front:
                    shift(after(cur), 0)
                if pre:
                    select(after(cur, 2))
                if front:
                    copy_values(after(cur))

            def end(e):
                normalise(e)
                copy_sums(e)
                residual(e)

            dve.memset(kz[:, :, :, :, :], 0.0).then_inc(consts_done, 1)
            dve.memset(v[:, :, :, D:W], 1.0).then_inc(consts_done, 1)
            for e in range(X):
                last = dve.memset(rank_w[:, e:e + 1], float(X - e))
            last.then_inc(consts_done, 1)
            dve.wait_ge(consts_done, 4)
            pipeline(dve, start, body, end)

        @block.gpsimd
        def _(pool):
            def inverse_deviation(e):
                b, p, i = e
                wait_all(pool, consts_done, (moments_done, b + 1))
                pool.tensor_scalar(var_eps[:, :], moments[:, 1:2], LN_EPS, None, ALU.add).then_inc(eps_added, 1)
                pool.wait_ge(eps_added, b + 1)
                pool.tensor_tensor(rstd[:, :], var_eps[:, :], minus_half[:, :], ALU.pow).then_inc(rstd_done, 1)

            def spread_mix(e):
                b, p, i = e
                pool.wait_ge(te_loaded[p], 64 * i + 64)
                wait(pool, vt_ready, 4 * b)
                for k in range(T16):
                    pool.tensor_tensor(mix_bd[:, k, :, :], mix_te[:, p, k, :].unsqueeze(1).to_broadcast([P, 16, H]),
                                       c.tok16[:, :].unsqueeze(2).to_broadcast([P, 16, H]), ALU.mult).then_inc(mix_bd_done, 1)

            def spread_pick(e):
                b, p, i = e
                wait(pool, u_ready, 2 * b)
                for n in range(T8):
                    pool.tensor_tensor(pick_bd[:, n, :, :], pick_th[:, p, n, :].unsqueeze(1).to_broadcast([P, 16, X]),
                                       c.tok8[:, n % 2, :].unsqueeze(2).to_broadcast([P, 16, X]), ALU.mult).then_inc(pick_bd_done, 1)

            def start():
                inverse_deviation((0, 0, 0))
                inverse_deviation((1, 1, 0))
                spread_mix((0, 0, 0))

            def body(cur, back, front, pre):
                if pre:
                    inverse_deviation(after(cur, 2))
                if front:
                    spread_mix(after(cur))
                spread_pick(cur)

            pool.memset(minus_half[:, :], -0.5).then_inc(consts_done, 1)
            pool.wait_ge(consts_done, 4)
            pipeline(pool, start, body, lambda e: None)


class Names:
    pass


def flamingo_kernel(nc, ins, out):
    d = Names()
    (d.x, d.ctx, d.mask, d.g_xattn, d.g_ffn, d.wq, d.bq, d.wk, d.bk, d.wv, d.bv, d.wo, d.bo,
     d.wq2, d.wk2, d.wv2, d.ws, d.wd, d.wo2) = ins
    d.out = out
    z = Shapes(d.x, d.ctx, d.wq2, d.wv2)
    with ExitStack() as ctx:
        sb = lambda name, shape: ctx.enter_context(nc.sbuf_tensor(name, shape, F32))
        c = Names()
        c.X = sb("X", [z.S, z.B, z.E])
        c.ident = sb("ident", [P, P])
        c.headmask = sb("headmask", [P, z.HT])
        c.tok16, c.tok8 = sb("tok16", [P, 16]), sb("tok8", [P, 2, 16])
        c.tanh_g = sb("tanh_g", [z.S, 2])
        c.wq2T, c.wk2T = sb("wq2T", [P, z.EC, z.M2 * P]), sb("wk2T", [P, z.EC, z.M2 * P])
        c.wv2T = sb("wv2T", [P, z.EC, z.X * z.D2])
        c.wgT = sb("wgT", [P, z.EC, 2 * z.H2 * z.X])
        c.wo2T = sb("wo2T", [P, z.X // 2, z.E])
        with ExitStack() as inner:
            sb1 = lambda name, shape: inner.enter_context(nc.sbuf_tensor(name, shape, F32))
            c.QT = sb1("QT", [P, z.EC, z.B * z.S])
            c.wq, c.wk, c.wv, c.wo = (sb1(n, [P, z.EC, z.E]) for n in ("wq_sb", "wk_sb", "wv_sb", "wo_sb"))
            c.bk, c.bv = sb1("bk_sb", [P, z.EC]), sb1("bv_sb", [z.KP, z.E])
            c.maskb = sb1("maskb", [z.S, z.S2])
            prepare(nc, z, d, c)
            cross(nc, z, d, c)
        switch(nc, z, d, c)


_INS = ['x', 'ctx_1024', 'mask_1x1xSxS2_fk1', 'g_xattn', 'g_ffn', 'L0_xattn_wq', 'L0_xattn_bq', 'L0_xattn_wk',
        'L0_xattn_bk', 'L0_xattn_wv', 'L0_xattn_bv', 'L0_xattn_wo', 'L0_xattn_bo', 'L0_ffn_Wq', 'L0_ffn_Wk',
        'L0_ffn_Wv', 'L0_ffn_Ws', 'L0_ffn_Wd', 'L0_ffn_Wo']


def kernel(**inputs):
    import numpy as _np
    import concourse.bacc as _bacc
    from concourse import mybir as _mybir
    from concourse.bass_utils import run_bass_kernel_spmd as _run

    nc = _bacc.Bacc("TRN2", target_bir_lowering=False, num_devices=1)
    arrays, args = {}, []
    for name in _INS:
        a = _np.ascontiguousarray(inputs[name])
        arrays[f"in_{name}_dram"] = a
        args.append(nc.dram_tensor(f"in_{name}_dram", a.shape, _mybir.dt.from_np(a.dtype), kind="ExternalInput").ap())
    out = nc.dram_tensor("out_0_dram", inputs["x"].shape, _mybir.dt.float32, kind="ExternalOutput").ap()
    flamingo_kernel(nc, args, out)
    r = _run(nc, [arrays], core_ids=[0])
    return r.results[0]["out_0_dram"]
```

```python
from contextlib import ExitStack

import concourse.bass as bass
from concourse import mybir

F32 = mybir.dt.float32
BF16 = mybir.dt.bfloat16
ALU = mybir.AluOpType
ACT = mybir.ActivationFunctionType
AXX = mybir.AxisListType.X

P = 128
PSUM_BANK = 512
LN_EPS = 1e-5
MASK_SCALE = -1e9
LEAST = -3.0e38

PARTS = 3
K_PARTS = (0, 1, 2, 0, 1, 2, 0, 1)
Q_PARTS = (0, 0, 0, 1, 1, 1, 2, 2)


def wait_all(eng, met, *waits):
    waits = [(sem, n if isinstance(n, int) else eng.to_reg(n)) for sem, n in waits]
    eng.wait_ge(met, 1)
    for sem, n in waits:
        eng.wait_ge(sem, n)


def flat(ap):
    return ap.rearrange("a s e -> (a s) e")


class Shapes:

    def __init__(self, x, ctx, wq2, wv2):
        self.B, self.S, self.E = x.shape
        self.S2 = ctx.shape[1]
        self.H, self.D = 16, self.E // 16
        self.KC, self.KP = 3, self.S2 // 3
        self.G = 4
        self.H2, self.D2, _ = wq2.shape
        self.X = wv2.shape[0]
        self.GX = 4
        self.EC = self.E // P
        self.M2 = self.H2 * self.D2 // P
        assert self.KC * self.KP == self.S2 and self.KP <= P and self.B % 4 == 0


def prepare(nc, z, d, c):
    B, S, E, EC = z.B, z.S, z.E, z.EC
    SMALL = 7
    with ExitStack() as ctx:
        sb = lambda name, shape: ctx.enter_context(nc.sbuf_tensor(name, shape, F32))
        sem = lambda name: ctx.enter_context(nc.semaphore(name))
        wq_nat, wk_nat = sb("wq_nat", [P, EC, E]), sb("wk_nat", [P, EC, E])
        gates_in = sb("gates_in", [S, 2])
        bias_in, bias_row = sb("bias_in", [1, 2, E]), sb("bias_row", [1, 2, E])
        psum_bias = ctx.enter_context(nc.psum_tensor("p_bias", [P, 2, EC], F32))
        small_loaded, qk_loaded, vo_loaded = sem("small_loaded"), sem("qk_loaded"), sem("vo_loaded")
        zeroed, consts_ready = sem("zeroed"), sem("consts_ready")
        permuted, bias_turned = sem("permuted"), sem("bias_turned")
        tanh_done, bias_done = sem("tanh_done"), sem("bias_done")
        block = ctx.enter_context(nc.Block())

        @block.sync
        def _(sp):
            row = lambda v: v.rearrange("(a n) -> a n", a=1)
            for n, src in enumerate((d.bq, d.bk)):
                sp.dma_start(bias_in[:, n, :], row(src)).then_inc(small_loaded, 16)
            for dst, src, loaded in ((wk_nat, d.wk, qk_loaded), (wq_nat, d.wq, qk_loaded), (c.wv, d.wv, vo_loaded), (c.wo, d.wo, vo_loaded)):
                sp.dma_start(dst[:, :, :], src.rearrange("(e p) n -> p e n", p=P)).then_inc(loaded, 16)
            sp.dma_start(gates_in[:, 0:1], row(d.g_xattn).to_broadcast([S, 1])).then_inc(small_loaded, 16)
            sp.dma_start(gates_in[:, 1:2], row(d.g_ffn).to_broadcast([S, 1])).then_inc(small_loaded, 16)
            sp.dma_start(c.bo[:, :], row(d.bo).to_broadcast([S, E])).then_inc(small_loaded, 16)
            sp.dma_start(c.bv[:, :], row(d.bv).to_broadcast([z.KP, E])).then_inc(small_loaded, 16)
            sp.dma_start(c.maskb[:, :], d.mask.rearrange("a b s k -> (a b s) k")).then_inc(small_loaded, 16)
            for b in range(2):
                sp.dma_start(c.ctx_in[:, b, :, :], d.ctx[b].rearrange("(k p) e -> p k e", p=z.KP)).then_inc(c.ctx_loaded[b], 16)
                if b == 0:
                    sp.dma_start(c.X[0:S, 0:z.GX, :], d.x[0:z.GX].rearrange("b s e -> s b e")).then_inc(c.x_loaded[0], 16)
            rows = lambda w: w.rearrange("h d c -> (h d) c").rearrange("(m p) c -> p m c", p=P)
            for load, (dst, src) in enumerate(((c.wq_in, d.wq2), (c.wk_in, d.wk2), (c.wv_in, d.wv2))):
                sp.dma_start(dst[:, :, :], rows(src)).then_inc(c.weights_loaded[load], 16)
            sp.dma_start(c.wg_in[:, 0, :], d.ws.rearrange("h e c -> (h e) c")).then_inc(c.weights_loaded[3], 16)
            sp.dma_start(c.wg_in[:, 1, :], d.wd.rearrange("h e c -> (h e) c")).then_inc(c.weights_loaded[3], 16)
            for f in range(EC):
                sp.dma_start(c.wo_in[:, f, :, :], d.wo2[:, f * P:(f + 1) * P, :].rearrange("e f d -> f e d")).then_inc(c.weights_loaded[3], 16)

        @block.scalar
        def _(act):
            act.wait_ge(small_loaded, 16 * SMALL)
            act.activation(c.tanh_g[:, :], gates_in[:, :], ACT.Tanh).then_inc(tanh_done, 1)

        @block.gpsimd
        def _(pool):
            pool.memset(c.ident[:, :], 0.0).then_inc(zeroed, 1)
            pool.memset(c.tok16[:, :], 1.0).then_inc(zeroed, 1)
            pool.memset(c.tok8[:, :], 1.0).then_inc(zeroed, 1)
            pool.wait_ge(zeroed, 3)
            steps = 0

            def keep(t, compare, fill, base, pattern, mult):
                nonlocal steps
                nc.gpsimd.affine_select(out=t, in_=t, compare_op=compare, fill=fill, base=base,
                                        pattern=pattern, channel_multiplier=mult).then_inc(consts_ready, 1)
                steps += 1
                pool.wait_ge(consts_ready, steps)

            keep(c.ident[:, :], ALU.not_equal, 1.0, 0, [[-1, P]], 1)
            for t, base, pattern, width in (
                (c.tok16[:, :], 0, [[-z.X, 16]], z.X),
                (c.tok8[:, :], 0, [[-z.H2, 8]], z.H2),
            ):
                keep(t, ALU.is_ge, 0.0, base, pattern, 1)
                keep(t, ALU.is_ge, 0.0, width - 1 - base, [[-a, n] for a, n in pattern], -1)

        @block.vector
        def _(dve):
            dve.wait_ge(qk_loaded, 16 * 2)
            for dst, src in ((c.wk, wk_nat), (c.wq, wq_nat)):
                dve.tensor_copy(dst[:, :, :].rearrange("p e (d h) -> p e d h", h=z.H),
                                src[:, :, :].rearrange("p e (h d) -> p e d h", h=z.H)).then_inc(permuted, 1)
            dve.wait_ge(small_loaded, 16 * SMALL)
            dve.tensor_copy(bias_row[:, :, :].rearrange("a n (d h) -> a n d h", h=z.H),
                            bias_in[:, :, :].rearrange("a n (h d) -> a n d h", h=z.H)).then_inc(permuted, 1)
            dve.tensor_scalar(c.maskb[:, :], c.maskb[:, :], MASK_SCALE, None, ALU.mult).then_inc(bias_done, 1)
            dve.wait_ge(tanh_done, 1)
            dve.tensor_scalar(c.bo[:, :], c.bo[:, :], c.tanh_g[:, 0:1], None, ALU.mult).then_inc(bias_done, 1)
            dve.wait_ge(bias_turned, 1)
            dve.tensor_scalar(c.bq[:, :], psum_bias[:, 0, :], float(z.D) ** -0.5, None, ALU.mult).then_inc(bias_done, 1)
            dve.tensor_copy(c.bk[:, :], psum_bias[:, 1, :]).then_inc(bias_done, 1)
            dve.wait_ge(vo_loaded, 16 * 2)

        @block.tensor
        def _(pe):
            pe.wait_ge(consts_ready, 5)
            pe.wait_ge(permuted, 3)
            for n in range(2):
                for t in range(EC):
                    last = nc.tensor.transpose(psum_bias[:, n, t:t + 1], bias_row[:, n, t * P:(t + 1) * P], c.ident[0:1, 0:1])
            last.then_inc(bias_turned, 1)


def weight_turns(z, c):
    turns = []
    for load, (src, dst, tiles) in enumerate(((c.wq_in, c.wq2T, z.M2), (c.wk_in, c.wk2T, z.M2), (c.wv_in, c.wv2T, z.X * z.D2 // P))):
        for e in range(z.EC):
            for m in range(0, tiles, 4):
                turns.append((load, [src[:, m + k, e * P:(e + 1) * P] for k in range(4)],
                              dst[:, e, m * P:(m + 4) * P]))
    turns.append((3, [c.wg_in[:, k, e * P:(e + 1) * P] for e in range(z.EC) for k in range(2)],
                  c.wgT[:, :, :].rearrange("p e n -> p (e n)")))
    for m in range(0, z.X // 2, 2):
        turns.append((3, [c.wo_in[:, f, 2 * (m + k):2 * (m + k) + 2, :].rearrange("p e d -> p (e d)")
                          for k in range(2) for f in range(z.EC)],
                      c.wo2T[:, m:m + 2, :].rearrange("p e f -> p (e f)")))
    return turns


def cross(nc, z, d, c):
    B, S, E, EC, H, G, KC, KP, S2, D = z.B, z.S, z.E, z.EC, z.H, z.G, z.KC, z.KP, z.S2, z.D
    NG = H // G
    X_LOADS = B // z.GX - 1
    STACK_LOADS = 16 * (len(Q_PARTS) + -(-len(K_PARTS) // PARTS))
    VW = 32
    with ExitStack() as ctx:
        sb = lambda name, shape, dt=F32: ctx.enter_context(nc.sbuf_tensor(name, shape, dt))
        ps = lambda name, shape: ctx.enter_context(nc.psum_tensor(name, shape, F32))
        sem = lambda name: ctx.enter_context(nc.semaphore(name))
        ctx_in, ctx_loaded = c.ctx_in, c.ctx_loaded
        ctxT = sb("ctxT", [P, 2, EC, S2])
        k32, k_rest = sb("k32", [P, EC, S2]), sb("k_rest", [P, EC, S2])
        k_parts = sb("k_parts", [P, PARTS, EC, S2], BF16)
        K_stack = sb("K_stack", [P, 2, H, S2], BF16)
        Q_stack = sb("Q_stack", [P, 2, H, S], BF16)
        V = sb("V", [KP, 2, KC, H, VW])
        raw = sb("raw", [S, 2, G, S2])
        neg_max = sb("neg_max", [S, 2, G])
        shifted = sb("shifted", [S, 2, G, S2])
        probsT = sb("probsT", [KP, 2, KC, G * S])
        headsT = sb("headsT", [P, NG * S])
        recip = sb("recip", [S, H])
        heads = sb("heads", [S, H, D])
        outT = sb("outT", [P, EC, S])
        minus_half = sb("minus_half", [S, 1])
        stats, moments = sb("stats", [S, 6]), sb("moments", [S, 2])
        var_eps, rstd = sb("var_eps", [S, 1]), sb("rstd", [S, 1])
        xn, xnT = sb("xn", [S, E]), sb("xnT", [P, EC, S])
        q32, q_rest = sb("q32", [P, EC, S]), sb("q_rest", [P, EC, S])
        q_parts = sb("q_parts", [P, PARTS, EC, S], BF16)
        bank_s = [ps(f"bank_s{i}", [P, PSUM_BANK]) for i in range(2)]
        bank_t = ps("bank_t", [P, KC, PSUM_BANK])
        bank_o = ps("bank_o", [P, PSUM_BANK])
        bank_ab = ps("bank_ab", [P, 2, PSUM_BANK])
        v_cleared, v_set = sem("v_cleared"), sem("v_set")
        ctxT_ready, ctxT_copied = sem("ctxT_ready"), sem("ctxT_copied")
        k_ready, k_copied = sem("k_ready"), sem("k_copied")
        va_ready, vb_ready, v_copied = sem("va_ready"), sem("vb_ready"), sem("v_copied")
        k_rest_done, k_second, k_split = sem("k_rest_done"), sem("k_second"), sem("k_split")
        k_stored = [sem(f"k_stored{i}") for i in range(2)]
        stack_loaded = [sem(f"stack_loaded{i}") for i in range(2)]
        half_set = sem("half_set")
        stats_done, moments_done, eps_added, rstd_done, xn_done, xbias_done = (
            sem(n) for n in ("stats_done", "moments_done", "eps_added", "rstd_done", "xn_done", "xbias_done"))
        xt_ready, xt_copied, q_ready, q_copied = sem("xt_ready"), sem("xt_copied"), sem("q_ready"), sem("q_copied")
        q_rest_done, q_second, q_split = sem("q_rest_done"), sem("q_second"), sem("q_split")
        q_stored = [sem(f"q_stored{i}") for i in range(2)]
        wt_ready, wt_copied = sem("wt_ready"), [sem(f"wt_copied{i}") for i in range(2)]
        turns, turn_banks = weight_turns(z, c), [bank_s[0], bank_s[1], bank_o]
        q_dram = nc.dram_tensor("q_dram", (B, PARTS, E, S), BF16).ap()
        k_dram = nc.dram_tensor("k_dram", (B, PARTS, E, S2), BF16).ap()
        scores_ready, scores_read, shift_done = sem("scores_ready"), sem("scores_read"), sem("shift_done")
        turned, exp_done, pv_done = sem("turned"), sem("exp_done"), sem("pv_done")
        headsT_copied, heads_ready, recip_done, heads_done = sem("headsT_copied"), sem("heads_ready"), sem("recip_done"), sem("heads_done")
        outT_ready, outT_copied, y_ready, x_done = sem("outT_ready"), sem("outT_copied"), sem("y_ready"), sem("x_done")
        block = ctx.enter_context(nc.Block())

        def batches(eng, body):
            body(0, 0, 0, True, True, False)
            body(1, 1, 0, False, True, False)
            with eng.Fori(1, B // 2 - 1) as i:
                body(2 * i, 0, i, False, True, False)
                body(2 * i + 1, 1, i, False, True, False)
            body(B - 2, 0, B // 2 - 1, False, False, False)
            body(B - 1, 1, B // 2 - 1, False, False, True)

        @block.sync
        def _(sp):
            def load(b, p):
                sp.dma_start(ctx_in[:, p, :, :], flat(d.ctx[bass.ds(b, 1)]).rearrange("(k p) e -> p k e", p=KP)).then_inc(ctx_loaded[p], 16)

            def exchange(b, p, i):
                start = isinstance(b, int) and b < 2

                def store_queries():
                    sp.wait_ge(q_split, b + 1)
                    sp.dma_start(q_dram[bass.ds(b, 1)].rearrange("a q (t p) s -> p (a q) t s", p=P), q_parts[:, :, :, :]).then_inc(q_stored[p], 16)

                sp.wait_ge(k_split, b + 1)
                sp.dma_start(k_dram[bass.ds(b, 1)].rearrange("a q (t p) k -> p (a q) t k", p=P), k_parts[:, :, :, :]).then_inc(k_stored[p], 16)
                if start:
                    store_queries()
                else:
                    sp.wait_ge(scores_ready, H * (b - 1))
                sp.wait_ge(k_stored[p], 16 * i + 16)
                for j in range(0, len(K_PARTS), PARTS):
                    n = min(PARTS, len(K_PARTS) - j)
                    sp.dma_start(K_stack[j * D:(j + n) * D, p, :, :].rearrange("d h k -> d (h k)"),
                                 k_dram[bass.ds(b, 1), 0:n].rearrange("a q (d h) k -> (a q d) (h k)", h=H)).then_inc(stack_loaded[p], 16)
                if not start:
                    store_queries()
                sp.wait_ge(q_stored[p], 16 * i + 16)
                for j, part in enumerate(Q_PARTS):
                    sp.dma_start(Q_stack[j * D:(j + 1) * D, p, :, :].rearrange("d h s -> d (h s)"),
                                 q_dram[bass.ds(b, 1), part].rearrange("a (d h) s -> (a d) (h s)", h=H)).then_inc(stack_loaded[p], 16)

            for b in range(2):
                sp.wait_ge(ctxT_ready, b + 1)
                load(b + 2, b)
            for b in range(2):
                exchange(b, b, 0)
            sp.wait_ge(wt_ready, len(turns))
            for g in range(z.GX, B, z.GX):
                sp.dma_start(c.X[0:S, g:g + z.GX, :], d.x[g:g + z.GX].rearrange("b s e -> s b e")).then_inc(c.x_loaded[1], 16)

            def body(b, p, i, load_next=True):
                if load_next:
                    sp.wait_ge(ctxT_ready, b + 3)
                    load(b + 4, p)
                exchange(b + 2, p, i + 1)

            for p in range(2):
                body(p, p, 0)
            with sp.Fori(1, B // 2 - 2) as i:
                for p in range(2):
                    body(2 * i + p, p, i)
            for p in range(2):
                body(B - 4 + p, p, B // 2 - 2, False)

        @block.tensor
        def _(pe):
            def transposes(b, i, p):
                pe.wait_ge(ctx_loaded[p], 16 * i + 16)
                start = isinstance(b, int) and b < 2
                if not start:
                    pe.wait_ge(v_copied, 2 * (b - 1))
                if not (start and b == 0):
                    pe.wait_ge(q_copied, (EC + 1) * b)
                for e in range(EC):
                    for k in range(KC):
                        last = nc.tensor.transpose(bank_ab[:, e, k * KP:(k + 1) * KP],
                                                   ctx_in[:, p, k, e * P:(e + 1) * P], c.ident[0:KP, 0:KP])
                last.then_inc(ctxT_ready, 1)

            def keys(b, p, t):
                if t == 0:
                    pe.wait_ge(ctxT_copied, b + 1)
                for e in range(EC):
                    last = nc.tensor.matmul(bank_ab[:, t, 0:S2], c.wk[:, e, t * P:(t + 1) * P], ctxT[:, p, e, :],
                                            start=(e == 0), stop=(e == EC - 1))
                last.then_inc(k_ready, 1)

            def turn_x(b):
                pe.wait_ge(xn_done, b + 1)
                for e in range(EC):
                    last = nc.tensor.transpose(bank_ab[:, 0, e * S:(e + 1) * S], xn[:, e * P:(e + 1) * P], c.ident[0:S, 0:S])
                last.then_inc(xt_ready, 1)

            def queries(b):
                pe.wait_ge(xt_copied, b + 1)
                for t in range(EC):
                    for e in range(EC):
                        last = nc.tensor.matmul(bank_ab[:, 0, t * S:(t + 1) * S], c.wq[:, e, t * P:(t + 1) * P], xnT[:, e, :],
                                                start=(e == 0), stop=(e == EC - 1))
                last.then_inc(q_ready, 1)

            def values(p, k, start=False):
                dst = bank_t[0:KP, k, 0:E] if start else bank_ab[0:KP, k // 2, (k % 2) * E:(k % 2 + 1) * E]
                for e in range(EC):
                    last = nc.tensor.matmul(dst, ctxT[:, p, e, k * KP:(k + 1) * KP],
                                            c.wv[:, e, :], start=(e == 0), stop=(e == EC - 1))
                return last

            def scores(b, p, i, h, first):
                if h == 0:
                    pe.wait_ge(stack_loaded[p], STACK_LOADS * i + STACK_LOADS)
                if not (first and h < 2):
                    pe.wait_ge(scores_read, H * b + h - 1)
                nc.tensor.matmul(bank_s[h % 2][0:S, 0:S2], Q_stack[:, p, h, :], K_stack[:, p, h, :],
                                 start=True, stop=True).then_inc(scores_ready, 1)

            def turn(b, g, first):
                pe.wait_ge(shift_done, H * b + G * g + G)
                for k in range(KC):
                    if not (first and g == 0):
                        pe.wait_ge(exp_done, KC * (NG * b + g - 1) + k + 1)
                    for j in range(G):
                        last = nc.tensor.transpose(bank_t[0:KP, k, j * S:(j + 1) * S],
                                                   shifted[:, g % 2, j, k * KP:(k + 1) * KP], c.ident[0:S, 0:S])
                    last.then_inc(turned, 1)

            def weigh(b, p, g, first):
                if g == 0:
                    pe.wait_ge(v_copied, 2 * b + 2)
                    if first:
                        pe.wait_ge(v_set, 1)
                    else:
                        pe.wait_ge(headsT_copied, b)
                for k in range(KC):
                    pe.wait_ge(exp_done, KC * (NG * b + g) + k + 1)
                    for j in range(G):
                        last = nc.tensor.matmul(bank_o[j * VW:(j + 1) * VW, g * S:(g + 1) * S], V[:, p, k, G * g + j, :],
                                                probsT[:, g % 2, k, j * S:(j + 1) * S], start=(k == 0), stop=(k == KC - 1))
                last.then_inc(pv_done, 1)

            def heads_back(b):
                pe.wait_ge(headsT_copied, b + 1)
                for g in range(NG):
                    last = nc.tensor.transpose(bank_ab[0:S, 0, g * P:(g + 1) * P], headsT[:, g * S:(g + 1) * S], c.ident[:, :])
                last.then_inc(heads_ready, 1)

            def heads_turn(b):
                pe.wait_ge(heads_done, b + 1)
                flat_heads = heads[:, :, :].rearrange("s h d -> s (h d)")
                for e in range(EC):
                    last = nc.tensor.transpose(bank_ab[:, 1, e * S:(e + 1) * S], flat_heads[:, e * P:(e + 1) * P], c.ident[0:S, 0:S])
                last.then_inc(outT_ready, 1)

            def project(b):
                pe.wait_ge(outT_copied, b + 1)
                for e in range(EC):
                    last = nc.tensor.matmul(bank_ab[0:S, 1, 0:E], outT[:, e, :], c.wo[:, e, :], start=(e == 0), stop=(e == EC - 1))
                last.then_inc(y_ready, 1)

            def body(b, p, i, first, ahead, last):
                back, front = not first, not last
                S_ = lambda *hs: [scores(b, p, i, h, first) for h in hs]
                S_(0, 1)
                if back:
                    turn(b - 1, NG - 1, False)
                S_(2)
                if ahead:
                    transposes(b + 2, i + 1, p)
                S_(3)
                if back:
                    weigh(b - 1, 1 - p, NG - 1, False)
                S_(4)
                if ahead:
                    keys(b + 2, p, 0)
                S_(5)
                turn(b, 0, first)
                S_(6, 7)
                if ahead:
                    keys(b + 2, p, 1)
                weigh(b, p, 0, first)
                if back:
                    if ahead:
                        pe.wait_ge(k_copied, 2 * (EC * (b + 2) + 1))
                    heads_back(b - 1)
                S_(8)
                turn(b, 1, False)
                S_(9)
                if ahead:
                    pe.wait_ge(k_copied, 2 * EC * (b + 3))
                if back:
                    heads_turn(b - 1)
                S_(10)
                if front:
                    values(1 - p, 0)
                    values(1 - p, 1).then_inc(va_ready, 1)
                S_(11)
                weigh(b, p, 1, False)
                S_(12)
                if back:
                    project(b - 1)
                S_(13)
                turn(b, 2, False)
                if ahead:
                    pe.wait_ge(v_copied, 2 * b + 3)
                    turn_x(b + 2)
                S_(14, 15)
                if front:
                    if back:
                        pe.wait_ge(x_done, b)
                    values(1 - p, 2).then_inc(vb_ready, 1)
                if ahead:
                    queries(b + 2)
                weigh(b, p, 2, False)

            def turn_weights(*numbers):
                for n in numbers:
                    load, srcs, _ = turns[n]
                    if n == 0 or load != turns[n - 1][0]:
                        pe.wait_ge(c.weights_loaded[load], 16 * (4 if load == 3 else 1))
                    if n >= 3:
                        pe.wait_ge(wt_copied[(n - 3) % 2], (n - 3) // 2 + 1)
                    for k, src in enumerate(srcs):
                        last = nc.tensor.transpose(turn_banks[n % 3][:, k * P:(k + 1) * P], src, c.ident[:, :])
                    last.then_inc(wt_ready, 1)

            transposes(0, 0, 0)
            keys(0, 0, 0)
            keys(0, 0, 1)
            values(0, 0, True)
            values(0, 1, True).then_inc(va_ready, 1)
            values(0, 2, True).then_inc(vb_ready, 1)
            pe.wait_ge(k_copied, 2 * EC)
            turn_x(0)
            queries(0)
            turn_weights(0, 1)
            transposes(1, 0, 1)
            turn_weights(2, 3)
            keys(1, 1, 0)
            keys(1, 1, 1)
            turn_weights(4, 5)
            pe.wait_ge(k_copied, 4 * EC)
            turn_x(1)
            turn_weights(6)
            queries(1)
            turn_weights(*range(7, len(turns)))
            for n in range(2):
                pe.wait_ge(wt_copied[n], (len(turns) + 1 - n) // 2)
            pe.wait_ge(v_copied, 2)
            batches(pe, body)
            turn(B - 1, NG - 1, False)
            weigh(B - 1, 1, NG - 1, False)
            heads_back(B - 1)
            heads_turn(B - 1)
            project(B - 1)

        @block.scalar
        def _(act):
            def ctx_copy(b, p, start):
                act.wait_ge(ctxT_ready, b + 1)
                if not start:
                    act.wait_ge(vb_ready, b - 1)
                act.activation(ctxT[:, p, :, :], bank_ab[:, :, 0:S2], ACT.Copy).then_inc(ctxT_copied, 1)

            def key_copy(b, p, i, t):
                act.wait_ge(k_ready, EC * b + t + 1)
                if t == 0 and not (isinstance(b, int) and b == 0):
                    act.wait_ge(k_split, b)
                    act.wait_ge(k_stored[1 - p], 16 * (i + p))
                for dst in (k32[:, t, :], k_parts[:, 0, t, :]):
                    act.activation(dst, bank_ab[:, t, 0:S2], ACT.Identity, bias=c.bk[:, t:t + 1]).then_inc(k_copied, 1)

            def copy_x(b):
                act.wait_ge(xt_ready, b + 1)
                if not (isinstance(b, int) and b == 0):
                    act.wait_ge(q_ready, b)
                act.activation(xnT[:, :, :].rearrange("p e s -> p (e s)"), bank_ab[:, 0, 0:EC * S], ACT.Copy).then_inc(xt_copied, 1)

            def query_copy(b, p, i):
                act.wait_ge(q_ready, b + 1)
                if not (isinstance(b, int) and b == 0):
                    act.wait_ge(q_split, b)
                    act.wait_ge(q_stored[1 - p], 16 * (i + p))
                for t in range(EC):
                    act.activation(q32[:, t, :], bank_ab[:, 0, t * S:(t + 1) * S], ACT.Identity,
                                   bias=c.bq[:, t:t + 1], scale=float(D) ** -0.5).then_inc(q_copied, 1)
                act.wait_ge(q_copied, (EC + 1) * b + EC)
                act.activation(q_parts[:, 0, :, :], q32[:, :, :], ACT.Copy).then_inc(q_copied, 1)

            def key_second(b):
                act.wait_ge(k_rest_done, b + 1)
                act.activation(k_parts[:, 1, :, :], k_rest[:, :, :], ACT.Copy).then_inc(k_second, 1)

            def exps(b, g, first):
                if not (first and g < 2):
                    act.wait_ge(pv_done, NG * b + g - 1)
                for k in range(KC):
                    act.wait_ge(turned, KC * (NG * b + g) + k + 1)
                    act.activation(probsT[:, g % 2, k, :], bank_t[0:KP, k, 0:G * S], ACT.Exp).then_inc(exp_done, 1)

            def heads_copy(b, first):
                act.wait_ge(pv_done, NG * b + NG)
                if not first:
                    act.wait_ge(heads_ready, b)
                act.activation(headsT[:, :], bank_o[:, 0:NG * S], ACT.Copy).then_inc(headsT_copied, 1)

            def out_copy(b, first):
                act.wait_ge(outT_ready, b + 1)
                if not first:
                    act.wait_ge(y_ready, b)
                act.activation(outT[:, :, :].rearrange("p e s -> p (e s)"), bank_ab[:, 1, 0:EC * S], ACT.Copy).then_inc(outT_copied, 1)

            def body(b, p, i, first, ahead, last):
                second = isinstance(b, int) and b == 1
                if not first:
                    exps(b - 1, NG - 1, False)
                if ahead:
                    ctx_copy(b + 2, p, False)
                if not first:
                    heads_copy(b - 1, second)
                if ahead:
                    key_copy(b + 2, p, i + 1, 0)
                exps(b, 0, first)
                if ahead:
                    key_copy(b + 2, p, i + 1, 1)
                exps(b, 1, first)
                if not first:
                    out_copy(b - 1, second)
                if ahead:
                    key_second(b + 2)
                exps(b, 2, False)
                if ahead:
                    copy_x(b + 2)
                    query_copy(b + 2, p, i + 1)

            def copy_weights(*numbers):
                for n in numbers:
                    act.wait_ge(wt_ready, n + 1)
                    act.activation(turns[n][2], turn_banks[n % 3][:, :], ACT.Copy).then_inc(wt_copied[0], 1)

            for b in range(2):
                ctx_copy(b, b, True)
                if b == 1:
                    copy_weights(2)
                for t in range(EC):
                    key_copy(b, b, 0, t)
                if b == 1:
                    copy_weights(4)
                copy_x(b)
                if b == 1:
                    copy_weights(6)
                key_second(b)
                query_copy(b, b, 0)
                if b == 0:
                    copy_weights(0)
            copy_weights(*range(8, len(turns), 2))
            batches(act, body)
            exps(B - 1, NG - 1, False)
            heads_copy(B - 1, False)
            out_copy(B - 1, False)

        @block.vector
        def _(dve):
            def value_copy(b, p, half, start=False):
                dve.wait_ge(va_ready if half == 0 else vb_ready, b + 1)
                for k in ((0, 1) if half == 0 else (2,)):
                    src = bank_t[0:KP, k, 0:E] if start else bank_ab[0:KP, k // 2, (k % 2) * E:(k % 2 + 1) * E]
                    last = dve.tensor_tensor(V[:, p, k, :, 0:D], src.rearrange("p (h d) -> p h d", d=D),
                                             c.bv[:, :].rearrange("p (h d) -> p h d", d=D), ALU.add)
                last.then_inc(v_copied, 1)

            def score_max(b, first, *heads):
                for h in heads:
                    g, j = h // G, h % G
                    free = [] if first and h < 2 * G else [(shift_done, H * b + h - 2 * G + 1)]
                    wait_all(dve, v_set, (scores_ready, H * b + h + 1), *free)
                    dve.tensor_tensor_reduce(raw[:, g % 2, j, :], bank_s[h % 2][0:S, 0:S2], c.maskb[:, :], -1.0, -LEAST,
                                             ALU.add, ALU.min, neg_max[:, g % 2, j:j + 1]).then_inc(scores_read, 1)

            def normalise(b, first):
                sums = bank_ab[0:S, 0, :].rearrange("s (h w) -> s h w", w=VW)
                dve.wait_ge(heads_ready, b + 1)
                if not first:
                    dve.wait_ge(heads_done, b)
                dve.reciprocal(recip[:, :].unsqueeze(2), sums[:, :, D:D + 1]).then_inc(recip_done, 1)
                dve.wait_ge(recip_done, b + 1)
                if not first:
                    dve.wait_ge(outT_ready, b)
                dve.tensor_tensor(heads[:, :, :], sums[:, :, 0:D], recip[:, :].unsqueeze(2).to_broadcast([S, H, D]), ALU.mult).then_inc(heads_done, 1)

            def moments_of(b):
                xb = c.X[0:S, bass.ds(b, 1), :].rearrange("s a e -> s (a e)")
                dve.bn_stats(stats[:, :], xb).then_inc(stats_done, 1)
                wait_all(dve, c.x_loaded[0], (stats_done, b + 1))
                dve.bn_aggr(moments[:, :], stats[:, :]).then_inc(moments_done, 1)

            def normalise_x(b):
                xb = c.X[0:S, bass.ds(b, 1), :].rearrange("s a e -> s (a e)")
                dve.wait_ge(rstd_done, b + 1)
                if not (isinstance(b, int) and b == 0):
                    dve.wait_ge(xt_ready, b)
                dve.tensor_scalar(xn[:, :], xb, moments[:, 0:1], rstd[:, 0:1], ALU.subtract, ALU.mult).then_inc(xn_done, 1)

            def key_third(b):
                dve.wait_ge(k_second, b + 1)
                dve.tensor_tensor(k_parts[:, 2, :, :], k_rest[:, :, :], k_parts[:, 1, :, :], ALU.subtract).then_inc(k_split, 1)

            def split_queries(b):
                dve.wait_ge(q_copied, (EC + 1) * (b + 1))
                if not (isinstance(b, int) and b == 0):
                    dve.wait_ge(q_split, b)
                dve.tensor_tensor(q_rest[:, :, :], q32[:, :, :], q_parts[:, 0, :, :], ALU.subtract).then_inc(q_rest_done, 1)
                dve.wait_ge(q_rest_done, b + 1)
                dve.tensor_copy(q_parts[:, 1, :, :], q_rest[:, :, :]).then_inc(q_second, 1)
                dve.wait_ge(q_second, b + 1)
                dve.tensor_tensor(q_parts[:, 2, :, :], q_rest[:, :, :], q_parts[:, 1, :, :], ALU.subtract).then_inc(q_split, 1)

            def residual(b):
                dve.wait_ge(y_ready, b + 1)
                dve.wait_ge(xbias_done, b + 1)
                xb = c.X[0:S, bass.ds(b, 1), :].rearrange("s a e -> s (a e)")
                dve.scalar_tensor_tensor(xb, bank_ab[0:S, 1, 0:E], c.tanh_g[:, 0:1], xb, ALU.mult, ALU.add).then_inc(x_done, 1)

            def body(b, p, i, first, ahead, last):
                second = isinstance(b, int) and b == 1
                if ahead:
                    moments_of(b + 2)
                score_max(b, first, 0, 1)
                if not first and not last:
                    split_queries(b + 1)
                score_max(b, first, *range(2, 7))
                if ahead:
                    normalise_x(b + 2)
                score_max(b, first, 7)
                if not first:
                    normalise(b - 1, second)
                score_max(b, first, 8, 9, 10)
                if not last:
                    value_copy(b + 1, 1 - p, 0)
                score_max(b, first, 11, 12)
                if ahead:
                    key_third(b + 2)
                if not first:
                    residual(b - 1)
                score_max(b, first, 13, 14, 15)
                if not last:
                    value_copy(b + 1, 1 - p, 1)
                if second:
                    dve.wait_ge(c.x_loaded[1], 16 * X_LOADS)

            dve.wait_ge(c.x_loaded[0], 16)
            def copy_weights(*numbers):
                for n in numbers:
                    dve.wait_ge(wt_ready, n + 1)
                    dve.tensor_copy(turns[n][2], turn_banks[n % 3][:, :]).then_inc(wt_copied[1], 1)

            moments_of(0)
            normalise_x(0)
            dve.wait_ge(v_set, 1)
            value_copy(0, 0, 0, True)
            value_copy(0, 0, 1, True)
            key_third(0)
            split_queries(0)
            moments_of(1)
            copy_weights(1)
            normalise_x(1)
            copy_weights(3, 5)
            key_third(1)
            split_queries(1)
            copy_weights(*range(7, len(turns), 2))
            batches(dve, body)
            normalise(B - 1, False)
            residual(B - 1)

        @block.gpsimd
        def _(pool):
            def shift(b, g, first):
                for j in range(G):
                    h = G * g + j
                    free = [] if j or (first and g < 2) else [(turned, KC * (NG * b + g - 1))]
                    wait_all(pool, v_set, (scores_read, H * b + h + 1), *free)
                    pool.tensor_scalar(shifted[:, g % 2, j, :], raw[:, g % 2, j, :], -1.0, neg_max[:, g % 2, j:j + 1],
                                       ALU.mult, ALU.add).then_inc(shift_done, 1)

            def key_rest(b):
                pool.wait_ge(k_copied, 2 * EC * (b + 1))
                if not (isinstance(b, int) and b == 0):
                    pool.wait_ge(k_split, b)
                pool.tensor_tensor(k_rest[:, :, :], k32[:, :, :], k_parts[:, 0, :, :], ALU.subtract).then_inc(k_rest_done, 1)

            def inverse_deviation(b):
                wait_all(pool, half_set, (moments_done, b + 1))
                pool.tensor_scalar(var_eps[:, :], moments[:, 1:2], LN_EPS, None, ALU.add).then_inc(eps_added, 1)
                pool.wait_ge(eps_added, b + 1)
                pool.tensor_tensor(rstd[:, :], var_eps[:, :], minus_half[:, :], ALU.pow).then_inc(rstd_done, 1)

            def add_bias(b):
                pool.wait_ge(xn_done, b + 1)
                xb = c.X[0:S, bass.ds(b, 1), :].rearrange("s a e -> s (a e)")
                pool.tensor_tensor(xb, xb, c.bo[:, :], ALU.add).then_inc(xbias_done, 1)

            def body(b, p, i, first, ahead, last):
                shift(b, 0, first)
                if ahead:
                    inverse_deviation(b + 2)
                shift(b, 1, first)
                if ahead:
                    key_rest(b + 2)
                shift(b, 2, first)
                if ahead:
                    add_bias(b + 2)
                shift(b, 3, first)

            pool.memset(minus_half[:, :], -0.5).then_inc(half_set, 1)
            pool.memset(V[:, :, :, :, :], 0.0).then_inc(v_cleared, 1)
            pool.wait_ge(half_set, 1)
            for b in range(2):
                inverse_deviation(b)
                if b == 0:
                    pool.wait_ge(v_cleared, 1)
                    for p in range(2):
                        for k in range(KC):
                            last_set = pool.memset(V[:, p, k, :, D:D + 1], 1.0)
                    last_set.then_inc(v_set, 1)
                key_rest(b)
                add_bias(b)
            batches(pool, body)


def switch(nc, z, d, c):
    B, S, E, EC, G, H, D, X, M2 = z.B, z.S, z.E, z.EC, z.G, z.H2, z.D2, z.X, z.M2
    NG = H // G
    T16, T8 = S // 16, S // 8
    W = D + 1
    TOP_STEPS, TOP_BEST = 13, 7
    with ExitStack() as ctx:
        sb = lambda name, shape, dt=F32: ctx.enter_context(nc.sbuf_tensor(name, shape, dt))
        ps = lambda name, shape: ctx.enter_context(nc.psum_tensor(name, shape, F32))
        sem = lambda name: ctx.enter_context(nc.semaphore(name))
        dram = lambda name, shape: nc.dram_tensor(name, shape, F32).ap()
        proj_dram = dram("proj_dram", (B, S, X * D))
        mix_dram = dram("mix_dram", (B, S, X * H))
        pick_dram = dram("pick_dram", (B, S, H * X))

        minus_half = sb("minus_half2", [S, 1])
        rank_w = sb("rank_w", [S, X])
        stats, moments = sb("stats2", [S, 6]), sb("moments2", [S, 2])
        var_eps, rstd = sb("var_eps2", [S, 1]), sb("rstd2", [S, 1])
        xn = sb("xn2", [S, E])
        xnT = sb("xnT2", [P, EC, 4, S])
        gates = sb("gates", [S, 2 * H, X])
        proj = sb("proj", [S, X * D])
        best = sb("best", [S, 2, 2 * H])
        tie = sb("tie", [S, 2 * H, X])
        first_tie = sb("first_tie", [S, 2 * H])
        one_hot = sb("one_hot", [S, 2, 2 * H, X])
        rest = sb("rest", [S, 2 * H, X])
        sig = sb("sig", [S, 2, H])
        mix_part = sb("mix_part", [S, 2, H, X])
        mix, pick = sb("mix", [S, X, H]), sb("pick", [S, H, X])
        proj_te = sb("proj_te", [P, 2, T16, D])
        mix_te = sb("mix_te", [P, 2, T16, H])
        pick_th = sb("pick_th", [P, 2, T8, X])
        mix_bd = sb("mix_bd", [P, T16, 16, H])
        pick_bd = sb("pick_bd", [P, T8, 8, X], BF16)
        qT = sb("qT", [P, 2, M2, 2, S])
        kz = sb("kz", [P, 2, M2, 2, 2, S])
        vT = sb("vT", [P, H // 2, S])
        v = sb("v", [S, 2, H, W])
        neg_max = sb("max2", [S, 2, G])
        shifted = sb("shifted2", [S, 2, G, S])
        probsT = sb("probsT2", [S, 2, G * S])
        attT = sb("attT", [W, S, H])
        recip = sb("recip2", [P, T8])
        att, att_rest = sb("att", [P, T8, D]), sb("att_rest", [P, T8, D])
        att_parts = sb("att_parts", [P, PARTS, T8, D], BF16)
        uT = sb("uT", [P, X // 2, S])
        bank_ab = ps("bank2_ab", [P, 2, PSUM_BANK])
        bank_s = [ps(f"bank2_s{i}", [P, PSUM_BANK]) for i in range(2)]
        bank_t, bank_o = ps("bank2_t", [P, PSUM_BANK]), ps("bank2_o", [P, PSUM_BANK])
        bank_gh = ps("bank2_gh", [P, 2, PSUM_BANK])

        consts_done, kz_cleared, ones_set = sem("consts_done"), sem("kz_cleared"), sem("ones_set")
        stats_done, moments_done, eps_added, rstd_done, xn_done = (sem(n) for n in ("stats2_done", "moments2_done", "eps2_added", "rstd2_done", "xn2_done"))
        xt_ready, xt_copied = sem("xt2_ready"), sem("xt2_copied")
        gates_ready, gates_copied = sem("gates_ready"), sem("gates_copied")
        proj_ready, proj_copied = sem("proj_ready"), sem("proj_copied")
        mix_part_done = sem("mix_part_done")
        top_step, negexp_done, mix_done, pick_done = sem("top_step"), sem("negexp_done"), sem("mix_done"), sem("pick_done")
        proj_stored, mix_stored, pick_stored = ([sem(f"{n}{p}") for p in range(2)] for n in ("proj_stored", "mix_stored", "pick_stored"))
        te_loaded = [sem(f"te_loaded{p}") for p in range(2)]
        mix_bd_done, pick_bd_done = sem("mix_bd_done"), sem("pick_bd_done")
        q_ready, q_copied, kk_ready, kk_copied = sem("q2_ready"), sem("q2_copied"), sem("k2_ready"), sem("k2_copied")
        vt_ready, vt_copied, v_ready, v_copied = sem("vt_ready"), sem("vt_copied"), sem("v2_ready"), sem("v2_copied")
        scores_ready, max_done, shift_done = sem("scores2_ready"), sem("max2_done"), sem("shift2_done")
        turned, exp_done, pv_done, attT_copied = sem("turned2"), sem("exp2_done"), sem("pv2_done"), sem("attT_copied")
        att_first, att_rest_done, att_second, att_split = sem("att_first"), sem("att_rest_done"), sem("att_second"), sem("att_split")
        att_ready, recip_done, att_done = sem("att_ready"), sem("recip2_done"), sem("att_done")
        u_ready, u_copied, y_ready, out_done = sem("u_ready"), sem("u_copied"), sem("y2_ready"), sem("out_done")
        stored = [sem(f"out_stored{p}") for p in range(2)]
        block = ctx.enter_context(nc.Block())

        def split(e):
            b, r, j = e
            return b, r % 2, 2 * j + r // 2

        def after(e, n=1):
            b, r, j = e
            return b + n, (r + n) % 4, j + (r + n) // 4

        def before(e):
            return after(e, -1)

        def pair_of(e, n=0):
            b, r, j = e
            return 2 * j + r // 2 + n, (r // 2 + n) % 2

        def pipeline(eng, start, body, end):
            def run(b, r, j, known):
                has = Names()
                has.back = not known or b > 0
                has.front, has.pre, has.pair, has.ahead = (not known or b + n < B for n in (1, 2, 2, 4))
                body((b, r, j), has)

            start()
            for r in range(4):
                run(r, r, 0, True)
            with eng.Fori(1, B // 4 - 1) as j:
                for r in range(4):
                    run(4 * j + r, r, j, False)
            for r in range(4):
                run(B - 4 + r, r, B // 4 - 1, True)
            end((B - 1, 3, B // 4 - 1))

        def wait(eng, sem, n):
            if not isinstance(n, int) or n > 0:
                eng.wait_ge(sem, n)

        @block.sync
        def _(sp):
            def exchange(e):
                b, p, i = split(e)
                rows = lambda t, w: t[bass.ds(b, 1)].rearrange("a s n -> (a s n)").rearrange("(g p w) -> p g w", p=P, w=w)
                start = isinstance(b, int) and b < 2
                sp.wait_ge(pick_done, b + 1)
                sp.dma_start(flat(pick_dram[bass.ds(b, 1)]), pick[:, :, :].rearrange("s h e -> s (h e)")).then_inc(pick_stored[p], 16)
                sp.wait_ge(mix_done, b + 1)
                sp.dma_start(flat(mix_dram[bass.ds(b, 1)]), mix[:, :, :].rearrange("s e h -> s (e h)")).then_inc(mix_stored[p], 16)
                sp.wait_ge(proj_copied, b + 1)
                sp.dma_start(flat(proj_dram[bass.ds(b, 1)]), proj[:, :]).then_inc(proj_stored[p], 16)
                wait_all(sp, consts_done, (mix_stored[p], 16 * i + 16), *([] if start else [(mix_bd_done, T16 * (b - 1))]))
                sp.dma_start(mix_te[:, p, :, :], rows(mix_dram, H)).then_inc(te_loaded[p], 16)
                wait_all(sp, consts_done, (proj_stored[p], 16 * i + 16), *([] if start else [(vt_ready, 4 * (b - 1))]))
                sp.dma_start(proj_te[:, p, :, :], rows(proj_dram, D)).then_inc(te_loaded[p], 16)
                wait_all(sp, consts_done, (pick_stored[p], 16 * i + 16), *([] if start else [(pick_bd_done, T8 * (b - 1))]))
                sp.dma_start(pick_th[:, p, :, :], rows(pick_dram, X)).then_inc(te_loaded[p], 16)

            def store(e):
                b, p, i = split(e)
                sp.wait_ge(out_done, b + 1)
                sp.dma_start(flat(d.out[bass.ds(b, 1)]), c.X[0:S, bass.ds(b, 1), :].rearrange("s a e -> s (a e)")).then_inc(stored[p], 16)

            def start():
                exchange((0, 0, 0))
                exchange((1, 1, 0))

            def body(cur, has):
                if has.back:
                    store(before(cur))
                if has.pre:
                    exchange(after(cur, 2))

            pipeline(sp, start, body, store)
            for p in range(2):
                sp.wait_ge(stored[p], 16 * (B // 2))

        @block.tensor
        def _(pe):
            def turn_x(e):
                b, p, i = split(e)
                pe.wait_ge(xn_done, b + 1)
                for e in range(EC):
                    last = nc.tensor.transpose(bank_ab[:, 0, e * S:(e + 1) * S], xn[:, e * P:(e + 1) * P], c.ident[0:S, 0:S])
                last.then_inc(xt_ready, 1)

            def make_gates(e):
                b, r, j = e
                pe.wait_ge(xt_copied, b + 1)
                for e in range(EC):
                    last = nc.tensor.matmul(bank_ab[0:S, 1, 0:2 * H * X], xnT[:, e, r, :], c.wgT[:, e, :], start=(e == 0), stop=(e == EC - 1))
                last.then_inc(gates_ready, 1)

            def make_proj(e):
                b, r, j = e
                pe.wait_ge(gates_copied, b + 1)
                for e in range(EC):
                    last = nc.tensor.matmul(bank_ab[0:S, 1, 0:X * D], xnT[:, e, r, :], c.wv2T[:, e, :], start=(e == 0), stop=(e == EC - 1))
                last.then_inc(proj_ready, 1)

            def project(pair, weights, f, ready):
                Q, h = pair
                for m in range(2):
                    for e in range(EC):
                        w = weights[:, e, (2 * f + m) * P:(2 * f + m + 1) * P]
                        last = nc.tensor.matmul(bank_ab[:, f % 2, m * 2 * S:(m + 1) * 2 * S], w,
                                                xnT[:, e, 2 * h:2 * h + 2, :].rearrange("p r s -> p (r s)"), start=(e == 0), stop=(e == EC - 1))
                last.then_inc(ready, 1)

            def queries(pair, f):
                Q, h = pair
                if f == 0:
                    wait(pe, out_done, 2 * Q - 3)
                    pe.wait_ge(xt_copied, 2 * Q + 2)
                elif f == 1:
                    pe.wait_ge(proj_copied, 1 if isinstance(Q, int) and Q == 0 else 2 * Q)
                else:
                    pe.wait_ge(q_copied, 4 * Q + f - 1)
                project(pair, c.wq2T, f, q_ready)

            def keys(pair, f):
                Q, h = pair
                if f == 0:
                    wait(pe, out_done, 2 * Q - 2)
                    pe.wait_ge(q_copied, 4 * Q + 4)
                elif f == 1:
                    pe.wait_ge(proj_copied, 2 * Q + 1)
                else:
                    pe.wait_ge(kk_copied, 2 * (4 * Q + f - 1))
                project(pair, c.wk2T, f, kk_ready)

            def fill(e, f):
                (queries if e[1] % 2 == 0 else keys)(pair_of(e, 1), f)

            def fill_left(e, f):
                n = 4 * pair_of(e, 1)[0] + f + 1
                if e[1] % 2 == 0:
                    pe.wait_ge(q_copied, n)
                else:
                    pe.wait_ge(kk_copied, 2 * n)

            def mix_values(e, n):
                b, p, i = split(e)
                if n == 0:
                    pe.wait_ge(te_loaded[p], 48 * i + 48)
                if n < 2:
                    wait(pe, u_copied, 4 * (b - 1))
                else:
                    pe.wait_ge(vt_copied, 8 * b + 2 * (n - 2) + 2)
                for k in (2 * n, 2 * n + 1):
                    if k < T16:
                        pe.wait_ge(mix_bd_done, T16 * b + k + 1)
                        last = nc.tensor.matmul(bank_gh[0:D, n % 2, (k % 2) * 256:(k % 2 + 1) * 256],
                                                proj_te[:, p, k, :],
                                                mix_bd[:, k, :, :].rearrange("p t h -> p (t h)"), start=True, stop=True)
                last.then_inc(vt_ready, 1)

            def turn_values(e):
                b, p, i = split(e)
                pe.wait_ge(vt_copied, 8 * b + 8)
                for n in range(2):
                    for m in range(H // 4):
                        last = nc.tensor.transpose(bank_gh[0:S, n, m * P:(m + 1) * P], vT[:, n * H // 4 + m, :], c.ident[:, :])
                    last.then_inc(v_ready, 1)

            def scores(e, g):
                b, r, j = e
                Q, h = pair_of(e)
                if g == 0:
                    pe.wait_ge(q_copied, 4 * Q + 4)
                    pe.wait_ge(kk_copied, 8 * Q + 8)
                wait(pe, shift_done, NG * b + g - 1)
                for m in (2 * g, 2 * g + 1):
                    last = nc.tensor.matmul(bank_s[g % 2][0:S, (m % 2) * 2 * S:(m % 2 + 1) * 2 * S], qT[:, h, m, r % 2, :],
                                            kz[:, h, m, r % 2, :, :].rearrange("p a s -> p (a s)"), start=True, stop=True)
                last.then_inc(scores_ready, 1)

            def turn(e, g):
                b, p, i = split(e)
                pe.wait_ge(shift_done, NG * b + g + 1)
                wait(pe, exp_done, NG * b + g)
                for j in range(G):
                    last = nc.tensor.transpose(bank_t[0:S, j * S:(j + 1) * S], shifted[:, g % 2, j, :], c.ident[0:S, 0:S])
                last.then_inc(turned, 1)

            def weigh(e, g):
                b, p, i = split(e)
                if g == 0:
                    pe.wait_ge(v_copied, 2 * b + 2)
                    if isinstance(b, int) and b == 0:
                        pe.wait_ge(ones_set, 1)
                        pe.wait_ge(kz_cleared, 1)
                pe.wait_ge(exp_done, NG * b + g + 1)
                wait(pe, attT_copied, NG * b + g)
                for j in range(G):
                    last = nc.tensor.matmul(bank_o[0:W, j * S:(j + 1) * S], v[:, p, G * g + j, :], probsT[:, g % 2, j * S:(j + 1) * S],
                                            start=True, stop=True)
                last.then_inc(pv_done, 1)

            def attention_rows(e):
                b, p, i = split(e)
                pe.wait_ge(attT_copied, NG * b + NG)
                pe.wait_ge(v_copied, 2 * B if isinstance(b, int) and b == B - 1 else 2 * b + 4)
                for n in range(T8):
                    last = nc.tensor.transpose(bank_gh[:, n // 7, (n % 7) * W:(n % 7 + 1) * W],
                                               attT[:, 8 * n:8 * n + 8, :].rearrange("d t h -> d (t h)"), c.ident[0:W, 0:W])
                    if n % 7 == 6:
                        last.then_inc(att_ready, 1)

            def sum_heads(e):
                b, p, i = split(e)
                pe.wait_ge(att_split, b + 1)
                pe.wait_ge(pick_bd_done, T8 * b + T8)
                for n in range(T8):
                    for q in range(PARTS):
                        last = nc.tensor.matmul(bank_gh[0:D, n // 8, (n % 8) * 8 * X:(n % 8 + 1) * 8 * X], att_parts[:, q, n, :],
                                                pick_bd[:, n, :, :].rearrange("p t e -> p (t e)"), start=(q == 0), stop=(q == PARTS - 1))
                    if n in (7, T8 - 1):
                        last.then_inc(u_ready, 1)

            def output(e):
                b, p, i = split(e)
                pe.wait_ge(u_copied, 4 * b + 4)
                for m in range(X // 2):
                    last = nc.tensor.matmul(bank_ab[0:S, 0, 0:E], uT[:, m, :], c.wo2T[:, m, :], start=(m == 0), stop=(m == X // 2 - 1))
                last.then_inc(y_ready, 1)

            def start():
                entry = [(b, b, 0) for b in range(4)]
                turn_x(entry[0])
                make_gates(entry[0])
                make_proj(entry[0])
                turn_x(entry[1])
                for f in range(4):
                    queries((0, 0), f)
                for f in range(4):
                    keys((0, 0), f)
                pe.wait_ge(kk_copied, 8)
                make_gates(entry[1])
                turn_x(entry[2])
                make_proj(entry[1])
                pe.wait_ge(xt_copied, 3)
                turn_x(entry[3])
                for n in range(4):
                    mix_values((0, 0, 0), n)
                turn_values((0, 0, 0))
                scores((0, 0, 0), 0)

            def body(cur, has):
                scores(cur, 1)
                if has.pair:
                    fill(cur, 0)
                if has.back:
                    attention_rows(before(cur))
                turn(cur, 0)
                if has.pair:
                    fill(cur, 1)
                weigh(cur, 0)

                scores(cur, 2)
                if has.pair:
                    fill(cur, 2)
                    fill(cur, 3)
                turn(cur, 1)
                if has.back:
                    sum_heads(before(cur))
                weigh(cur, 1)

                scores(cur, 3)
                if has.pair:
                    fill_left(cur, 2)
                if has.ahead:
                    turn_x(after(cur, 4))
                if has.front:
                    mix_values(after(cur), 0)
                    mix_values(after(cur), 1)
                if has.pre:
                    fill_left(cur, 3)
                    make_gates(after(cur, 2))
                turn(cur, 2)
                if has.back:
                    if has.ahead:
                        pe.wait_ge(xt_copied, cur[0] + 5)
                    elif not has.pair:
                        pe.wait_ge(out_done, cur[0] - 1)
                    output(before(cur))
                weigh(cur, 2)

                if has.front:
                    scores(after(cur), 0)
                    mix_values(after(cur), 2)
                    mix_values(after(cur), 3)
                turn(cur, 3)
                if has.pre:
                    make_proj(after(cur, 2))
                if has.front:
                    turn_values(after(cur))
                weigh(cur, 3)

            def end(e):
                attention_rows(e)
                sum_heads(e)
                pe.wait_ge(out_done, B - 1)
                output(e)

            pipeline(pe, start, body, end)

        @block.scalar
        def _(act):
            def copy_x(e):
                b, r, j = e
                act.wait_ge(xt_ready, b + 1)
                wait(act, kk_ready, 4 * (pair_of(e)[0] - 1))
                wait(act, proj_ready, b - 3)
                act.activation(xnT[:, :, r, :], bank_ab[:, 0, 0:EC * S].rearrange("p (e s) -> p e s", e=EC), ACT.Copy).then_inc(xt_copied, 1)

            def copy_gates(e):
                b, p, i = split(e)
                act.wait_ge(gates_ready, b + 1)
                wait(act, top_step, TOP_STEPS * b)
                act.activation(gates[:, :, :].rearrange("s g e -> s (g e)"), bank_ab[0:S, 1, 0:2 * H * X], ACT.Copy).then_inc(gates_copied, 1)

            def negated_exp(e):
                b, p, i = split(e)
                act.wait_ge(top_step, TOP_STEPS * b + TOP_BEST)
                act.activation(sig[:, :, :], best[:, :, 0:H], ACT.Exp, scale=-1.0).then_inc(negexp_done, 1)

            def copy_proj(e):
                b, p, i = split(e)
                act.wait_ge(proj_ready, b + 1)
                wait(act, proj_stored[1 - p], 16 * (i + p))
                act.activation(proj[:, :], bank_ab[0:S, 1, 0:X * D], ACT.Copy).then_inc(proj_copied, 1)

            def copy_queries(pair, f):
                Q, h = pair
                if f == 0:
                    wait(act, scores_ready, NG * 2 * (Q - 1))
                act.wait_ge(q_ready, 4 * Q + f + 1)
                act.activation(qT[:, h, 2 * f:2 * f + 2, :, :].rearrange("p m r s -> p (m r s)"),
                               bank_ab[:, f % 2, 0:4 * S], ACT.Copy, scale=float(D) ** -0.5).then_inc(q_copied, 1)

            def copy_keys(pair, f):
                Q, h = pair
                act.wait_ge(kk_ready, 4 * Q + f + 1)
                for a in range(2):
                    act.activation(kz[64 * a:64 * a + 64, h, 2 * f:2 * f + 2, :, a, :],
                                   bank_ab[64 * a:64 * a + 64, f % 2, 0:4 * S].rearrange("p (m r s) -> p m r s", m=2, r=2), ACT.Copy).then_inc(kk_copied, 1)

            def copy_fill(e, f):
                (copy_queries if e[1] % 2 == 0 else copy_keys)(pair_of(e, 1), f)

            def first_part(e):
                b, p, i = split(e)
                act.wait_ge(att_done, 2 * b + 2)
                wait(act, u_ready, 2 * b)
                act.activation(att_parts[:, 0, :, :], att[:, :, :], ACT.Copy).then_inc(att_first, 1)

            def second_part(e):
                b, p, i = split(e)
                act.wait_ge(att_rest_done, b + 1)
                act.activation(att_parts[:, 1, :, :], att_rest[:, :, :], ACT.Copy).then_inc(att_second, 1)

            def copy_mixed(e, n):
                b, p, i = split(e)
                act.wait_ge(vt_ready, 4 * b + n + 1)
                if n == 0:
                    wait(act, v_ready, 2 * b)
                tokens = min(32, S - 32 * n)
                for a in range(2):
                    src = bank_gh[0:D, n % 2, 0:tokens * H].rearrange("p (t m a) -> p m t a", a=2, m=H // 2)[:, :, :, a]
                    act.activation(vT[D * a:D * a + D, :, 32 * n:32 * n + tokens], src, ACT.Copy).then_inc(vt_copied, 1)

            def copy_values(e):
                b, p, i = split(e)
                wait(act, pv_done, NG * (b - 1))
                for n in range(2):
                    act.wait_ge(v_ready, 2 * b + n + 1)
                    act.activation(v[:, p, n * H // 2:(n + 1) * H // 2, 0:D], bank_gh[0:S, n, :].rearrange("s (h d) -> s h d", d=D), ACT.Copy).then_inc(v_copied, 1)

            def exps(e, g):
                b, p, i = split(e)
                act.wait_ge(turned, NG * b + g + 1)
                wait(act, pv_done, NG * b + g - 1)
                act.activation(probsT[:, g % 2, :], bank_t[0:S, 0:G * S], ACT.Exp).then_inc(exp_done, 1)

            def copy_attention(e, g):
                b, p, i = split(e)
                act.wait_ge(pv_done, NG * b + g + 1)
                if g == 0:
                    wait(act, att_ready, 2 * b)
                act.activation(attT[:, :, G * g:G * g + G], bank_o[0:W, 0:G * S].rearrange("w (j s) -> w s j", j=G), ACT.Copy).then_inc(attT_copied, 1)

            def start():
                entry = [(b, b, 0) for b in range(4)]
                copy_x(entry[0])
                copy_gates(entry[0])
                copy_proj(entry[0])
                copy_x(entry[1])
                act.wait_ge(kz_cleared, 1)
                for f in range(4):
                    copy_queries((0, 0), f)
                negated_exp(entry[0])
                for f in range(4):
                    copy_keys((0, 0), f)
                copy_gates(entry[1])
                copy_x(entry[2])
                copy_proj(entry[1])
                copy_x(entry[3])
                negated_exp(entry[1])
                for n in range(4):
                    copy_mixed((0, 0, 0), n)
                copy_values((0, 0, 0))

            def body(cur, has):
                if has.pair:
                    copy_fill(cur, 0)
                exps(cur, 0)
                if has.back:
                    first_part(before(cur))
                if has.pair:
                    copy_fill(cur, 1)
                copy_attention(cur, 0)
                if has.back:
                    second_part(before(cur))
                if has.pair:
                    copy_fill(cur, 2)
                    copy_fill(cur, 3)
                exps(cur, 1)
                copy_attention(cur, 1)
                if has.ahead:
                    copy_x(after(cur, 4))
                if has.front:
                    copy_mixed(after(cur), 0)
                    copy_mixed(after(cur), 1)
                if has.pre:
                    copy_gates(after(cur, 2))
                exps(cur, 2)
                copy_attention(cur, 2)
                if has.front:
                    copy_mixed(after(cur), 2)
                    copy_mixed(after(cur), 3)
                exps(cur, 3)
                if has.front:
                    copy_values(after(cur))
                copy_attention(cur, 3)
                if has.pre:
                    negated_exp(after(cur, 2))
                    copy_proj(after(cur, 2))

            def end(e):
                first_part(e)
                second_part(e)

            pipeline(act, start, body, end)

        @block.vector
        def _(dve):
            gsz = [S, 2 * H, X]

            def moments_of(e):
                b, p, i = split(e)
                xb = c.X[0:S, bass.ds(b, 1), :].rearrange("s a e -> s (a e)")
                dve.bn_stats(stats[:, :], xb).then_inc(stats_done, 1)
                wait_all(dve, consts_done, (stats_done, b + 1))
                dve.bn_aggr(moments[:, :], stats[:, :]).then_inc(moments_done, 1)

            def normalise_x(e):
                b, p, i = split(e)
                xb = c.X[0:S, bass.ds(b, 1), :].rearrange("s a e -> s (a e)")
                dve.wait_ge(rstd_done, b + 1)
                wait(dve, xt_ready, b)
                dve.tensor_scalar(xn[:, :], xb, moments[:, 0:1], rstd[:, 0:1], ALU.subtract, ALU.mult).then_inc(xn_done, 1)

            def select(e):
                b, p, i = split(e)
                dve.wait_ge(gates_copied, b + 1)
                steps = 0

                def step(ins):
                    nonlocal steps
                    steps += 1
                    ins.then_inc(top_step, 1)
                    dve.wait_ge(top_step, TOP_STEPS * b + steps)

                wait(dve, negexp_done, b)
                src = gates
                for r in range(2):
                    step(dve.tensor_reduce(best[:, r, :], src[:, :, :], AXX, ALU.max))
                    step(dve.tensor_tensor(tie[:, :, :], src[:, :, :], best[:, r, :].unsqueeze(2).to_broadcast(gsz), ALU.is_ge))
                    step(dve.tensor_tensor(tie[:, :, :], tie[:, :, :], rank_w[:, :].unsqueeze(1).to_broadcast(gsz), ALU.mult))
                    step(dve.tensor_reduce(first_tie[:, :], tie[:, :, :], AXX, ALU.max))
                    step(dve.tensor_tensor(one_hot[:, r, :, :], tie[:, :, :], first_tie[:, :].unsqueeze(2).to_broadcast(gsz), ALU.is_ge))
                    if r == 0:
                        step(dve.scalar_tensor_tensor(rest[:, :, :], one_hot[:, 0, :, :], LEAST, gates[:, :, :], ALU.mult, ALU.add))
                    src = rest
                wait(dve, pick_stored[1 - p], 16 * (i + p))
                dve.tensor_tensor(pick[:, :, :], one_hot[:, 0, H:2 * H, :], one_hot[:, 1, H:2 * H, :], ALU.add).then_inc(pick_done, 1)
                dve.wait_ge(negexp_done, b + 1)
                step(dve.tensor_scalar(sig[:, :, :], sig[:, :, :], 1.0, None, ALU.add))
                step(dve.reciprocal(sig[:, :, :], sig[:, :, :]))
                for r in range(2):
                    last = dve.tensor_tensor(mix_part[:, r, :, :], one_hot[:, r, 0:H, :], sig[:, r, :].unsqueeze(2).to_broadcast([S, H, X]), ALU.mult)
                    last.then_inc(mix_part_done, 1)
                dve.wait_ge(mix_part_done, 2 * b + 2)
                wait(dve, mix_stored[1 - p], 16 * (i + p))
                dve.tensor_tensor(mix[:, :, :].rearrange("s e h -> s h e"), mix_part[:, 0, :, :], mix_part[:, 1, :, :], ALU.add).then_inc(mix_done, 1)

            def shift(e, g):
                b, p, i = split(e)
                dve.wait_ge(scores_ready, NG * b + g + 1)
                sc = bank_s[g % 2][0:S, 0:G * S].rearrange("s (j t) -> s j t", j=G)
                dve.tensor_reduce(neg_max[:, g % 2, :], sc, AXX, ALU.max).then_inc(max_done, 1)
                dve.wait_ge(max_done, NG * b + g + 1)
                wait(dve, turned, NG * b + g - 1)
                dve.tensor_tensor(shifted[:, g % 2, :, :], sc, neg_max[:, g % 2, :].unsqueeze(2).to_broadcast([S, G, S]), ALU.subtract).then_inc(shift_done, 1)

            def normalise(e):
                b, p, i = split(e)
                if not (isinstance(b, int) and b == 0):
                    dve.wait_ge(att_split, b)
                for n in range(2):
                    a = bank_gh[:, n, 0:7 * W].rearrange("p (t w) -> p t w", w=W)
                    dve.wait_ge(att_ready, 2 * b + n + 1)
                    dve.reciprocal(recip[:, 7 * n:7 * n + 7].unsqueeze(2), a[:, :, D:W]).then_inc(recip_done, 1)
                    dve.wait_ge(recip_done, 2 * b + n + 1)
                    dve.tensor_tensor(att[:, 7 * n:7 * n + 7, :], a[:, :, 0:D],
                                      recip[:, 7 * n:7 * n + 7].unsqueeze(2).to_broadcast([P, 7, D]), ALU.mult).then_inc(att_done, 1)

            def rest_of_attention(e):
                b, p, i = split(e)
                dve.wait_ge(att_first, b + 1)
                dve.tensor_tensor(att_rest[:, :, :], att[:, :, :], att_parts[:, 0, :, :], ALU.subtract).then_inc(att_rest_done, 1)

            def third_part(e):
                b, p, i = split(e)
                dve.wait_ge(att_second, b + 1)
                dve.tensor_tensor(att_parts[:, 2, :, :], att_rest[:, :, :], att_parts[:, 1, :, :], ALU.subtract).then_inc(att_split, 1)

            def copy_sums(e):
                b, p, i = split(e)
                wait(dve, y_ready, b)
                for n in range(2):
                    dve.wait_ge(u_ready, 2 * b + n + 1)
                    tokens = min(64, S - 64 * n)
                    for a in range(2):
                        src = bank_gh[0:D, n, 0:tokens * X].rearrange("p (t m a) -> p m t a", a=2, m=X // 2)[:, :, :, a]
                        dve.tensor_copy(uT[D * a:D * a + D, :, 64 * n:64 * n + tokens], src).then_inc(u_copied, 1)

            def residual(e):
                b, p, i = split(e)
                dve.wait_ge(y_ready, b + 1)
                xb = c.X[0:S, bass.ds(b, 1), :].rearrange("s a e -> s (a e)")
                dve.scalar_tensor_tensor(xb, bank_ab[0:S, 0, 0:E], c.tanh_g[:, 1:2], xb, ALU.mult, ALU.add).then_inc(out_done, 1)

            def start():
                entry = [(b, b, 0) for b in range(4)]
                for e in entry[0:2]:
                    moments_of(e)
                    normalise_x(e)
                dve.memset(v[:, :, :, D:W], 1.0).then_inc(ones_set, 1)
                select(entry[0])
                for e in entry[2:4]:
                    moments_of(e)
                    normalise_x(e)
                select(entry[1])
                shift((0, 0, 0), 0)

            def body(cur, has):
                if has.back:
                    normalise(before(cur))
                shift(cur, 1)
                if has.back:
                    rest_of_attention(before(cur))
                if has.ahead:
                    moments_of(after(cur, 4))
                if has.back:
                    third_part(before(cur))
                if has.ahead:
                    normalise_x(after(cur, 4))
                shift(cur, 2)
                if has.back:
                    copy_sums(before(cur))
                shift(cur, 3)
                if has.back:
                    residual(before(cur))
                if has.front:
                    shift(after(cur), 0)
                if has.pre:
                    select(after(cur, 2))

            def end(e):
                normalise(e)
                rest_of_attention(e)
                third_part(e)
                copy_sums(e)
                residual(e)

            for e in range(X):
                last = dve.memset(rank_w[:, e:e + 1], float(X - e))
            last.then_inc(consts_done, 1)
            dve.wait_ge(consts_done, 2)
            pipeline(dve, start, body, end)

        @block.gpsimd
        def _(pool):
            def inverse_deviation(e):
                b, p, i = split(e)
                wait_all(pool, consts_done, (moments_done, b + 1))
                pool.tensor_scalar(var_eps[:, :], moments[:, 1:2], LN_EPS, None, ALU.add).then_inc(eps_added, 1)
                pool.wait_ge(eps_added, b + 1)
                pool.tensor_tensor(rstd[:, :], var_eps[:, :], minus_half[:, :], ALU.pow).then_inc(rstd_done, 1)

            def spread_mix(e):
                b, p, i = split(e)
                pool.wait_ge(te_loaded[p], 48 * i + 48)
                wait(pool, vt_ready, 4 * b)
                for k in range(T16):
                    pool.tensor_tensor(mix_bd[:, k, :, :], mix_te[:, p, k, :].unsqueeze(1).to_broadcast([P, 16, H]),
                                       c.tok16[:, :].unsqueeze(2).to_broadcast([P, 16, H]), ALU.mult).then_inc(mix_bd_done, 1)

            def spread_pick(e):
                b, p, i = split(e)
                wait(pool, u_ready, 2 * b)
                for n in range(T8):
                    pool.tensor_tensor(pick_bd[:, n, :, :], pick_th[:, p, n, :].unsqueeze(1).to_broadcast([P, 8, X]),
                                       c.tok8[:, :].unsqueeze(2).to_broadcast([P, 8, X]), ALU.mult).then_inc(pick_bd_done, 1)

            def start():
                inverse_deviation((0, 0, 0))
                inverse_deviation((1, 1, 0))
                pool.memset(kz[:, :, :, :, :, :], 0.0).then_inc(kz_cleared, 1)
                inverse_deviation((2, 2, 0))
                inverse_deviation((3, 3, 0))
                spread_mix((0, 0, 0))

            def body(cur, has):
                if has.ahead:
                    inverse_deviation(after(cur, 4))
                if has.front:
                    spread_mix(after(cur))
                spread_pick(cur)

            pool.memset(minus_half[:, :], -0.5).then_inc(consts_done, 1)
            pool.wait_ge(consts_done, 2)
            pipeline(pool, start, body, lambda e: None)


class Names:
    pass


def flamingo_kernel(nc, ins, out):
    d = Names()
    (d.x, d.ctx, d.mask, d.g_xattn, d.g_ffn, d.wq, d.bq, d.wk, d.bk, d.wv, d.bv, d.wo, d.bo,
     d.wq2, d.wk2, d.wv2, d.ws, d.wd, d.wo2) = ins
    d.out = out
    z = Shapes(d.x, d.ctx, d.wq2, d.wv2)
    with ExitStack() as ctx:
        sb = lambda name, shape: ctx.enter_context(nc.sbuf_tensor(name, shape, F32))
        c = Names()
        c.X = sb("X", [P, z.B, z.E])
        c.ident = sb("ident", [P, P])
        c.tok16, c.tok8 = sb("tok16", [P, 16]), sb("tok8", [P, 8])
        c.tanh_g = sb("tanh_g", [z.S, 2])
        c.wq2T, c.wk2T = sb("wq2T", [P, z.EC, z.M2 * P]), sb("wk2T", [P, z.EC, z.M2 * P])
        c.wv2T = sb("wv2T", [P, z.EC, z.X * z.D2])
        c.wgT = sb("wgT", [P, z.EC, 2 * z.H2 * z.X])
        c.wo2T = sb("wo2T", [P, z.X // 2, z.E])
        with ExitStack() as inner:
            sb1 = lambda name, shape: inner.enter_context(nc.sbuf_tensor(name, shape, F32))
            c.ctx_in = sb1("ctx_in", [z.KP, 2, z.KC, z.E])
            c.ctx_loaded = [inner.enter_context(nc.semaphore(f"ctx_loaded{i}")) for i in range(2)]
            c.x_loaded = [inner.enter_context(nc.semaphore(f"x_loaded{i}")) for i in range(2)]
            c.wq, c.wk, c.wv, c.wo = (sb1(n, [P, z.EC, z.E]) for n in ("wq_sb", "wk_sb", "wv_sb", "wo_sb"))
            c.bq, c.bk = sb1("bq_sb", [P, z.EC]), sb1("bk_sb", [P, z.EC])
            c.bv, c.bo = sb1("bv_sb", [z.KP, z.E]), sb1("bo_sb", [z.S, z.E])
            c.maskb = sb1("maskb", [z.S, z.S2])
            free = z.B
            places = []
            for n in (z.M2, z.M2, z.X * z.D2 // P, 2, z.X * z.D2 * z.EC // z.E):
                free -= n
                places.append(c.X[:, free:free + n, :])
            c.wq_in, c.wk_in, c.wv_in, c.wg_in, wo_in = places
            c.wo_in = wo_in.rearrange("p (f a) (x d) -> p f (a x) d", f=z.EC, d=z.D2)
            assert free >= z.GX
            c.weights_loaded = [inner.enter_context(nc.semaphore(f"weights_loaded{i}")) for i in range(4)]
            prepare(nc, z, d, c)
            cross(nc, z, d, c)
        switch(nc, z, d, c)


_INS = ['x', 'ctx_1024', 'mask_1x1xSxS2_fk1', 'g_xattn', 'g_ffn', 'L0_xattn_wq', 'L0_xattn_bq', 'L0_xattn_wk',
        'L0_xattn_bk', 'L0_xattn_wv', 'L0_xattn_bv', 'L0_xattn_wo', 'L0_xattn_bo', 'L0_ffn_Wq', 'L0_ffn_Wk',
        'L0_ffn_Wv', 'L0_ffn_Ws', 'L0_ffn_Wd', 'L0_ffn_Wo']


def kernel(**inputs):
    import numpy as _np
    import concourse.bacc as _bacc
    from concourse import mybir as _mybir
    from concourse.bass_utils import run_bass_kernel_spmd as _run

    nc = _bacc.Bacc("TRN2", target_bir_lowering=False, num_devices=1)
    arrays, args = {}, []
    for name in _INS:
        a = _np.ascontiguousarray(inputs[name])
        arrays[f"in_{name}_dram"] = a
        args.append(nc.dram_tensor(f"in_{name}_dram", a.shape, _mybir.dt.from_np(a.dtype), kind="ExternalInput").ap())
    out = nc.dram_tensor("out_0_dram", inputs["x"].shape, _mybir.dt.float32, kind="ExternalOutput").ap()
    flamingo_kernel(nc, args, out)
    r = _run(nc, [arrays], core_ids=[0])
    return r.results[0]["out_0_dram"]
```
